# Optimizing a Trainium2 kernel written in Bass

```python
import numpy as np
import jax
import jax.numpy as jnp

def _softmax(x, axis=-1):
    return jax.nn.softmax(x, axis=axis)

def _gelu(x):
    return jax.nn.gelu(x, approximate=True)

def _silu(x):
    return jax.nn.silu(x)

def _sigmoid(x):
    return jax.nn.sigmoid(x)

def _layernorm(x, axis=-1, eps=1e-05):
    m = jnp.mean(x, axis=axis, keepdims=True)
    v = jnp.var(x, axis=axis, keepdims=True)
    return (x - m) / jnp.sqrt(v + eps)

def _scatter_add(tgt, idx, src, axis=0):
    return tgt.at[idx].add(src)

def _segment_sum(src, seg, n):
    return jax.ops.segment_sum(src, seg, n)
kernel_name = 'mk_audio_tower_d1_tok_audfeat256_r4_4c1b69'

def setup_inputs(seed: int=0):
    np.random.seed(seed)
    _w = jnp.asarray

    def _rec_inputs():
        import jax
        import jax.numpy as jnp
        _rk = jax.random.key(seed)
        x = jax.random.uniform(jax.random.fold_in(_rk, 1), (8, 4, 375), jnp.float32, 0.0, 0.999986)
        return x
    x = _rec_inputs()

    def _L0_tok_setup():
        import jax, jax.numpy as jnp
        import numpy as np
        T = 8
        key = jax.random.key(seed)
        ks = jax.random.split(key, 9)
        bs, dims, L, d = (16, 4, 512, 64)
        x = jax.random.uniform(ks[0], (bs, dims, L), dtype=jnp.float32)
        s_in = 1.0 / np.sqrt(dims)
        s_d = 1.0 / np.sqrt(d)
        W1 = jax.random.uniform(ks[1], (d, dims), minval=-s_in, maxval=s_in, dtype=jnp.float32)
        b1 = jax.random.uniform(ks[2], (d,), minval=-s_in, maxval=s_in, dtype=jnp.float32)
        W2 = jax.random.uniform(ks[3], (d, d), minval=-s_d, maxval=s_d, dtype=jnp.float32)
        b2 = jax.random.uniform(ks[4], (d,), minval=-s_d, maxval=s_d, dtype=jnp.float32)
        W3 = jax.random.uniform(ks[5], (d, dims), minval=-s_in, maxval=s_in, dtype=jnp.float32)
        b3 = jax.random.uniform(ks[6], (d,), minval=-s_in, maxval=s_in, dtype=jnp.float32)
        W4 = jax.random.uniform(ks[7], (d, d), minval=-s_d, maxval=s_d, dtype=jnp.float32)
        b4 = jax.random.uniform(ks[8], (d,), minval=-s_d, maxval=s_d, dtype=jnp.float32)
        return dict(x=x, W1=W1, b1=b1, W2=W2, b2=b2, W3=W3, b3=b3, W4=W4, b4=b4)
    _L0_tok_all = _L0_tok_setup()
    _L0_tok_in = {k: v for k, v in _L0_tok_all.items() if k in ('W1', 'b1', 'W2', 'b2', 'W3', 'b3', 'W4', 'b4')}
    del _L0_tok_all

    def _L0_attn_setup():
        import jax, jax.numpy as jnp
        import numpy as np
        H = 8
        key = jax.random.key(seed)
        ks = jax.random.split(key, 10)
        B, N, D, E = (1, 1024, 64, 16384)
        s = 0.02
        return {'x': jax.random.normal(ks[0], (B, N, D), jnp.float32), 'edge_index': jax.random.randint(ks[1], (2, E), 0, N, jnp.int32), 'edge_attr': jax.random.normal(ks[2], (E, 3), jnp.float32), 'Wq': jax.random.normal(ks[3], (D, D), jnp.float32) * s, 'bq': jnp.zeros((D,), jnp.float32), 'Wk': jax.random.normal(ks[4], (D, D), jnp.float32) * s, 'bk': jnp.zeros((D,), jnp.float32), 'Wv': jax.random.normal(ks[5], (D, D), jnp.float32) * s, 'bv': jnp.zeros((D,), jnp.float32), 'Wo': jax.random.normal(ks[6], (D, D), jnp.float32) * s, 'bo': jnp.zeros((D,), jnp.float32), 'We': jax.random.normal(ks[7], (3, H), jnp.float32) * s, 'be': jnp.zeros((H,), jnp.float32)}
    _L0_attn_all = _L0_attn_setup()
    _L0_attn_in = {k: v for k, v in _L0_attn_all.items() if k in ('edge_index', 'edge_attr', 'Wq', 'bq', 'Wk', 'bk', 'Wv', 'bv', 'Wo', 'bo', 'We', 'be')}
    del _L0_attn_all

    def _L0_ffn_setup():
        import jax, jax.numpy as jnp
        import numpy as np
        B, N, D = (16, 1024, 64)
        NUM_EXPERTS, TOP_K, HEADS = (4, 2, 4)
        N_EDGES = 262144
        LN_EPS = 1e-05

        def _layernorm(x, g, b):
            mu = x.mean(-1, keepdims=True)
            var = ((x - mu) ** 2).mean(-1, keepdims=True)
            return (x - mu) * jax.lax.rsqrt(var + LN_EPS) * g + b

        def _forward(x, edge_index, W_gat, att_src, att_dst, b_gat, ln_gamma, ln_beta, W1, b1, W2, b2):
            Bc, Nc, Dc = x.shape
            M = Bc * Nc
            x_flat = x.reshape(M, Dc)
            h = (x_flat @ W_gat).reshape(M, HEADS, NUM_EXPERTS)
            loops = jnp.arange(M, dtype=edge_index.dtype)
            src = jnp.concatenate([edge_index[0], loops])
            dst = jnp.concatenate([edge_index[1], loops])
            a_src = (h * att_src).sum(-1)
            a_dst = (h * att_dst).sum(-1)
            e = jax.nn.leaky_relu(a_src[src] + a_dst[dst], negative_slope=0.2)
            e_max = jax.ops.segment_max(e, dst, num_segments=M)
            ee = jnp.exp(e - e_max[dst])
            denom = jax.ops.segment_sum(ee, dst, num_segments=M)
            alpha = ee / (denom[dst] + 1e-16)
            msg = h[src] * alpha[:, :, None]
            agg = jax.ops.segment_sum(msg, dst, num_segments=M).reshape(M, HEADS * NUM_EXPERTS) + b_gat
            scores = _layernorm(agg, ln_gamma, ln_beta).reshape(M, HEADS, NUM_EXPERTS).mean(1)
            scores = scores.reshape(Bc, Nc, NUM_EXPERTS)
            topk_s, topk_i = jax.lax.top_k(scores, TOP_K)
            w = jax.nn.softmax(topk_s, axis=-1)
            out = jnp.zeros_like(x)
            for ei in range(NUM_EXPERTS):
                g = jnp.where(topk_i == ei, w, 0.0).sum(-1)
                hh = jax.nn.gelu(x @ W1[ei] + b1[ei], approximate=False)
                out = out + g[..., None] * (hh @ W2[ei] + b2[ei])
            return out
        key = jax.random.key(seed)
        ks = jax.random.split(key, 8)
        s = 0.05
        return {'x': jax.random.normal(ks[0], (B, N, D), jnp.float32), 'W_gat': jax.random.normal(ks[1], (D, HEADS * NUM_EXPERTS), jnp.float32) * s, 'att_src': jax.random.normal(ks[2], (HEADS, NUM_EXPERTS), jnp.float32) * s, 'att_dst': jax.random.normal(ks[3], (HEADS, NUM_EXPERTS), jnp.float32) * s, 'b_gat': jnp.zeros((HEADS * NUM_EXPERTS,), jnp.float32), 'ln_gamma': jnp.ones((HEADS * NUM_EXPERTS,), jnp.float32), 'ln_beta': jnp.zeros((HEADS * NUM_EXPERTS,), jnp.float32), 'W1': jax.random.normal(ks[4], (NUM_EXPERTS, D, 2 * D), jnp.float32) * s, 'b1': jnp.zeros((NUM_EXPERTS, 2 * D), jnp.float32), 'W2': jax.random.normal(ks[5], (NUM_EXPERTS, 2 * D, D), jnp.float32) * s, 'b2': jnp.zeros((NUM_EXPERTS, D), jnp.float32), 'edge_index': jax.random.randint(ks[6], (2, N_EDGES), 0, B * N, jnp.int32)}
    _L0_ffn_all = _L0_ffn_setup()
    _L0_ffn_in = {k: v for k, v in _L0_ffn_all.items() if k in ('W_gat', 'att_src', 'att_dst', 'b_gat', 'ln_gamma', 'ln_beta', 'W1', 'b1', 'W2', 'b2', 'edge_index')}
    del _L0_ffn_all
    return {'x': x, 'L0_tok_W1': _L0_tok_in['W1'], 'L0_tok_b1': _L0_tok_in['b1'], 'L0_tok_W2': _L0_tok_in['W2'], 'L0_tok_b2': _L0_tok_in['b2'], 'L0_tok_W3': _L0_tok_in['W3'], 'L0_tok_b3': _L0_tok_in['b3'], 'L0_tok_W4': _L0_tok_in['W4'], 'L0_tok_b4': _L0_tok_in['b4'], 'L0_attn_edge_index': _L0_attn_in['edge_index'], 'L0_attn_edge_attr': _L0_attn_in['edge_attr'], 'L0_attn_Wq': _L0_attn_in['Wq'], 'L0_attn_bq': _L0_attn_in['bq'], 'L0_attn_Wk': _L0_attn_in['Wk'], 'L0_attn_bk': _L0_attn_in['bk'], 'L0_attn_Wv': _L0_attn_in['Wv'], 'L0_attn_bv': _L0_attn_in['bv'], 'L0_attn_Wo': _L0_attn_in['Wo'], 'L0_attn_bo': _L0_attn_in['bo'], 'L0_attn_We': _L0_attn_in['We'], 'L0_attn_be': _L0_attn_in['be'], 'L0_ffn_W_gat': _L0_ffn_in['W_gat'], 'L0_ffn_att_src': _L0_ffn_in['att_src'], 'L0_ffn_att_dst': _L0_ffn_in['att_dst'], 'L0_ffn_b_gat': _L0_ffn_in['b_gat'], 'L0_ffn_ln_gamma': _L0_ffn_in['ln_gamma'], 'L0_ffn_ln_beta': _L0_ffn_in['ln_beta'], 'L0_ffn_W1': _L0_ffn_in['W1'], 'L0_ffn_b1': _L0_ffn_in['b1'], 'L0_ffn_W2': _L0_ffn_in['W2'], 'L0_ffn_b2': _L0_ffn_in['b2'], 'L0_ffn_edge_index': _L0_ffn_in['edge_index']}

def reference(x, L0_tok_W1, L0_tok_b1, L0_tok_W2, L0_tok_b2, L0_tok_W3, L0_tok_b3, L0_tok_W4, L0_tok_b4, L0_attn_edge_index, L0_attn_edge_attr, L0_attn_Wq, L0_attn_bq, L0_attn_Wk, L0_attn_bk, L0_attn_Wv, L0_attn_bv, L0_attn_Wo, L0_attn_bo, L0_attn_We, L0_attn_be, L0_ffn_W_gat, L0_ffn_att_src, L0_ffn_att_dst, L0_ffn_b_gat, L0_ffn_ln_gamma, L0_ffn_ln_beta, L0_ffn_W1, L0_ffn_b1, L0_ffn_W2, L0_ffn_b2, L0_ffn_edge_index):
    import jax
    import jax.numpy as jnp

    def _L0_tok_ref(x, W1, b1, W2, b2, W3, b3, W4, b4):
        import jax, jax.numpy as jnp
        import numpy as np
        T = 8
        a = jnp.einsum('bdl,od->blo', x, W1) + b1
        bs, L, d = a.shape
        zcol = jnp.zeros((bs, 1, d), a.dtype)
        shift_r = lambda v: jnp.concatenate([zcol, v[:, :-1]], axis=1)
        shift_l = lambda v: jnp.concatenate([v[:, 1:], zcol], axis=1)
        up = jnp.zeros_like(a)
        down = jnp.zeros_like(a)
        for _ in range(T):
            up = jax.nn.relu(a + shift_r(up) @ W2.T + b2)
            down = jax.nn.relu(a + shift_l(down) @ W2.T + b2)
        c = jnp.einsum('bdl,od->blo', x, W3) + b3
        miu = jax.nn.relu(c + (shift_r(up) @ W4.T + b4) + (shift_l(down) @ W4.T + b4))
        return miu

    def _L0_attn_ref(x, edge_index, edge_attr, Wq, bq, Wk, bk, Wv, bv, Wo, bo, We, be):
        import jax, jax.numpy as jnp
        import numpy as np
        H = 8
        B, N, D = x.shape
        hd = D // H
        q = (x @ Wq + bq).reshape(B, N, H, hd)
        k = (x @ Wk + bk).reshape(B, N, H, hd)
        v = (x @ Wv + bv).reshape(B, N, H, hd)
        scores = jnp.einsum('bihd,bjhd->bhij', q, k) / jnp.sqrt(jnp.asarray(hd, x.dtype))
        eb = edge_attr @ We + be
        edge_tgt = edge_index[1]
        col_bias = jnp.zeros((H, N), x.dtype).at[:, edge_tgt].set(eb.T)
        scores = scores + col_bias[None, :, None, :]
        attn = jax.nn.softmax(scores, axis=-1)
        out = jnp.einsum('bhij,bjhd->bihd', attn, v).reshape(B, N, D)
        return out @ Wo + bo

    def _L0_ffn_ref(x, W_gat, att_src, att_dst, b_gat, ln_gamma, ln_beta, W1, b1, W2, b2, edge_index):
        import jax, jax.numpy as jnp
        import numpy as np
        B, N, D = (16, 1024, 64)
        NUM_EXPERTS, TOP_K, HEADS = (4, 2, 4)
        N_EDGES = 262144
        LN_EPS = 1e-05

        def _layernorm(x, g, b):
            mu = x.mean(-1, keepdims=True)
            var = ((x - mu) ** 2).mean(-1, keepdims=True)
            return (x - mu) * jax.lax.rsqrt(var + LN_EPS) * g + b

        def _forward(x, edge_index, W_gat, att_src, att_dst, b_gat, ln_gamma, ln_beta, W1, b1, W2, b2):
            Bc, Nc, Dc = x.shape
            M = Bc * Nc
            x_flat = x.reshape(M, Dc)
            h = (x_flat @ W_gat).reshape(M, HEADS, NUM_EXPERTS)
            loops = jnp.arange(M, dtype=edge_index.dtype)
            src = jnp.concatenate([edge_index[0], loops])
            dst = jnp.concatenate([edge_index[1], loops])
            a_src = (h * att_src).sum(-1)
            a_dst = (h * att_dst).sum(-1)
            e = jax.nn.leaky_relu(a_src[src] + a_dst[dst], negative_slope=0.2)
            e_max = jax.ops.segment_max(e, dst, num_segments=M)
            ee = jnp.exp(e - e_max[dst])
            denom = jax.ops.segment_sum(ee, dst, num_segments=M)
            alpha = ee / (denom[dst] + 1e-16)
            msg = h[src] * alpha[:, :, None]
            agg = jax.ops.segment_sum(msg, dst, num_segments=M).reshape(M, HEADS * NUM_EXPERTS) + b_gat
            scores = _layernorm(agg, ln_gamma, ln_beta).reshape(M, HEADS, NUM_EXPERTS).mean(1)
            scores = scores.reshape(Bc, Nc, NUM_EXPERTS)
            topk_s, topk_i = jax.lax.top_k(scores, TOP_K)
            w = jax.nn.softmax(topk_s, axis=-1)
            out = jnp.zeros_like(x)
            for ei in range(NUM_EXPERTS):
                g = jnp.where(topk_i == ei, w, 0.0).sum(-1)
                hh = jax.nn.gelu(x @ W1[ei] + b1[ei], approximate=False)
                out = out + g[..., None] * (hh @ W2[ei] + b2[ei])
            return out
        return _forward(x, edge_index, W_gat, att_src, att_dst, b_gat, ln_gamma, ln_beta, W1, b1, W2, b2)
    h = _L0_tok_ref(x, L0_tok_W1, L0_tok_b1, L0_tok_W2, L0_tok_b2, L0_tok_W3, L0_tok_b3, L0_tok_W4, L0_tok_b4)
    h = h + _L0_attn_ref(_layernorm(h, axis=-1), L0_attn_edge_index, L0_attn_edge_attr, L0_attn_Wq, L0_attn_bq, L0_attn_Wk, L0_attn_bk, L0_attn_Wv, L0_attn_bv, L0_attn_Wo, L0_attn_bo, L0_attn_We, L0_attn_be)
    h = h + _L0_ffn_ref(_layernorm(h, axis=-1), L0_ffn_W_gat, L0_ffn_att_src, L0_ffn_att_dst, L0_ffn_b_gat, L0_ffn_ln_gamma, L0_ffn_ln_beta, L0_ffn_W1, L0_ffn_b1, L0_ffn_W2, L0_ffn_b2, L0_ffn_edge_index)
    return h

_drawn_inputs = setup_inputs


def setup_inputs(seed=0):
    import zlib

    import numpy as np

    out = dict(_drawn_inputs(seed))
    spreads = {'L0_attn_bq': (0.0, 2.0),
     'L0_attn_bk': (0.0, 2.0),
     'L0_attn_bv': (0.0, 0.1),
     'L0_attn_bo': (0.0, 0.1),
     'L0_attn_be': (0.0, 2.0),
     'L0_ffn_b_gat': (0.0, 0.1),
     'L0_ffn_ln_gamma': (1.0, 0.2),
     'L0_ffn_ln_beta': (0.0, 0.1),
     'L0_ffn_b1': (0.0, 0.1),
     'L0_ffn_b2': (0.0, 0.1)}
    factors = {'L0_attn_edge_attr': 26.344,
     'L0_attn_Wq': 8.0,
     'L0_attn_Wk': 8.0,
     'L0_attn_We': 8.0,
     'L0_ffn_att_src': 4.272,
     'L0_ffn_att_dst': 16.429}
    for name, (base, spread) in spreads.items():
        noise = np.random.default_rng([zlib.crc32(name.encode()), seed]).standard_normal(out[name].shape)
        drawn = base * np.exp(spread * noise) if base else spread * noise
        out[name] = jnp.asarray(drawn.astype(out[name].dtype))
    for name, factor in factors.items():
        out[name] = (out[name] * factor).astype(out[name].dtype)
    return out
```

```python
from contextlib import ExitStack

import numpy as np

import concourse.bass as bass
from concourse import mybir

F32 = mybir.dt.float32
F16 = mybir.dt.float16
BF16 = mybir.dt.bfloat16
I32 = mybir.dt.int32
ALU = mybir.AluOpType
ACT = mybir.ActivationFunctionType
AX = mybir.AxisListType.X
MAX_ALL = bass.bass_isa.ReduceOp.max

B, DIN, L, D = 8, 4, 375, 64
STEPS = 8
H, HD = 8, 8
M = B * L
P = 125
KT = L // P
NT = M // P
GH, EX = 4, 4
GF = GH * EX
HID = 2 * D
E_ATT = 16384
JA = E_ATT // 128
E_GAT = 262144
JG = E_GAT // 128
LAST = M - 1
EPS = 1e-5
NEG = -1e30
MAGIC = 12582912.0

CAP = 104
RANKS = 8
SLOTS = 128 * RANKS
SRC_BITS, TILE_BITS = 12, 5
SKIP = float(P * SLOTS + 72000)
GROUP = 64
RES = 2 * GH + GF

Q_PART = (0, 0, 1, 0, 2, 1)
K_PART = (0, 1, 0, 2, 0, 1)
BIAS_ROW = 8 * len(Q_PART)
ONES_ROW = 3 * H


def constants():
    bf = mybir.dt.np(BF16)
    sel = np.zeros((128, 2, 3, 4, 128), np.float32)
    ext = np.zeros((3 * H + 1, 2, 4, 128), np.float32)
    row = np.zeros((3 * H, H, P), np.float32)
    for h in range(H):
        pair, base = h // 2, 64 * (h % 2)
        for c, (qp, kp) in enumerate(zip(Q_PART, K_PART)):
            for d in range(HD):
                sel[h * HD + d, 0, qp, pair, base + c * HD + d] = 1
                sel[64 + h * HD + d, 1, kp, pair, base + c * HD + d] = 1
        for part in range(3):
            ext[ONES_ROW, 0, pair, base + BIAS_ROW + part] = 1
            ext[h * 3 + part, 1, pair, base + BIAS_ROW + part] = 1
            row[h * 3 + part, h, :] = 1
    eye = np.eye(128, dtype=np.float32)
    lane = np.broadcast_to(np.arange(128, dtype=np.float32), (128, 128))
    iota = np.broadcast_to(np.arange(512, dtype=np.float32), (128, 512))
    scale = np.ones((128, 1), np.float32)
    scale[:64] = HD ** -0.5
    hot = np.broadcast_to(np.arange(128, dtype=np.float32)[None, :, None], (128, 128, 16))
    hot = np.ascontiguousarray(hot).astype(bf)
    lower = np.tril(np.ones((EX, EX), np.float32), -1)
    return {
        "c_sel": sel.astype(bf), "c_ext": ext.astype(bf), "c_row": row.astype(bf),
        "c_eye": eye, "c_eyeb": eye.astype(bf), "c_iota": np.ascontiguousarray(iota),
        "c_scale": scale, "c_hot": hot,
        "c_part": RANKS * np.arange(128, dtype=np.float32)[:, None],
        "c_lower": np.ascontiguousarray(np.broadcast_to(lower.reshape(1, -1), (128, EX * EX))),
    }


def graph_transformer_block(nc, x, w_step, w_in, w_mix, w_c,
                            att_tgt, att_attr, w_qk, w_v, w_o, w_e,
                            w_gat, att_vec, w1, b2, w2, gat_src, gat_dst,
                            c_sel, c_ext, c_row, c_eye, c_eyeb, c_iota, c_scale, c_hot, c_part, c_lower,
                            out):
    ctx = ExitStack()
    with ctx:
        def sb(name, shape, dt=F32):
            return ctx.enter_context(nc.sbuf_tensor(name, shape, dt))

        def sem(name):
            return ctx.enter_context(nc.semaphore(name))

        exchange = nc.dram_tensor("exchange", (P * SLOTS, 1), F32, kind="Internal").ap()
        node_rows = nc.dram_tensor("node_rows", (M, GF + GH), F32, kind="Internal").ap()
        edge_rows = nc.dram_tensor("edge_rows", (P * CAP, RES), F32, kind="Internal").ap()

        ps = ctx.enter_context(nc.psum_tensor("ps", [128, 8, 512], F32))

        wstep = sb("wstep", [128, 128])
        win = sb("win", [6, 128])
        wmix = sb("wmix", [128, D])
        wc = sb("wc", [7, D])
        wqk = sb("wqk", [D + 1, 128])
        wv = sb("wv", [D + 1, 32 * H])
        wo = sb("wo", [D + 1, D])
        wgat = sb("wgat", [D, GF])
        we = sb("we", [128, 4, H])
        vecs = sb("vecs", [128, 5, GF])
        w1s = sb("w1s", [D + 1, EX, HID])
        w2s = sb("w2s", [HID, EX, D])
        b2s = sb("b2s", [1, EX, D])
        sel = sb("sel", [128, 2, 3, 4, 128], BF16)
        ext = sb("ext", [ONES_ROW + 1, 2, 4, 128], BF16)
        row = sb("row", [3 * H, H, P], BF16)
        eye = sb("eye", [128, 128])
        eyeb = sb("eyeb", [128, 128], BF16)
        iota = sb("iota", [128, 512])
        qk_scale = sb("qk_scale", [128, 1])
        hot = sb("hot", [128, 128, 16], BF16)
        part = sb("part", [128, 1])
        lower = sb("lower", [128, EX * EX])
        ones1 = sb("ones1", [1, 128])
        tok_x = sb("tok_x", [128, B, L])
        xaug = tok_x[0:7, :, :]
        state = sb("state", [128, B, L + 2])
        add_in = sb("add_in", [128, B, L])
        big = sb("big", [128, 8, JG])

        def view(first, at, shape, dt=F32):
            n = int(np.prod(shape))
            flat = big[:, first:8, :].rearrange("p a b -> p (a b)")
            flat = flat[:, at:at + n] if dt is F32 else flat[:, at:at + n // 2].bitcast(dt)
            names = "abcd"[:len(shape)]
            if len(shape) == 1:
                return flat
            return flat.rearrange(f"p ({' '.join(names)}) -> p {' '.join(names)}", **dict(zip(names[1:], shape[1:])))

        h = sb("h", [128, NT, D])
        xn = sb("xn", [128, NT, D])
        sq = sb("sq", [128, NT, D])
        stat = sb("stat", [128, 4, NT])
        xT = add_in[0:D + 1, :, :].rearrange("p b l -> p (b l)")
        probs = view(0, 0, [2, KT, L])
        vv = view(2, 0, [2, KT, 32 * H])
        qst = view(3, 0, [2, 4, L], BF16)
        kst = view(3, L * 4, [2, 4, L], BF16)
        qk32 = view(5, 0, [L])
        rest = view(5, L, [L])
        parts = view(5, 2 * L, [3, L + 1], BF16)[:, :, 0:L]
        oT = view(5, 4 * L, [2, L])
        xb = view(5, 6 * L, [2, L])[0:D + 1]
        onT = view(5, 8 * L, [L])[0:D + 1]
        on = view(5, 9 * L, [KT, D])
        negmax = sb("negmax", [128, KT, H])
        nrest = sb("nrest", [128, KT, H])
        nparts = sb("nparts", [128, KT, H, 3], BF16)
        maxT = sb("maxT", [3 * H, L], BF16)
        rden = sb("rden", [128, KT, 4])
        tgt = sb("tgt", [128, JA])
        tgt_i = sb("tgt_i", [128, JA], I32)
        hit = sb("hit", [128, 2, 384], F16)
        iota_h = sb("iota_h", [128, 384], F16)
        lane_last = sb("lane_last", [128, 384], F16)
        last = sb("last", [128, KT, 128])
        lastf = sb("lastf", [128, 2, KT])
        last_i = sb("last_i", [128, KT], I32)
        attr = sb("attr", [128, KT, 3])
        bias = sb("bias", [128, KT, H])
        bparts = sb("bparts", [128, KT, H, 3], BF16)
        biasT = sb("biasT", [ONES_ROW + 1, L], BF16)
        src_i = big[:, 0, :].bitcast(I32)
        dst_i = big[:, 1, :].bitcast(I32)
        f_tile, f_own, f_key, f_real, f_tmp = (big[:, k, :] for k in range(2, 7))
        half = big[:, 7, :].bitcast(BF16)
        own_h, tile_h = half[:, 0:JG], half[:, JG:2 * JG]
        hot_own = sb("hot_own", [128, 2, 128, 16], BF16)
        hot_tile = sb("hot_tile", [128, 2, NT, 16], BF16)
        lane_list = sb("lane_list", [128, CAP])
        lane_int = sb("lane_int", [128, CAP], I32)
        lane_tmp = sb("lane_tmp", [128, 4, CAP])
        slot_i = sb("slot_i", [128, CAP], I32)
        own_tab = sb("own_tab", [128, SLOTS])
        own_list = sb("own_list", [128, CAP])
        own_int = sb("own_int", [128, CAP], I32)
        own_tmp_i = sb("own_tmp_i", [128, 2, CAP], I32)
        src_idx = sb("src_idx", [128, CAP], I32)
        seg = sb("seg", [128, CAP])
        keep = sb("keep", [128, CAP])
        member = sb("member", [128, CAP, NT])
        at_least = view(5, 0, [NT, CAP])
        endf = sb("endf", [128, 2, NT])
        end_idx = sb("end_idx", [128, NT], I32)
        has_real = sb("has_real", [128, NT])
        flags = sb("flags", [128, 4])
        clamped = sb("clamped", [128, NT])
        clampT = sb("clampT", [NT, 128])
        got = state[:, :, :].rearrange("p a b -> p (a b)")[:, 0:CAP * (GF + GH)].rearrange(
            "p (c f) -> p c f", f=GF + GH)
        msg = view(7, 0, [CAP, GF])
        adst_e = sb("adst_e", [128, CAP, GH])
        score = sb("score", [128, CAP, GH])
        run_max = sb("run_max", [128, CAP, GH])
        expo = sb("expo", [128, 2, CAP, GH])
        tab = sb("tab", [128, NT, GF + GH])
        adst = sb("adst", [128, NT, GH])
        gprod = sb("gprod", [128, NT, GF])
        lastrow = sb("lastrow", [128, GF + GH])
        ends = sb("ends", [128, NT, RES])
        st_max = sb("st_max", [128, NT, GH])
        st_den = sb("st_den", [128, NT, GH])
        st_num = sb("st_num", [128, NT, GF])
        s1, s2, s3, s4 = (sb(f"s{k}", [128, NT, GH]) for k in range(1, 5))
        acc = view(3, CAP * NT, [NT, RES])
        raw_i = sb("raw_i", [128, 2, GROUP], I32)
        over_i = sb("over_i", [1, 1], I32)
        flag_row = sb("flag_row", [1, 1])
        wts = sb("wts", [128, 3, NT, GH])
        gnum = sb("gnum", [128, NT, GF])
        gsq = sb("gsq", [128, NT, GF])
        own_row = sb("own_row", [128, 1])
        gate = sb("gate", [128, NT, EX])
        hid = tok_x[:, 0:EX, :]
        yexp = view(0, 0, [NT, EX, D])
        wide = view(3, 0, [CAP * NT])
        res = view(5, 0, [CAP, RES])

        tok_in = sem("tok_in")
        mix_in = sem("mix_in")
        edges_in = sem("edges_in")
        consts_in = sem("consts_in")
        tgt_in = sem("tgt_in")
        weights_in = sem("weights_in")
        zeros_set = sem("zeros_set")
        exchange_zeroed = sem("exchange_zeroed")
        state_zeroed = sem("state_zeroed")
        vec = sem("vec")
        act_own = sem("act_own")
        tok_sum = sem("tok_sum")
        tok_state = sem("tok_state")
        mix_done = sem("mix_done")
        h_ready = sem("h_ready")
        slots_ready = sem("slots_ready")
        scattered = sem("scattered")
        table_in = sem("table_in")
        hot_ready = sem("hot_ready")
        hot_used = sem("hot_used")
        hist_done = sem("hist_done")
        hist_copied = sem("hist_copied")
        histT_done = sem("histT_done")
        lane_last_ready = sem("lane_last_ready")
        lastT_done = sem("lastT_done")
        last_ready = sem("last_ready")
        attr_in = sem("attr_in")
        bparts_ready = sem("bparts_ready")
        biasT_done = sem("biasT_done")
        biasT_ready = sem("biasT_ready")
        centred = sem("centred")
        squared = sem("squared")
        var_ready = sem("var_ready")
        std_ready = sem("std_ready")
        xn_ready = sem("xn_ready")
        xT_done = sem("xT_done")
        xT_ready = sem("xT_ready")
        misc_full = sem("misc_full")
        misc_free = sem("misc_free")
        xb_ready = sem("xb_ready")
        qk32_ready = sem("qk32_ready")
        parts_ready = sem("parts_ready")
        score_full = sem("score_full")
        scoreT_full = sem("scoreT_full")
        max_done = sem("max_done")
        exp_done = sem("exp_done")
        pv_done = sem("pv_done")
        oT_ready = sem("oT_ready")
        negmax_ready = sem("negmax_ready")
        attn_added = sem("attn_added")
        gat_done = sem("gat_done")
        tab_ready = sem("tab_ready")
        tab_out = sem("tab_out")
        lastrow_in = sem("lastrow_in")
        gathered = sem("gathered")
        lists_ready = sem("lists_ready")
        hid_full = sem("hid_full")
        hid_ready = sem("hid_ready")
        y_full = sem("y_full")
        y_copied = sem("y_copied")
        exp_in = sem("exp_in")
        exp_out = sem("exp_out")
        res_ready = sem("res_ready")
        res_out = sem("res_out")
        ends_in = sem("ends_in")
        out_ready = sem("out_ready")
        out_done = sem("out_done")
        flags_ready = sem("flags_ready")
        flags_done = sem("flags_done")
        over_own = sem("over_own")
        over_ready = sem("over_ready")
        g_next = sem("g_next")
        g_raw_in = sem("g_raw_in")
        g_lists = sem("g_lists")
        g_gathered = sem("g_gathered")
        g_rows_in = sem("g_rows_in")
        g_ends_gathered = sem("g_ends_gathered")
        g_exp_in = sem("g_exp_in")
        g_exp_out = sem("g_exp_out")
        g_res = sem("g_res")
        g_res_out = sem("g_res_out")
        g_ends_in = sem("g_ends_in")
        vec_banks = sem("vec_banks")
        ones_set = sem("ones_set")
        cut = sem("cut")
        ncut = sem("ncut")
        rden_ready = sem("rden_ready")
        onT_one = sem("onT_one")

        block = ctx.enter_context(nc.Block())

        class Own:

            def __init__(self, eng, own):
                self.eng, self.own, self.n = eng, own, 0

            def did(self, ins):
                ins.then_inc(self.own, 1)
                self.n += 1

            def settle(self):
                self.eng.wait_ge(self.own, self.n)

        def take(eng, s, n):
            eng.wait_ge(s, n)
            eng.sem_clear(s)

        def if_lists_overflowed(eng, body):
            eng.wait_ge(over_ready, 1)
            over = eng.value_load(over_i[0:1, 0:1], min_val=0, max_val=1)
            with eng.If(over > 0):
                with eng.Fori(0, E_GAT // GROUP) as i:
                    body(i)

        N_CONSTS = 8
        N_WEIGHTS = 10
        HALF_U = ((0, 2), (64, 0))

        PRE = ["qk", "v01", "v2", "q0", "q1", "k0", "k1", "q2", "q3", "k2", "k3"]
        POST = ["norm0", "norm1", "onT", "out"]

        def order(prelims):
            seq = [("score", k) for k in range(H)] + [("maxT", 0)]
            pre = list(PRE) if prelims else []
            for k in range(H):
                seq.append(("exp", k))
                if k:
                    seq.append(("pv", k - 1))
                for _ in range(2 if k >= H - 3 else 1):
                    if pre:
                        seq.append((pre.pop(0), 0))
            seq.append(("pv", H - 1))
            seq += [(s, 0) for s in pre] + [(s, 0) for s in POST]
            return seq

        MISC = 1 + len(PRE) + len(POST)

        def batches(eng, body):
            with eng.Fori(0, B - 2, 2) as b:
                body(b, 0, True)
                body(b + 1, 1, True)
            body(B - 2, 0, True)
            body(B - 1, 1, False)

        @block.sync
        def _(sp):
            sp.dma_start(src_i, gat_src).then_inc(edges_in, 16)
            sp.dma_start(dst_i, gat_dst).then_inc(edges_in, 16)
            for a, b_ in ((wstep[:, :], w_step), (win[:, :], w_in), (eye[:, :], c_eye)):
                sp.dma_start(a, b_).then_inc(tok_in, 16)
            sp.wait_ge(zeros_set, 1)
            sp.dma_start(xaug[0:DIN, :, :], x.rearrange("b c l -> c b l")).then_inc(tok_in, 16)
            for a, b_ in ((wmix[:, :], w_mix), (wc[:, :], w_c)):
                sp.dma_start(a, b_).then_inc(mix_in, 16)
            sp.dma_start(tgt_i[:, :], att_tgt).then_inc(tgt_in, 16)
            for a, b_ in ((sel[:, :, :, :, :], c_sel), (ext[:, :, :, :], c_ext), (row[:, :, :], c_row),
                          (eyeb[:, :], c_eyeb), (iota[:, :], c_iota), (qk_scale[:, :], c_scale),
                          (hot[:, :, :], c_hot), (part[:, :], c_part)):
                sp.dma_start(a, b_).then_inc(consts_in, 16)
            sp.wait_ge(zeros_set, 2)
            sp.dma_start(exchange.rearrange("(p s) a -> p (s a)", p=P), own_tab[0:P, :]).then_inc(exchange_zeroed, 16)
            for a, b_ in ((wqk[:, :], w_qk), (wv[:, :], w_v), (wo[:, :], w_o), (wgat[:, :], w_gat),
                          (w1s[:, :, :], w1), (w2s[:, :, :], w2), (b2s[:, :, :], b2),
                          (lower[:, :], c_lower),
                          (we[:, :, :], w_e.rearrange("(o k) h -> o k h", o=1).to_broadcast([128, 4, H])),
                          (vecs[:, :, :], att_vec.rearrange("(o k) h -> o k h", o=1).to_broadcast([128, 5, GF]))):
                sp.dma_start(a, b_).then_inc(weights_in, 16)
            sp.wait_ge(scattered, 16 * CAP)
            sp.dma_start(own_tab[0:P, :], exchange.rearrange("(p s) a -> p (s a)", p=P)).then_inc(table_in, 16)
            sp.wait_ge(tab_ready, 1)
            sp.dma_start(node_rows.rearrange("(t p) f -> p t f", p=P), tab[0:P, :, :]).then_inc(tab_out, 16)
            sp.wait_ge(tab_out, 16)
            sp.dma_start(lastrow[:, :], node_rows[LAST:LAST + 1, :].to_broadcast([128, GF + GH])).then_inc(lastrow_in, 16)
            sp.wait_ge(res_ready, 1)
            sp.dma_start(edge_rows.rearrange("(p c) f -> p c f", p=P), res[0:P, :, :]).then_inc(res_out, 16)

            def group_in(i):
                take(sp, g_next, 1)
                for k, a in enumerate((gat_src, gat_dst)):
                    flat = a.rearrange("(o p) j -> o (p j)", o=1)
                    sp.dma_start(raw_i[:, k, :], flat[:, bass.ds(i * GROUP, GROUP)].to_broadcast([128, GROUP])).then_inc(g_raw_in, 16)
                take(sp, g_res, 1)
                sp.dma_start(edge_rows.rearrange("(p c) f -> p c f", p=P), res[0:P, :, :]).then_inc(g_res_out, 16)

            if_lists_overflowed(sp, group_in)
            sp.wait_ge(out_ready, 1)
            sp.dma_start(out.rearrange("b (k p) d -> p (b k) d", p=P), h[0:P, :, :]).then_inc(out_done, 16)
            sp.wait_ge(out_done, 16)

        @block.gpsimd
        def _(pool):
            pool.memset(xaug[:, :, :], 1.0).then_inc(zeros_set, 1)
            pool.wait_ge(zeros_set, 1)
            pool.memset(own_tab[:, :], 0.0).then_inc(zeros_set, 1)
            pool.wait_ge(slots_ready, 1)
            pool.wait_ge(exchange_zeroed, 16)
            for c in range(CAP):
                pool.indirect_dma_start(
                    out=exchange, out_offset=bass.IndirectOffsetOnAxis(ap=slot_i[:, c:c + 1], axis=0),
                    in_=lane_list[:, c:c + 1], in_offset=None,
                    bounds_check=P * SLOTS - 1, oob_is_err=False).then_inc(scattered, 16)
            pool.wait_ge(last_ready, 1)
            for k in range(KT):
                pool.indirect_dma_start(
                    out=attr[0:P, k, :], out_offset=None, in_=att_attr,
                    in_offset=bass.IndirectOffsetOnAxis(ap=last_i[0:P, k:k + 1], axis=0)).then_inc(attr_in, 16)
            def gather_rows(n, done):
                for c in range(n):
                    pool.indirect_dma_start(
                        out=got[0:P, c, :], out_offset=None, in_=node_rows,
                        in_offset=bass.IndirectOffsetOnAxis(ap=src_idx[0:P, c:c + 1], axis=0)).then_inc(done, 16)

            def gather_ends(done):
                for t in range(NT):
                    pool.indirect_dma_start(
                        out=ends[0:P, t, :], out_offset=None, in_=edge_rows,
                        in_offset=bass.IndirectOffsetOnAxis(ap=end_idx[0:P, t:t + 1], axis=0)).then_inc(done, 16)

            pool.wait_ge(lists_ready, 1)
            pool.wait_ge(tab_out, 16)
            gather_rows(CAP, gathered)
            pool.wait_ge(res_out, 16)
            gather_ends(ends_in)

            def landed(done, n, tell):
                pool.wait_ge(done, 16 * n)
                pool.dma_reset(range(done.num, done.num + 1))
                pool.sem_clear(done)
                pool.sem_inc(tell, 1)

            def group_rows(i):
                take(pool, g_lists, 1)
                gather_rows(GROUP, g_gathered)
                landed(g_gathered, GROUP, g_rows_in)
                take(pool, g_res_out, 16)
                gather_ends(g_ends_gathered)
                landed(g_ends_gathered, NT, g_ends_in)

            if_lists_overflowed(pool, group_rows)

        @block.tensor
        def _(pe):
            pe.wait_ge(tok_in, 64)
            for b in range(B):
                pe.matmul(ps[:, b, 0:L], win[0:6, :], xaug[0:6, b, :], start=True, stop=True).then_inc(tok_sum, 1)
            pe.wait_ge(state_zeroed, 1)
            with pe.Fori(1, STEPS) as r:
                for b in range(B):
                    pe.wait_ge(tok_state, (r - 1) * (2 * B) + 2 * (b + 1))
                    pe.matmul(ps[:, b, 0:L], eye[:, :], add_in[:, b, :], start=True, stop=False)
                    pe.matmul(ps[:, b, 0:L], wstep[:, :], state[:, b, 1:L + 1], start=False, stop=True).then_inc(tok_sum, 1)
            pe.wait_ge(mix_in, 32)
            pe.wait_ge(tok_state, STEPS * 2 * B)
            for t in range(NT):
                b, k = divmod(t, KT)
                bank, col = divmod(t, 8)
                o = ps[0:P, bank, col * D:(col + 1) * D]
                pe.matmul(o, state[:, b, 1 + k * P:1 + (k + 1) * P], wmix[:, :], start=True, stop=False)
                mm = pe.matmul(o, xaug[0:7, b, k * P:(k + 1) * P], wc[:, :], start=False, stop=True)
            mm.then_inc(mix_done, 1)

            pe.wait_ge(consts_in, 16 * N_CONSTS)

            def count(block_no, par, first=False, last_=False):
                pe.wait_ge(hot_ready, block_no + 1)
                for j in range(16):
                    mm = pe.matmul(ps[0:NT, 4, 0:P], hot_tile[:, par, :, j], hot_own[:, par, 0:P, j],
                                   start=(first and j == 0), stop=(last_ and j == 15))
                mm.then_inc(hist_done if last_ else hot_used, 1)

            count(0, 0, first=True)
            count(1, 1)
            with pe.Fori(1, JG // 32 - 1) as i:
                for par in range(2):
                    count(2 * i + par, par)
            count(JG // 16 - 2, 0)
            count(JG // 16 - 1, 1, last_=True)
            pe.wait_ge(hist_copied, 1)
            pe.matmul(ps[0:P, 5, 0:NT], clampT[:, 0:P], eye[0:NT, 0:NT], start=True, stop=True).then_inc(histT_done, 1)

            pe.wait_ge(lane_last_ready, 1)
            for k in range(KT):
                mm = pe.matmul(ps[0:P, 6, k * 128:(k + 1) * 128], lane_last[:, k * P:(k + 1) * P], eyeb[:, :],
                               start=True, stop=True)
            mm.then_inc(lastT_done, 1)
            pe.wait_ge(bparts_ready, 1)
            for k in range(KT):
                mm = pe.matmul(ps[0:3 * H, 7, k * P:(k + 1) * P], bparts[0:P, k, :, :].rearrange("p h c -> p (h c)"),
                               eyeb[0:P, 0:P], start=True, stop=True)
            mm.then_inc(biasT_done, 1)

            def turn_xn(n):
                pe.wait_ge(xn_ready, n)
                for b in range(B):
                    for k in range(KT):
                        mm = pe.matmul(ps[0:D, b, k * P:(k + 1) * P], xn[0:P, b * KT + k, :], eye[0:P, 0:P],
                                       start=True, stop=True)
                    mm.then_inc(xT_done, 1)

            pe.wait_ge(h_ready, 3)
            pe.wait_ge(vec_banks, 1)
            turn_xn(1)

            pe.wait_ge(biasT_ready, 1)
            pe.wait_ge(weights_in, 16 * N_WEIGHTS)
            misc = ps[:, 7, :]

            def pass_through(kind, par, n, b=None):
                pe.wait_ge(misc_free, n)
                if kind == "qk":
                    pe.wait_ge(xb_ready, b + 1)
                    mm = pe.matmul(misc[:, 0:L], wqk[:, :], xb[:, par, :], start=True, stop=True)
                elif kind in ("v01", "v2"):
                    for k in ((0, 1) if kind == "v01" else (2,)):
                        mm = pe.matmul(misc[0:P, 256 * (k % 2):256 * (k % 2) + 256],
                                       xb[:, par, k * P:(k + 1) * P], wv[:, :], start=True, stop=True)
                elif kind[0] in "qk" and len(kind) == 2:
                    side, pair = "qk".index(kind[0]), int(kind[1])
                    if kind == "q0":
                        pe.wait_ge(parts_ready, b + 1)
                    for part_ in range(3):
                        pe.matmul(misc[:, 0:L], sel[:, side, part_, pair, :], parts[:, part_, :],
                                  start=(part_ == 0), stop=False)
                    mm = pe.matmul(misc[:, 0:L], ext[:, side, pair, :], biasT[:, :], start=False, stop=True)
                elif kind == "maxT":
                    pe.wait_ge(negmax_ready, b + 1)
                    for k in range(KT):
                        mm = pe.matmul(misc[0:3 * H, k * P:(k + 1) * P], nparts[0:P, k, :, :].rearrange("p h c -> p (h c)"),
                                       eyeb[0:P, 0:P], start=True, stop=True)
                elif kind in ("norm0", "norm1"):
                    g = int(kind[4])
                    pe.wait_ge(oT_ready, 2 * b + g + 2)
                    for k in range(KT):
                        mm = pe.matmul(misc[0:P, k * 128:(k + 1) * 128], oT[:, g, k * P:(k + 1) * P], eye[:, :],
                                       start=True, stop=True)
                elif kind == "onT":
                    for k in range(KT):
                        mm = pe.matmul(misc[0:D, k * P:(k + 1) * P], on[0:P, k, :], eye[0:P, 0:P],
                                       start=True, stop=True)
                elif kind == "out":
                    for k in range(KT):
                        mm = pe.matmul(misc[0:P, k * D:(k + 1) * D], onT[:, k * P:(k + 1) * P], wo[:, :],
                                       start=True, stop=True)
                mm.then_inc(misc_full, 1)

            pe.wait_ge(xT_ready, 8)
            pe.wait_ge(onT_one, 1)
            for n, kind in enumerate(PRE):
                pass_through(kind, 0, n, 0)
            pe.wait_ge(misc_free, len(PRE))

            def batch(b, par, prelims):
                n = b * MISC + len(PRE)
                pe.wait_ge(misc_free, n - len(POST))
                for kind, k in order(prelims):
                    base, pair, q0 = 64 * (k % 2), k // 2, 32 * (k % 4)
                    bank = 3 * (k % 2)
                    if kind == "score":
                        if k < 2:
                            pe.wait_ge(exp_done, b * H + k + 1)
                        else:
                            pe.wait_ge(max_done, b * H + k - 1)
                        for t in range(KT):
                            mm = pe.matmul(ps[0:P, bank + t, 0:L], qst[base:base + 64, par, pair, t * P:(t + 1) * P],
                                           kst[base:base + 64, par, pair, :], start=True, stop=True)
                        mm.then_inc(score_full, 1)
                    elif kind == "exp":
                        if k < 2:
                            pe.wait_ge(max_done, b * H + H - 1 + k)
                        else:
                            pe.wait_ge(exp_done, b * H + k + 1)
                        for t in range(KT):
                            pe.matmul(ps[0:P, bank + t, 0:L], kst[base:base + 64, par, pair, t * P:(t + 1) * P],
                                      qst[base:base + 64, par, pair, :], start=True, stop=False)
                            mm = pe.matmul(ps[0:P, bank + t, 0:L], row[:, k, :], maxT[:, :], start=False, stop=True)
                        mm.then_inc(scoreT_full, 1)
                    elif kind == "pv":
                        pe.wait_ge(exp_done, b * H + k + 3)
                        if k % 4 == 0:
                            pe.wait_ge(oT_ready, 2 * b + k // 4 + 1)
                        for t in range(KT):
                            mm = pe.matmul(ps[q0:q0 + 32, 6, 0:L], vv[0:P, par, t, 32 * k:32 * k + 32],
                                           probs[0:P, k % 2, t, :], start=(t == 0), stop=(t == KT - 1))
                        mm.then_inc(pv_done, 1)
                    else:
                        nxt = kind in PRE
                        pass_through(kind, 1 - par if nxt else par, n, b + 1 if nxt else b)
                        n = n + 1
                    if kind == "maxT":
                        pe.wait_ge(misc_free, n)

            batches(pe, batch)

            pe.wait_ge(attn_added, B)
            turn_xn(2)
            pe.wait_ge(xT_ready, 16)
            for t in range(NT):
                mm = pe.matmul(ps[0:P, 7, t * GF:(t + 1) * GF], xT[0:D, t * P:(t + 1) * P], wgat[:, :],
                               start=True, stop=True)
            mm.then_inc(gat_done, 1)

            pe.sem_inc(y_full, EX)
            pe.wait_ge(tab_ready, 1)
            with pe.Fori(0, B) as b:
                for e in range(EX):
                    pe.wait_ge(hid_ready, b * EX + e + 1)
                    pe.matmul(ps[:, e, 0:L], w1s[:, e, :], xT[:, bass.ds(b * L, L)], start=True, stop=True).then_inc(hid_full, 1)
                for e in range(EX):
                    pe.wait_ge(hid_ready, b * EX + e + 5)
                    pe.wait_ge(y_copied, b * EX + e + 1)
                    for k in range(KT):
                        o = ps[0:P, 4 + e, k * D:(k + 1) * D]
                        pe.matmul(o, hid[:, e, k * P:(k + 1) * P], w2s[:, e, :], start=True, stop=False)
                        mm = pe.matmul(o, ones1[:, 0:P], b2s[:, e, :], start=False, stop=True)
                    mm.then_inc(y_full, 1)
            pe.wait_ge(flags_ready, 1)
            pe.wait_ge(hid_ready, B * EX + EX)
            pe.matmul(ps[0:1, 0, 0:128], flags[:, 3:4], eye[:, :], start=True, stop=True).then_inc(flags_done, 1)

        @block.scalar
        def _(act):
            own = Own(act, act_own)
            act.wait_ge(state_zeroed, 1)
            for b in range(B):
                act.wait_ge(tok_sum, b + 1)
                own.did(act.activation(add_in[:, b, :], ps[:, b, 0:L], ACT.Copy))
                act.wait_ge(act_own, b + 1)
                for p0, at in HALF_U:
                    act.activation(state[p0:p0 + 64, b, at:at + L], ps[p0:p0 + 64, b, 0:L], ACT.Relu).then_inc(tok_state, 1)
            with act.Fori(1, STEPS) as r:
                for b in range(B):
                    act.wait_ge(tok_sum, r * B + b + 1)
                    for p0, at in HALF_U:
                        act.activation(state[p0:p0 + 64, b, at:at + L], ps[p0:p0 + 64, b, 0:L], ACT.Relu).then_inc(tok_state, 1)
            act.wait_ge(mix_done, 1)
            for k in range(3):
                act.activation(h[0:P, 8 * k:8 * k + 8, :].rearrange("p t d -> p (t d)"), ps[0:P, k, :], ACT.Relu).then_inc(h_ready, 1)

            def norm_part(n):
                act.wait_ge(centred, n)
                act.activation(sq[0:P, :, :], xn[0:P, :, :], ACT.Square).then_inc(squared, 1)
                act.wait_ge(var_ready, n)
                act.activation(stat[0:P, 3, :], stat[0:P, 2, :], ACT.Sqrt).then_inc(std_ready, 1)
                for b in range(B):
                    act.wait_ge(xT_done, (n - 1) * B + b + 1)
                    act.activation(xT[0:D, b * L:(b + 1) * L], ps[0:D, b, 0:L], ACT.Copy).then_inc(xT_ready, 1)

            norm_part(1)

            def batch_in(b, par):
                act.activation(xb[:, par, :], xT[:, bass.ds(b * L, L)], ACT.Copy).then_inc(xb_ready, 1)

            def passed(kind, par, n, b, first=False):
                if kind == "qk":
                    act.wait_ge(misc_full, n + 1)
                    if not first:
                        act.wait_ge(parts_ready, b)
                    act.activation(qk32[:, :], ps[:, 7, 0:L], ACT.Copy, scale=qk_scale[:, 0:1]).then_inc(misc_free, 1)
                elif kind == "v01":
                    act.wait_ge(misc_full, n + 1)
                    act.activation(vv[0:P, par, 0:2, :].rearrange("p k c -> p (k c)"), ps[0:P, 7, :], ACT.Copy).then_inc(misc_free, 1)
                elif kind == "v2":
                    act.wait_ge(misc_full, n + 1)
                    act.activation(vv[0:P, par, 2, :], ps[0:P, 7, 0:256], ACT.Copy).then_inc(misc_free, 1)
                elif kind in ("k0", "k1", "k2", "k3"):
                    act.wait_ge(misc_full, n + 1)
                    act.activation(kst[:, par, int(kind[1]), :], ps[:, 7, 0:L], ACT.Copy).then_inc(misc_free, 1)
                elif kind == "onT":
                    act.wait_ge(misc_full, n + 1)
                    act.activation(onT[0:D, :], ps[0:D, 7, 0:L], ACT.Copy).then_inc(misc_free, 1)

            act.wait_ge(xT_ready, B)
            act.wait_ge(ones_set, 1)
            batch_in(0, 0)
            for n, kind in enumerate(PRE):
                passed(kind, 0, n, 0, first=True)

            def batch(b, par, prelims):
                n = b * MISC + len(PRE)
                for kind, k in order(prelims):
                    if kind == "exp":
                        act.wait_ge(scoreT_full, b * H + k + 1)
                        act.wait_ge(pv_done, b * H + k + 1)
                        act.activation(probs[0:P, k % 2, :, :], ps[0:P, 3 * (k % 2):3 * (k % 2) + 3, 0:L],
                                       ACT.Exp).then_inc(exp_done, 1)
                        if k == 0 and prelims:
                            batch_in(b + 1, 1 - par)
                    elif kind == "pv":
                        if k % 4 == 3:
                            act.wait_ge(pv_done, b * H + k + 3)
                            act.activation(oT[:, k // 4, :], ps[:, 6, 0:L], ACT.Copy).then_inc(oT_ready, 1)
                    elif kind != "score":
                        nxt = kind in PRE
                        passed(kind, 1 - par if nxt else par, n, b + 1 if nxt else b)
                        n = n + 1

            act.sem_inc(exp_done, 2)
            act.sem_inc(pv_done, 2)
            act.sem_inc(oT_ready, 1)
            batches(act, batch)
            norm_part(2)

            act.sem_inc(hid_ready, EX)
            with act.Fori(0, B) as b:
                for e in range(EX):
                    act.wait_ge(hid_full, b * EX + e + 1)
                    act.wait_ge(y_full, b * EX + e + 1)
                    act.activation(hid[:, e, :], ps[:, e, 0:L], ACT.Gelu).then_inc(hid_ready, 1)

            def exponentials(n, out_, in_):
                act.wait_ge(exp_in, n)
                act.activation(out_, in_, ACT.Exp).then_inc(exp_out, 1)

            exponentials(1, expo[0:P, :, :, :], expo[0:P, :, :, :])

            def group_exponentials(i):
                take(act, g_exp_in, 1)
                act.activation(expo[0:P, :, :, :], expo[0:P, :, :, :], ACT.Exp).then_inc(g_exp_out, 1)
                take(act, g_exp_in, 1)
                act.activation(wts[0:P, 0:2, :, :], wts[0:P, 0:2, :, :], ACT.Exp).then_inc(g_exp_out, 1)

            if_lists_overflowed(act, group_exponentials)
            exponentials(2, wts[0:P, :, :, :], wts[0:P, :, :, :])
            act.wait_ge(centred, 3)
            act.activation(gsq[0:P, :, :], gnum[0:P, :, :], ACT.Square).then_inc(squared, 1)
            act.wait_ge(var_ready, 3)
            act.activation(stat[0:P, 3, :], stat[0:P, 2, :], ACT.Sqrt).then_inc(std_ready, 1)
            exponentials(3, gate[0:P, :, :], gate[0:P, :, :])

        @block.vector
        def _(v):
            own = Own(v, vec)
            did, settle = own.did, own.settle

            def bc(ap, axis, shape):
                return ap.unsqueeze(axis).to_broadcast(shape)

            v.memset(state[:, :, :], 0.0).then_inc(state_zeroed, 1)
            did(v.memset(flags[:, :], 0.0))
            did(v.memset(biasT[:, :], 1.0))
            did(v.memset(ones1[:, :], 1.0))
            did(v.memset(lane_last[:, :], 0.0))

            v.wait_ge(edges_in, 32)

            def edge_keys(src, dst, key, own_tile, tile, real, tmp):
                did(v.tensor_scalar(tmp, dst, 1.0 / P, 0.504 - 1.0, ALU.mult, ALU.add))
                settle()
                did(v.tensor_scalar(tile, tmp, MAGIC, -MAGIC, ALU.add, ALU.add))
                settle()
                did(v.tensor_scalar(tmp, tile, float(2 ** TILE_BITS * P - 1), None, ALU.mult))
                settle()
                did(v.scalar_tensor_tensor(out=own_tile, in0=dst, scalar=float(2 ** TILE_BITS), in1=tmp,
                                           op0=ALU.mult, op1=ALU.subtract))
                settle()
                did(v.scalar_tensor_tensor(out=key, in0=own_tile, scalar=float(2 ** SRC_BITS), in1=src,
                                           op0=ALU.mult, op1=ALU.add))
                did(v.tensor_scalar(tmp, dst, float(M), None, ALU.is_lt))
                settle()
                did(v.scalar_tensor_tensor(out=real, in0=src, scalar=float(LAST), in1=tmp,
                                           op0=ALU.is_lt, op1=ALU.mult))
                settle()
                did(v.scalar_tensor_tensor(out=key, in0=key, scalar=1.0, in1=real, op0=ALU.add, op1=ALU.mult))

            edge_keys(src_i, dst_i, f_key, f_own, f_tile, f_real, f_tmp)
            did(v.scalar_tensor_tensor(out=tile_h, in0=f_real, scalar=200.0, in1=f_tile, op0=ALU.mult, op1=ALU.add))
            did(v.scalar_tensor_tensor(out=own_h, in0=f_tile, scalar=-float(P), in1=dst_i, op0=ALU.mult, op1=ALU.add))
            settle()

            for c in range(0, CAP, 8):
                did(v.max(lane_list[:, c:c + 8], f_key))
                settle()
                did(v.match_replace(f_key, lane_list[:, c:c + 8], f_key, -1.0))
                settle()
            did(v.tensor_reduce(flags[:, 0:1], f_key, AX, ALU.max))
            did(v.tensor_scalar(lane_list[:, :], lane_list[:, :], 0.0, None, ALU.max))
            settle()
            did(v.tensor_copy(lane_int[:, :], lane_list[:, :]))
            settle()
            did(v.tensor_scalar(own_tmp_i[:, 0, :], lane_int[:, :], SRC_BITS + TILE_BITS, None, ALU.logical_shift_right))
            settle()
            lane_own, same, rank, slot = (lane_tmp[:, k, :] for k in range(4))
            did(v.tensor_copy(lane_own, own_tmp_i[:, 0, :]))
            did(v.memset(same[:, 0:1], 0.0))
            settle()
            did(v.tensor_tensor(same[:, 1:CAP], lane_own[:, 1:CAP], lane_own[:, 0:CAP - 1], ALU.is_equal))
            settle()
            did(v.tensor_tensor_scan(rank, same, same, 0.0, ALU.mult, ALU.add))
            settle()
            did(v.scalar_tensor_tensor(out=slot, in0=lane_own, scalar=float(SLOTS), in1=rank, op0=ALU.mult, op1=ALU.add))
            did(v.tensor_scalar(same, rank, float(RANKS), None, ALU.is_lt))
            settle()
            v.wait_ge(consts_in, 16 * N_CONSTS)
            did(v.tensor_scalar(slot, slot, part[:, 0:1], -SKIP, ALU.add, ALU.add))
            did(v.scalar_tensor_tensor(out=same, in0=lane_list[:, :], scalar=0.0, in1=same, op0=ALU.is_gt, op1=ALU.mult))
            did(v.tensor_scalar(lane_own, rank, float(RANKS), None, ALU.is_ge))
            settle()
            did(v.tensor_tensor(slot, slot, same, ALU.mult))
            did(v.scalar_tensor_tensor(out=lane_own, in0=lane_list[:, :], scalar=0.0, in1=lane_own, op0=ALU.is_gt, op1=ALU.mult))
            settle()
            did(v.tensor_reduce(flags[:, 1:2], lane_own, AX, ALU.max))
            v.tensor_scalar(slot_i[:, :], slot, SKIP, None, ALU.add).then_inc(slots_ready, 1)

            def hot_block(i, par):
                v.tensor_tensor(hot_own[:, par, 0:P, :], bc(own_h[:, bass.ds(i * 16, 16)], 1, [128, P, 16]),
                                hot[:, 0:P, :], ALU.is_equal)
                v.tensor_tensor(hot_tile[:, par, :, :], bc(tile_h[:, bass.ds(i * 16, 16)], 1, [128, NT, 16]),
                                hot[:, 0:NT, :], ALU.is_equal).then_inc(hot_ready, 1)

            hot_block(0, 0)
            hot_block(1, 1)
            with v.Fori(1, JG // 32) as i:
                for par in range(2):
                    v.wait_ge(hot_used, 2 * i + par - 1)
                    hot_block(2 * i + par, par)

            v.wait_ge(tgt_in, 16)
            did(v.tensor_copy(tgt[:, :], tgt_i[:, :]))
            did(v.tensor_copy(iota_h[:, :], iota[:, 0:384]))
            settle()
            base = own.n
            with v.Fori(0, JA // 2) as i:
                for par in range(2):
                    j = 2 * i + par
                    v.tensor_scalar(hit[:, par, :], iota_h[:, :], tgt[:, bass.ds(j, 1)], iota[:, bass.ds(j + 1, 1)],
                                    ALU.is_equal, ALU.mult).then_inc(vec, 1)
                    v.wait_ge(vec, base + 4 * i + 2 * par + 1)
                    v.tensor_tensor(lane_last[:, :], lane_last[:, :], hit[:, par, :], ALU.max).then_inc(vec, 1)
                    v.wait_ge(vec, base + 4 * i + 2 * par + 2)
            own.n += 2 * JA
            v.sem_inc(lane_last_ready, 1)

            v.wait_ge(hist_done, 1)
            v.tensor_copy(clampT[:, 0:P], ps[0:NT, 4, 0:P]).then_inc(hist_copied, 1)
            v.wait_ge(histT_done, 1)
            did(v.tensor_copy(clamped[0:P, :], ps[0:P, 5, 0:NT]))

            v.wait_ge(lastT_done, 1)
            lane_no = iota[0:P, 0:128].unsqueeze(1).to_broadcast([P, KT, 128])
            lastp = ps[0:P, 6, 0:KT * 128].rearrange("p (k l) -> p k l", k=KT)
            did(v.scalar_tensor_tensor(out=last[0:P, :, :], in0=lastp, scalar=0.0, in1=lane_no, op0=ALU.is_gt, op1=ALU.mult))
            settle()
            did(v.scalar_tensor_tensor(out=last[0:P, :, :], in0=last[0:P, :, :], scalar=float(JA), in1=lastp,
                                       op0=ALU.mult, op1=ALU.add))
            settle()
            did(v.tensor_reduce(lastf[0:P, 0, :], last[0:P, :, :], AX, ALU.max))
            settle()
            did(v.tensor_scalar(lastf[0:P, 1, :], lastf[0:P, 0, :], 0.0, None, ALU.is_gt))
            v.tensor_scalar(last_i[0:P, :], lastf[0:P, 0, :], -1.0, 0.0, ALU.add, ALU.max).then_inc(last_ready, 1)
            v.wait_ge(attr_in, 16 * KT)
            v.wait_ge(weights_in, 16 * N_WEIGHTS)
            for k in range(KT):
                for i in range(3):
                    did(v.scalar_tensor_tensor(out=bias[0:P, k, :], in0=we[0:P, i, :], scalar=attr[0:P, k, i:i + 1],
                                               in1=we[0:P, 3, :] if i == 0 else bias[0:P, k, :],
                                               op0=ALU.mult, op1=ALU.add))
                    settle()
                did(v.tensor_scalar(bias[0:P, k, :], bias[0:P, k, :], lastf[0:P, 1, k:k + 1], None, ALU.mult))
            settle()

            def three_parts(out_parts, value, left, last_sem):
                did(v.tensor_copy(out_parts(0), value))
                settle()
                did(v.tensor_tensor(left, value, out_parts(0), ALU.subtract))
                settle()
                did(v.tensor_copy(out_parts(1), left))
                settle()
                v.tensor_tensor(out_parts(2), left, out_parts(1), ALU.subtract).then_inc(last_sem, 1)

            three_parts(lambda c: bparts[0:P, :, :, c], bias[0:P, :, :], nrest[0:P, :, :], bparts_ready)
            v.wait_ge(biasT_done, 1)
            v.tensor_copy(biasT[0:3 * H, :], ps[0:3 * H, 7, 0:L]).then_inc(biasT_ready, 1)
            v.wait_ge(mix_done, 1)
            v.memset(xT[D:D + 1, :], 1.0).then_inc(ones_set, 1)
            v.sem_inc(vec_banks, 1)

            v.wait_ge(table_in, 16)
            for c in range(0, CAP, 8):
                did(v.max(own_list[0:P, c:c + 8], own_tab[0:P, :]))
                settle()
                did(v.match_replace(own_tab[0:P, :], own_list[0:P, c:c + 8], own_tab[0:P, :], -1.0))
                settle()
            did(v.tensor_reduce(flags[0:P, 2:3], own_tab[0:P, :], AX, ALU.max))

            def decode(ready):
                did(v.tensor_scalar(own_list[0:P, :], own_list[0:P, :], 0.0, None, ALU.max))
                settle()
                did(v.tensor_copy(own_int[0:P, :], own_list[0:P, :]))
                did(v.tensor_scalar(keep[0:P, :], own_list[0:P, :], 0.0, None, ALU.is_le))
                settle()
                did(v.tensor_scalar(own_tmp_i[0:P, 0, :], own_int[0:P, :], SRC_BITS, 2 ** TILE_BITS - 1,
                                    ALU.logical_shift_right, ALU.bitwise_and))
                did(v.tensor_scalar(own_tmp_i[0:P, 1, :], own_int[0:P, :], 2 ** SRC_BITS - 1, None, ALU.bitwise_and))
                settle()
                did(v.scalar_tensor_tensor(out=seg[0:P, :], in0=keep[0:P, :], scalar=-64.0, in1=own_tmp_i[0:P, 0, :],
                                           op0=ALU.mult, op1=ALU.add))
                did(v.tensor_scalar(src_idx[0:P, :], own_tmp_i[0:P, 1, :], -1.0, 0.0, ALU.add, ALU.max))
                settle()
                did(v.memset(keep[0:P, 0:1], 0.0))
                did(v.tensor_tensor(keep[0:P, 1:CAP], seg[0:P, 1:CAP], seg[0:P, 0:CAP - 1], ALU.is_equal))
                did(v.tensor_tensor(member[0:P, :, :], bc(seg[0:P, :], 2, [P, CAP, NT]),
                                    bc(iota[0:P, 0:NT], 1, [P, CAP, NT]), ALU.is_equal))
                did(v.tensor_tensor(at_least[0:P, :, :], bc(seg[0:P, :], 1, [P, NT, CAP]),
                                    bc(iota[0:P, 0:NT], 2, [P, NT, CAP]), ALU.is_ge))
                settle()
                did(v.tensor_scalar(keep[0:P, :], keep[0:P, :], -1.0, -NEG, ALU.add, ALU.mult))
                did(v.tensor_reduce(endf[0:P, 0, :], at_least[0:P, :, :], AX, ALU.add))
                did(v.tensor_scalar(own_row[0:P, :], part[0:P, :], float(CAP) / RANKS, None, ALU.mult))
                settle()
                did(v.tensor_tensor(has_real[0:P, 0:NT - 1], endf[0:P, 0, 0:NT - 1], endf[0:P, 0, 1:NT], ALU.is_gt))
                did(v.tensor_scalar(has_real[0:P, NT - 1:NT], endf[0:P, 0, NT - 1:NT], 0.0, None, ALU.is_gt))
                did(v.tensor_scalar(endf[0:P, 1, :], endf[0:P, 0, :], -1.0, 0.0, ALU.add, ALU.max))
                settle()
                v.tensor_scalar(end_idx[0:P, :], endf[0:P, 1, :], own_row[0:P, 0:1], None, ALU.add).then_inc(ready, 1)

            settle()
            did(v.tensor_reduce(flags[:, 3:4], flags[:, 0:3], AX, ALU.max))
            decode(lists_ready)
            settle()
            v.sem_inc(flags_ready, 1)

            def normalise(n, x_, c_, width, mean_row):
                r3 = [P, NT, width]
                did(v.tensor_reduce(stat[0:P, 0, :], x_, AX, ALU.add))
                settle()
                did(v.tensor_scalar(stat[0:P, 1, :], stat[0:P, 0, :], 1.0 / width, None, ALU.mult))
                settle()
                v.tensor_tensor(c_, x_, bc(stat[0:P, 1, :], 2, r3), ALU.subtract).then_inc(centred, 1)
                v.wait_ge(squared, n)
                did(v.tensor_reduce(stat[0:P, 0, :], mean_row, AX, ALU.add))
                settle()
                v.tensor_scalar(stat[0:P, 2, :], stat[0:P, 0, :], 1.0 / width, EPS, ALU.mult, ALU.add).then_inc(var_ready, 1)
                v.wait_ge(std_ready, n)
                did(v.reciprocal(stat[0:P, 1, :], stat[0:P, 3, :]))
                settle()
                ins = v.tensor_tensor(c_, c_, bc(stat[0:P, 1, :], 2, r3), ALU.mult)
                return ins

            v.wait_ge(h_ready, 3)
            normalise(1, h[0:P, :, :], xn[0:P, :, :], D, sq[0:P, :, :]).then_inc(xn_ready, 1)

            v.memset(onT[D:D + 1, :], 1.0).then_inc(onT_one, 1)

            def make_parts(b, n):
                v.wait_ge(misc_free, n + 1)
                v.tensor_copy(parts[:, 0, :], qk32[:, :]).then_inc(cut, 1)
                v.wait_ge(cut, 3 * b + 1)
                v.tensor_tensor(rest[:, :], qk32[:, :], parts[:, 0, :], ALU.subtract).then_inc(cut, 1)
                v.wait_ge(cut, 3 * b + 2)
                v.tensor_copy(parts[:, 1, :], rest[:, :]).then_inc(cut, 1)
                v.wait_ge(cut, 3 * b + 3)
                v.tensor_tensor(parts[:, 2, :], rest[:, :], parts[:, 1, :], ALU.subtract).then_inc(parts_ready, 1)

            def passed(kind, par, n, b):
                if kind == "qk":
                    make_parts(b, n)
                elif kind in ("q0", "q1", "q2", "q3"):
                    v.wait_ge(misc_full, n + 1)
                    v.tensor_copy(qst[:, par, int(kind[1]), :], ps[:, 7, 0:L]).then_inc(misc_free, 1)
                elif kind == "maxT":
                    v.wait_ge(misc_full, n + 1)
                    v.tensor_copy(maxT[:, :], ps[0:3 * H, 7, 0:L]).then_inc(misc_free, 1)
                elif kind in ("norm0", "norm1"):
                    g = int(kind[4])
                    v.wait_ge(misc_full, n + 1)
                    turned = ps[0:P, 7, 0:KT * 128].rearrange("p (k q c) -> p k q c", k=KT, q=4)
                    v.reciprocal(rden[0:P, :, :], turned[:, :, :, HD]).then_inc(rden_ready, 1)
                    v.wait_ge(rden_ready, 2 * b + g + 1)
                    v.tensor_tensor(on[0:P, :, g * 32:(g + 1) * 32].rearrange("p k (q d) -> p k q d", q=4),
                                    turned[:, :, :, 0:HD], bc(rden[0:P, :, :], 3, [P, KT, 4, HD]),
                                    ALU.mult).then_inc(misc_free, 1)
                elif kind == "out":
                    v.wait_ge(misc_full, n + 1)
                    rows = h[0:P, bass.ds(b * KT, KT), :]
                    v.tensor_tensor(rows, ps[0:P, 7, 0:KT * D].rearrange("p (k d) -> p k d", k=KT), rows,
                                    ALU.add).then_inc(misc_free, 1)

            for n, kind in enumerate(PRE):
                passed(kind, 0, n, 0)

            def batch(b, par, prelims):
                n = b * MISC + len(PRE)
                for kind, k in order(prelims):
                    if kind == "score":
                        v.wait_ge(score_full, b * H + k + 1)
                        v.tensor_reduce(negmax[0:P, :, k], ps[0:P, 3 * (k % 2):3 * (k % 2) + 3, 0:L], AX, ALU.max,
                                        negate=True).then_inc(max_done, 1)
                    elif kind not in ("exp", "pv"):
                        if kind == "maxT":
                            v.wait_ge(max_done, b * H + H)
                            part_ = [nparts[0:P, :, :, c] for c in range(3)]
                            v.tensor_copy(part_[0], negmax[0:P, :, :]).then_inc(ncut, 1)
                            v.wait_ge(ncut, 3 * b + 1)
                            v.tensor_tensor(nrest[0:P, :, :], negmax[0:P, :, :], part_[0], ALU.subtract).then_inc(ncut, 1)
                            v.wait_ge(ncut, 3 * b + 2)
                            v.tensor_copy(part_[1], nrest[0:P, :, :]).then_inc(ncut, 1)
                            v.wait_ge(ncut, 3 * b + 3)
                            v.tensor_tensor(part_[2], nrest[0:P, :, :], part_[1], ALU.subtract).then_inc(negmax_ready, 1)
                        nxt = kind in PRE
                        passed(kind, 1 - par if nxt else par, n, b + 1 if nxt else b)
                        n = n + 1

            batches(v, batch)
            v.wait_ge(misc_free, B * MISC)
            v.sem_inc(attn_added, B)
            normalise(2, h[0:P, :, :], xn[0:P, :, :], D, sq[0:P, :, :]).then_inc(xn_ready, 1)

            v.wait_ge(gat_done, 1)
            hg = ps[0:P, 7, 0:NT * GF].rearrange("p (t f) -> p t f", t=NT)
            r16 = [P, NT, GF]

            def by_head(ap):
                return ap.rearrange("p t (h e) -> p t h e", h=GH)

            did(v.tensor_copy(tab[0:P, :, 0:GF], hg))
            did(v.tensor_tensor(gprod[0:P, :, :], hg, bc(vecs[0:P, 0, :], 1, r16), ALU.mult))
            settle()
            did(v.tensor_reduce(tab[0:P, :, GF:GF + GH], by_head(gprod[0:P, :, :]), AX, ALU.add))
            settle()
            did(v.tensor_tensor(gprod[0:P, :, :], hg, bc(vecs[0:P, 1, :], 1, r16), ALU.mult))
            v.sem_inc(tab_ready, 1)
            settle()
            did(v.tensor_reduce(adst[0:P, :, :], by_head(gprod[0:P, :, :]), AX, ALU.add))
            settle()
            wide3 = wide[0:P, :].rearrange("p (c t) -> p c t", t=NT)

            def target_scores():
                for g in range(GH):
                    did(v.tensor_tensor(wide3, member[0:P, :, :], bc(adst[0:P, :, g], 1, [P, CAP, NT]), ALU.mult))
                    settle()
                    did(v.tensor_reduce(adst_e[0:P, :, g], wide3, AX, ALU.add))
                    settle()

            target_scores()

            v.sem_inc(y_copied, EX)
            with v.Fori(0, B) as b:
                for e in range(EX):
                    v.wait_ge(y_full, b * EX + e + EX + 1)
                    v.tensor_copy(yexp[0:P, bass.ds(b * KT, KT), e, :],
                                  ps[0:P, 4 + e, 0:KT * D].rearrange("p (k d) -> p k d", k=KT)).then_inc(y_copied, 1)

            def edge_sums(ask_exp):
                did(v.tensor_tensor(score[0:P, :, :], got[0:P, :, GF:GF + GH], adst_e[0:P, :, :], ALU.add))
                did(v.memset(expo[0:P, 0, 0:1, :], NEG))
                settle()
                did(v.scalar_tensor_tensor(out=score[0:P, :, :], in0=score[0:P, :, :], scalar=0.2, in1=score[0:P, :, :],
                                           op0=ALU.mult, op1=ALU.max))
                settle()
                for g in range(GH):
                    did(v.tensor_tensor_scan(run_max[0:P, :, g], keep[0:P, :], score[0:P, :, g], NEG, ALU.add, ALU.max))
                settle()
                did(v.tensor_tensor(expo[0:P, 0, 1:CAP, :], run_max[0:P, 0:CAP - 1, :], run_max[0:P, 1:CAP, :], ALU.subtract))
                did(v.tensor_tensor(expo[0:P, 1, :, :], score[0:P, :, :], run_max[0:P, :, :], ALU.subtract))
                did(v.tensor_copy(res[0:P, :, 0:GH], run_max[0:P, :, :]))
                settle()
                did(v.tensor_tensor(expo[0:P, 0, 1:CAP, :], expo[0:P, 0, 1:CAP, :], bc(keep[0:P, 1:CAP], 2, [P, CAP - 1, GH]),
                                    ALU.add))
                settle()
                ask_exp()
                decay, weight = expo[0:P, 0, :, :], expo[0:P, 1, :, :]
                did(v.tensor_tensor(by_head(msg[0:P, :, :]), by_head(got[0:P, :, 0:GF]), bc(weight, 3, [P, CAP, GH, EX]), ALU.mult))
                for g in range(GH):
                    did(v.tensor_tensor_scan(res[0:P, :, GH + g], decay[:, :, g], weight[:, :, g], 0.0, ALU.mult, ALU.add))
                settle()
                for f in range(GF):
                    did(v.tensor_tensor_scan(res[0:P, :, 2 * GH + f], decay[:, :, f // EX], msg[0:P, :, f], 0.0, ALU.mult, ALU.add))
                settle()

            def ask_exp():
                v.sem_inc(exp_in, 1)
                v.wait_ge(exp_out, 1)

            v.wait_ge(gathered, 16 * CAP)
            edge_sums(ask_exp)
            v.sem_inc(res_ready, 1)

            v.wait_ge(lastrow_in, 16)
            r4 = [P, NT, GH]
            e_self, e_clamp, e_real, mask = (s[0:P, :, :] for s in (s1, s2, s3, s4))
            did(v.tensor_tensor(e_self, tab[0:P, :, GF:GF + GH], adst[0:P, :, :], ALU.add))
            did(v.tensor_tensor(e_clamp, adst[0:P, :, :], bc(lastrow[0:P, GF:GF + GH], 1, r4), ALU.add))
            did(v.tensor_scalar(endf[0:P, 0, :], clamped[0:P, :], 0.0, None, ALU.is_gt))
            settle()
            for e_ in (e_self, e_clamp):
                did(v.scalar_tensor_tensor(out=e_, in0=e_, scalar=0.2, in1=e_, op0=ALU.mult, op1=ALU.max))
            did(v.tensor_scalar(endf[0:P, 0, :], endf[0:P, 0, :], -1.0, -NEG, ALU.add, ALU.mult))
            settle()
            did(v.tensor_tensor(e_clamp, e_clamp, bc(endf[0:P, 0, :], 2, r4), ALU.add))
            settle()
            did(v.tensor_tensor(mask, e_self, e_clamp, ALU.max))
            v.wait_ge(flags_done, 1)
            v.tensor_reduce(flag_row[0:1, 0:1], ps[0:1, 0, 0:128], AX, ALU.max).then_inc(over_own, 1)
            v.wait_ge(over_own, 1)
            v.tensor_scalar(over_i[:, :], flag_row[0:1, 0:1], 0.0, None, ALU.is_gt).then_inc(over_ready, 1)
            v.wait_ge(ends_in, 16 * NT)
            settle()

            def ask_group_exp():
                settle()
                v.sem_inc(g_exp_in, 1)
                take(v, g_exp_out, 1)

            r4 = [P, NT, GH]

            def group_sums(i):
                v.sem_clear(vec)
                own.n = 0
                v.sem_inc(g_next, 1)
                take(v, g_raw_in, 32)
                raw = [lane_tmp[0:P, k, 0:GROUP] for k in range(4)]
                key, tmp = own_tab[0:P, 0:GROUP], own_tab[0:P, GROUP:2 * GROUP]
                edge_keys(raw_i[0:P, 0, :], raw_i[0:P, 1, :], key, raw[0], raw[1], raw[2], tmp)
                settle()
                did(v.scalar_tensor_tensor(out=raw[0], in0=raw[1], scalar=-float(P), in1=raw_i[0:P, 1, :],
                                           op0=ALU.mult, op1=ALU.add))
                did(v.tensor_scalar(own_row[0:P, :], part[0:P, :], 1.0 / RANKS, None, ALU.mult))
                settle()
                did(v.scalar_tensor_tensor(out=key, in0=raw[0], scalar=own_row[0:P, 0:1], in1=key,
                                           op0=ALU.is_equal, op1=ALU.mult))
                did(v.memset(own_list[0:P, :], 0.0))
                settle()
                for c in range(0, GROUP, 8):
                    did(v.max(own_list[0:P, c:c + 8], key))
                    settle()
                    did(v.match_replace(key, own_list[0:P, c:c + 8], key, -1.0))
                    settle()
                decode(vec)
                own.n += 1
                settle()
                v.sem_inc(g_lists, 1)
                target_scores()
                take(v, g_rows_in, 1)
                edge_sums(ask_group_exp)
                v.sem_inc(g_res, 1)
                take(v, g_ends_in, 1)
                g_real, g_max = gsq[0:P, :, 0:GH], gsq[0:P, :, GH:2 * GH]
                did(v.tensor_scalar(endf[0:P, 1, :], has_real[0:P, :], -1.0, -NEG, ALU.add, ALU.mult))
                settle()
                did(v.tensor_tensor(g_real, ends[0:P, :, 0:GH], bc(endf[0:P, 1, :], 2, r4), ALU.add))
                settle()
                did(v.tensor_tensor(g_max, g_real, acc[0:P, :, 0:GH], ALU.max))
                settle()
                did(v.tensor_tensor(wts[0:P, 0, :, :], acc[0:P, :, 0:GH], g_max, ALU.subtract))
                did(v.tensor_tensor(wts[0:P, 1, :, :], g_real, g_max, ALU.subtract))
                settle()
                did(v.tensor_copy(acc[0:P, :, 0:GH], g_max))
                ask_group_exp()
                did(v.tensor_tensor(wts[0:P, 1, :, :], wts[0:P, 1, :, :], bc(has_real[0:P, :], 2, r4), ALU.mult))
                settle()
                for part_, k in ((acc, 0), (ends, 1)):
                    did(v.tensor_tensor(part_[0:P, :, GH:2 * GH], part_[0:P, :, GH:2 * GH], wts[0:P, k, :, :], ALU.mult))
                    did(v.tensor_tensor(by_head(part_[0:P, :, 2 * GH:RES]), by_head(part_[0:P, :, 2 * GH:RES]),
                                        bc(wts[0:P, k, :, :], 3, [P, NT, GH, EX]), ALU.mult))
                settle()
                did(v.tensor_tensor(acc[0:P, :, GH:RES], acc[0:P, :, GH:RES], ends[0:P, :, GH:RES], ALU.add))
                settle()

            counted = own.n
            v.wait_ge(over_ready, 1)
            over = v.value_load(over_i[0:1, 0:1], min_val=0, max_val=1)
            with v.If(over > 0):
                did(v.memset(acc[0:P, :, :], 0.0))
                settle()
                did(v.memset(acc[0:P, :, 0:GH], NEG))
                settle()
                with v.Fori(0, E_GAT // GROUP) as i:
                    group_sums(i)
                v.sem_clear(vec)
                own.n = 0
                did(v.tensor_copy(ends[0:P, :, :], acc[0:P, :, :]))
                did(v.memset(has_real[0:P, :], 1.0))
                settle()
                v.sem_inc(vec, counted - own.n)
            own.n = counted
            did(v.tensor_scalar(endf[0:P, 1, :], has_real[0:P, :], -1.0, -NEG, ALU.add, ALU.mult))
            settle()
            did(v.tensor_tensor(e_real, ends[0:P, :, 0:GH], bc(endf[0:P, 1, :], 2, r4), ALU.add))
            settle()
            did(v.tensor_tensor(mask, mask, e_real, ALU.max))
            settle()
            for k, e_ in enumerate((e_real, e_self, e_clamp)):
                did(v.tensor_tensor(wts[0:P, k, :, :], e_, mask, ALU.subtract))
            settle()
            v.sem_inc(exp_in, 1)
            v.wait_ge(exp_out, 2)
            did(v.tensor_tensor(wts[0:P, 2, :, :], wts[0:P, 2, :, :], bc(clamped[0:P, :], 2, r4), ALU.mult))
            did(v.tensor_tensor(e_real, ends[0:P, :, GH:2 * GH], wts[0:P, 0, :, :], ALU.mult))
            r44 = [P, NT, GH, EX]
            did(v.tensor_tensor(by_head(gnum[0:P, :, :]), by_head(ends[0:P, :, 2 * GH:RES]), bc(wts[0:P, 0, :, :], 3, r44), ALU.mult))
            did(v.tensor_tensor(by_head(gprod[0:P, :, :]), by_head(tab[0:P, :, 0:GF]), bc(wts[0:P, 1, :, :], 3, r44), ALU.mult))
            settle()
            did(v.tensor_tensor(e_real, e_real, wts[0:P, 1, :, :], ALU.add))
            did(v.tensor_tensor(gnum[0:P, :, :], gnum[0:P, :, :], gprod[0:P, :, :], ALU.add))
            settle()
            did(v.tensor_tensor(e_real, e_real, wts[0:P, 2, :, :], ALU.add))
            did(v.tensor_tensor(by_head(gprod[0:P, :, :]), by_head(bc(lastrow[0:P, 0:GF], 1, r16)),
                                bc(wts[0:P, 2, :, :], 3, r44), ALU.mult))
            settle()
            did(v.tensor_tensor(gnum[0:P, :, :], gnum[0:P, :, :], gprod[0:P, :, :], ALU.add))
            did(v.tensor_scalar(e_real, e_real, 1e-16, None, ALU.add))
            settle()
            did(v.reciprocal(e_real, e_real))
            settle()
            did(v.tensor_tensor(by_head(gnum[0:P, :, :]), by_head(gnum[0:P, :, :]), bc(e_real, 3, r44), ALU.mult))
            settle()
            did(v.tensor_tensor(gnum[0:P, :, :], gnum[0:P, :, :], bc(vecs[0:P, 2, :], 1, r16), ALU.add))
            settle()
            did(normalise(3, gnum[0:P, :, :], gnum[0:P, :, :], GF, gsq[0:P, :, :]))
            settle()
            did(v.tensor_tensor(gnum[0:P, :, :], gnum[0:P, :, :], bc(vecs[0:P, 3, :], 1, r16), ALU.mult))
            settle()
            did(v.tensor_tensor(gnum[0:P, :, :], gnum[0:P, :, :], bc(vecs[0:P, 4, :], 1, r16), ALU.add))
            settle()

            did(v.tensor_reduce(s1[0:P, :, :], gnum[0:P, :, :].rearrange("p t (h e) -> p t e h", h=GH), AX, ALU.add))
            settle()
            sc = s2[0:P, :, :]
            did(v.tensor_scalar(sc, s1[0:P, :, :], 1.0 / GH, None, ALU.mult))
            settle()
            ree = [P, NT, EX, EX]
            other, mine = bc(sc, 2, ree), bc(sc, 3, ree)
            first = lower[0:P, :].rearrange("p (e j) -> p e j", e=EX).unsqueeze(1).to_broadcast(ree)
            beats = gprod[0:P, :, :].rearrange("p t (e j) -> p t e j", e=EX)
            ties = gnum[0:P, :, :].rearrange("p t (e j) -> p t e j", e=EX)
            did(v.tensor_tensor(beats, other, mine, ALU.is_gt))
            did(v.tensor_tensor(ties, other, mine, ALU.is_equal))
            did(v.tensor_reduce(stat[0:P, 0, :], sc, AX, ALU.max))
            settle()
            did(v.tensor_tensor(ties, ties, first, ALU.mult))
            v.tensor_tensor(gate[0:P, :, :], sc, bc(stat[0:P, 0, :], 2, [P, NT, EX]), ALU.subtract).then_inc(exp_in, 1)
            settle()
            did(v.tensor_tensor(beats, beats, ties, ALU.add))
            settle()
            did(v.tensor_reduce(s3[0:P, :, :], beats, AX, ALU.add))
            settle()
            did(v.tensor_scalar(s3[0:P, :, :], s3[0:P, :, :], 2.0, None, ALU.is_lt))
            settle()
            v.wait_ge(exp_out, 3)
            did(v.tensor_tensor(gate[0:P, :, :], gate[0:P, :, :], s3[0:P, :, :], ALU.mult))
            settle()
            did(v.tensor_reduce(stat[0:P, 0, :], gate[0:P, :, :], AX, ALU.add))
            settle()
            did(v.reciprocal(stat[0:P, 1, :], stat[0:P, 0, :]))
            settle()
            did(v.tensor_tensor(gate[0:P, :, :], gate[0:P, :, :], bc(stat[0:P, 1, :], 2, [P, NT, EX]), ALU.mult))
            settle()
            v.wait_ge(y_copied, B * EX + EX)
            for e in range(EX):
                did(v.tensor_tensor(yexp[0:P, :, e, :], yexp[0:P, :, e, :], bc(gate[0:P, :, e], 2, [P, NT, D]), ALU.mult))
            settle()
            for e in range(EX):
                ins = v.tensor_tensor(h[0:P, :, :], h[0:P, :, :], yexp[0:P, :, e, :], ALU.add)
                if e < EX - 1:
                    did(ins)
                    settle()
                else:
                    ins.then_inc(out_ready, 1)


_ARGS = ("x", "w_step", "w_in", "w_mix", "w_c", "att_tgt", "att_attr", "w_qk", "w_v", "w_o", "w_e",
         "w_gat", "att_vec", "w1", "b2", "w2", "gat_src", "gat_dst")


def layouts(x, L0_tok_W1, L0_tok_b1, L0_tok_W2, L0_tok_b2, L0_tok_W3, L0_tok_b3, L0_tok_W4, L0_tok_b4,
            L0_attn_edge_index, L0_attn_edge_attr, L0_attn_Wq, L0_attn_bq, L0_attn_Wk, L0_attn_bk, L0_attn_Wv,
            L0_attn_bv, L0_attn_Wo, L0_attn_bo, L0_attn_We, L0_attn_be, L0_ffn_W_gat, L0_ffn_att_src,
            L0_ffn_att_dst, L0_ffn_b_gat, L0_ffn_ln_gamma, L0_ffn_ln_beta, L0_ffn_W1, L0_ffn_b1, L0_ffn_W2,
            L0_ffn_b2, L0_ffn_edge_index):
    cat = np.concatenate
    z = np.zeros((D, D), np.float32)
    step = cat([cat([L0_tok_W2.T, z], 1), cat([z, L0_tok_W2.T], 1)], 0)
    one_half = cat([L0_tok_W1.T, L0_tok_b1[None], L0_tok_b2[None]], 0)
    wv = np.zeros((D + 1, H, 32), np.float32)
    wv[:D, :, :HD] = L0_attn_Wv.reshape(D, H, HD)
    wv[D, :, :HD] = L0_attn_bv.reshape(H, HD)
    wv[D, :, HD] = 1
    w1 = cat([L0_ffn_W1, L0_ffn_b1[:, None, :]], 1)
    return {
        "x": x,
        "w_step": step,
        "w_in": cat([one_half, one_half], 1),
        "w_mix": cat([L0_tok_W4.T, L0_tok_W4.T], 0),
        "w_c": cat([L0_tok_W3.T, L0_tok_b3[None], L0_tok_b4[None], L0_tok_b4[None]], 0),
        "att_tgt": L0_attn_edge_index[1].reshape(128, JA),
        "att_attr": L0_attn_edge_attr,
        "w_qk": cat([cat([L0_attn_Wq, L0_attn_bq[None]], 0), cat([L0_attn_Wk, L0_attn_bk[None]], 0)], 1),
        "w_v": wv.reshape(D + 1, 32 * H),
        "w_o": cat([L0_attn_Wo, L0_attn_bo[None]], 0),
        "w_e": cat([L0_attn_We, L0_attn_be[None]], 0),
        "w_gat": L0_ffn_W_gat,
        "att_vec": np.stack([L0_ffn_att_src.reshape(-1), L0_ffn_att_dst.reshape(-1), L0_ffn_b_gat,
                             L0_ffn_ln_gamma, L0_ffn_ln_beta]),
        "w1": np.transpose(w1, (1, 0, 2)),
        "b2": L0_ffn_b2[None],
        "w2": np.transpose(L0_ffn_W2, (1, 0, 2)),
        "gat_src": L0_ffn_edge_index[0].reshape(128, JG),
        "gat_dst": L0_ffn_edge_index[1].reshape(128, JG),
    }


def kernel(**inputs):
    import concourse.bacc as bacc
    from concourse.bass_utils import run_bass_kernel_spmd

    laid = layouts(**{k: np.asarray(a) for k, a in inputs.items()})
    laid.update(constants())
    nc = bacc.Bacc("TRN2", target_bir_lowering=False, num_devices=1)
    arrays, args = {}, {}
    for name, a in laid.items():
        a = np.ascontiguousarray(a)
        arrays[f"in_{name}"] = a
        args[name] = nc.dram_tensor(f"in_{name}", a.shape, mybir.dt.from_np(a.dtype), kind="ExternalInput").ap()
    out = nc.dram_tensor("out_dram", (B, L, D), F32, kind="ExternalOutput").ap()
    graph_transformer_block(nc, out=out, **args)
    r = run_bass_kernel_spmd(nc, [arrays], core_ids=[0])
    return r.results[0]["out_dram"]
```

```python
from contextlib import ExitStack

import numpy as np

import concourse.bass as bass
from concourse import mybir

F32 = mybir.dt.float32
F16 = mybir.dt.float16
BF16 = mybir.dt.bfloat16
I32 = mybir.dt.int32
ALU = mybir.AluOpType
ACT = mybir.ActivationFunctionType
AX = mybir.AxisListType.X
MAX_ALL = bass.bass_isa.ReduceOp.max

B, DIN, L, D = 8, 4, 375, 64
STEPS = 8
H, HD = 8, 8
M = B * L
P = 125
KT = L // P
NT = M // P
GH, EX = 4, 4
GF = GH * EX
HID = 2 * D
E_ATT = 16384
JA = E_ATT // 128
E_GAT = 262144
JG = E_GAT // 128
LAST = M - 1
EPS = 1e-5
NEG = -1e30
MAGIC = 12582912.0

CAP = 104
RANKS = 8
SLOTS = 128 * RANKS
SRC_BITS, TILE_BITS = 12, 5
SKIP = float(P * SLOTS + 72000)
GROUP = 64
PART, KEEP = 128, 48
NPART = JG // PART
KEPT = NPART * KEEP
HOTS = KEPT // 16
ATTR_AT = 8
FEW = 72
NO_SLOT = float(L * 128)
RES = 2 * GH + GF

Q_PART = (0, 0, 1, 0, 2, 1)
K_PART = (0, 1, 0, 2, 0, 1)
BIAS_ROW = 8 * len(Q_PART)
ONES_ROW = 3 * H


def constants():
    bf = mybir.dt.np(BF16)
    sel = np.zeros((128, 2, 3, 4, 128), np.float32)
    ext = np.zeros((3 * H + 1, 2, 4, 128), np.float32)
    row = np.zeros((3 * H, H, P), np.float32)
    for h in range(H):
        pair, base = h // 2, 64 * (h % 2)
        for c, (qp, kp) in enumerate(zip(Q_PART, K_PART)):
            for d in range(HD):
                sel[h * HD + d, 0, qp, pair, base + c * HD + d] = 1
                sel[64 + h * HD + d, 1, kp, pair, base + c * HD + d] = 1
        for part in range(3):
            ext[ONES_ROW, 0, pair, base + BIAS_ROW + part] = 1
            ext[h * 3 + part, 1, pair, base + BIAS_ROW + part] = 1
            row[h * 3 + part, h, :] = 1
    eye = np.eye(128, dtype=np.float32)
    lane = np.broadcast_to(np.arange(128, dtype=np.float32), (128, 128))
    iota = np.broadcast_to(np.arange(512, dtype=np.float32), (128, 512))
    scale = np.ones((128, 1), np.float32)
    scale[:64] = HD ** -0.5
    hot = np.broadcast_to(np.arange(128, dtype=np.float32)[None, :, None], (128, 128, 16))
    hot = np.ascontiguousarray(hot).astype(bf)
    lower = np.tril(np.ones((EX, EX), np.float32), -1)
    return {
        "c_sel": sel.astype(bf), "c_ext": ext.astype(bf), "c_row": row.astype(bf),
        "c_eye": eye, "c_eyeb": eye.astype(bf), "c_iota": np.ascontiguousarray(iota),
        "c_scale": scale, "c_hot": hot,
        "c_part": RANKS * np.arange(128, dtype=np.float32)[:, None],
        "c_lower": np.ascontiguousarray(np.broadcast_to(lower.reshape(1, -1), (128, EX * EX))),
    }


def graph_transformer_block(nc, x, w_step, w_in, w_mix, w_c,
                            att_tgt, att_attr, w_qk, w_v, w_o, w_e,
                            w_gat, att_vec, w1, b2, w2, gat_src, gat_dst,
                            c_sel, c_ext, c_row, c_eye, c_eyeb, c_iota, c_scale, c_hot, c_part, c_lower,
                            out):
    ctx = ExitStack()
    with ctx:
        def sb(name, shape, dt=F32):
            return ctx.enter_context(nc.sbuf_tensor(name, shape, dt))

        def sem(name):
            return ctx.enter_context(nc.semaphore(name))

        exchange = nc.dram_tensor("exchange", (P * SLOTS, 1), F32, kind="Internal").ap()
        node_rows = nc.dram_tensor("node_rows", (M, GF + GH), F32, kind="Internal").ap()
        beyond_few = nc.dram_tensor("beyond_few", (128, 1), F32, kind="Internal").ap()
        last_edges = nc.dram_tensor("last_edges", (L * 128, 1), F32, kind="Internal").ap()
        edge_rows = nc.dram_tensor("edge_rows", (P * CAP, RES), F32, kind="Internal").ap()

        ps = ctx.enter_context(nc.psum_tensor("ps", [128, 8, 512], F32))

        wstep = sb("wstep", [128, 128])
        win = sb("win", [6, 128])
        wmix = sb("wmix", [128, D])
        wc = sb("wc", [7, D])
        wqk = sb("wqk", [D + 1, 128])
        wv = sb("wv", [D + 1, 32 * H])
        wo = sb("wo", [D + 1, D])
        wgat = sb("wgat", [D, GF])
        we = sb("we", [128, 4, H])
        vecs = sb("vecs", [128, 5, GF])
        w1s = sb("w1s", [D + 1, EX, HID])
        w2s = sb("w2s", [HID, EX, D])
        b2s = sb("b2s", [1, EX, D])
        sel = sb("sel", [128, 2, 3, 4, 128], BF16)
        ext = sb("ext", [ONES_ROW + 1, 2, 4, 128], BF16)
        row = sb("row", [3 * H, H, P], BF16)
        eye = sb("eye", [128, 128])
        eyeb = sb("eyeb", [128, 128], BF16)
        iota = sb("iota", [128, 512])
        qk_scale = sb("qk_scale", [128, 1])
        hot = sb("hot", [128, 128, 16], BF16)
        part = sb("part", [128, 1])
        lower = sb("lower", [128, EX * EX])
        ones1 = sb("ones1", [1, 128])
        tok_x = sb("tok_x", [128, B, L])
        xaug = tok_x[0:7, :, :]
        state = sb("state", [128, B, L + 2])
        add_in = sb("add_in", [128, B, L])
        big = sb("big", [128, 8, JG])

        def view(first, at, shape, dt=F32):
            n = int(np.prod(shape))
            flat = big[:, first:8, :].rearrange("p a b -> p (a b)")
            flat = flat[:, at:at + n] if dt is F32 else flat[:, at:at + n // 2].bitcast(dt)
            names = "abcd"[:len(shape)]
            if len(shape) == 1:
                return flat
            return flat.rearrange(f"p ({' '.join(names)}) -> p {' '.join(names)}", **dict(zip(names[1:], shape[1:])))

        h = sb("h", [128, NT, D])
        xn = sb("xn", [128, NT, D])
        sq = sb("sq", [128, NT, D])
        stat = sb("stat", [128, 4, NT])
        xT = add_in[0:D + 1, :, :].rearrange("p b l -> p (b l)")
        probs = view(0, 0, [2, KT, L])
        vv = view(2, 0, [2, KT, 32 * H])
        qst = view(3, 0, [2, 4, L], BF16)
        kst = view(3, L * 4, [2, 4, L], BF16)
        qk32 = view(5, 0, [L])
        rest = view(5, L, [L])
        parts = view(5, 2 * L, [3, L + 1], BF16)[:, :, 0:L]
        oT = view(5, 4 * L, [2, L])
        xb = view(5, 6 * L, [2, L])[0:D + 1]
        onT = view(5, 8 * L, [L])[0:D + 1]
        on = view(5, 9 * L, [KT, D])
        negmax = sb("negmax", [128, KT, H])
        nrest = sb("nrest", [128, KT, H])
        nparts = sb("nparts", [128, KT, H, 3], BF16)
        maxT = sb("maxT", [3 * H, L], BF16)
        rden = sb("rden", [128, KT, 4])
        tgt = sb("tgt", [128, JA])
        tgt_i = sb("tgt_i", [128, JA], I32)
        more_i = sb("more_i", [1, 1], I32)
        more_row = sb("more_row", [1, 128])
        more_top = sb("more_top", [1, 1])
        last = sb("last", [128, KT, 128])
        lastf = sb("lastf", [128, 2, KT])
        last_i = sb("last_i", [128, KT], I32)
        attr = sb("attr", [128, KT, 3])
        bias = sb("bias", [128, KT, H])
        bparts = sb("bparts", [128, KT, H, 3], BF16)
        biasT = sb("biasT", [ONES_ROW + 1, L], BF16)
        src_i = big[:, 0, :].bitcast(I32)
        dst_i = big[:, 1, :].bitcast(I32)
        f_tile, f_own, f_key, f_real, f_tmp = (big[:, k, :] for k in range(2, 7))
        kept = big[:, 7, 0:KEPT]
        kept_i, low_i, code_i = (big[:, k, 0:KEPT].bitcast(I32) for k in (0, 1, 2))
        no_count, kept_real = big[:, 3, 0:KEPT], big[:, 5, 0:KEPT]
        own_h = sb("own_h", [128, KEPT + 144], BF16)
        tile_h = sb("tile_h", [128, KEPT + 144], BF16)
        hot_own = sb("hot_own", [128, 2, 128, 16], BF16)
        hot_tile = sb("hot_tile", [128, 2, NT, 16], BF16)
        lane_list = sb("lane_list", [128, CAP])
        lane_int = sb("lane_int", [128, CAP], I32)
        lane_tmp = sb("lane_tmp", [128, 4, CAP])
        slot_i = sb("slot_i", [128, CAP], I32)
        own_tab = sb("own_tab", [128, SLOTS])
        own_list = sb("own_list", [128, CAP])
        own_int = sb("own_int", [128, CAP], I32)
        own_tmp_i = sb("own_tmp_i", [128, 2, CAP], I32)
        src_idx = sb("src_idx", [128, CAP], I32)
        seg = sb("seg", [128, CAP])
        keep = sb("keep", [128, CAP])
        member = sb("member", [128, CAP, NT])
        at_least = tok_x[:, :, :].rearrange("p a b -> p (a b)")[:, 0:NT * CAP].rearrange("p (t c) -> p t c", t=NT)
        spare = member[:, :, :].rearrange("p a b -> p (a b)")
        tgt_key, tgt_list, tgt_val, tgt_slot, tgt_new = (spare[:, k * JA:(k + 1) * JA] for k in range(5))
        tgt_no, tgt_j, tgt_slot_i = (spare[:, k * JA:(k + 1) * JA].bitcast(I32) for k in range(5, 8))
        endf = sb("endf", [128, 2, NT])
        end_idx = sb("end_idx", [128, NT], I32)
        has_real = sb("has_real", [128, NT])
        flags = sb("flags", [128, 5])
        clamped = sb("clamped", [128, NT])
        clampT = sb("clampT", [NT, 128])
        got = state[:, :, :].rearrange("p a b -> p (a b)")[:, 0:CAP * (GF + GH)].rearrange(
            "p (c f) -> p c f", f=GF + GH)
        msg = view(7, 0, [CAP, GF])
        adst_e = sb("adst_e", [128, CAP, GH])
        score = sb("score", [128, CAP, GH])
        run_max = sb("run_max", [128, CAP, GH])
        expo = sb("expo", [128, 2, CAP, GH])
        tab = sb("tab", [128, NT, GF + GH])
        adst = sb("adst", [128, NT, GH])
        gprod = sb("gprod", [128, NT, GF])
        lastrow = sb("lastrow", [128, GF + GH])
        ends = sb("ends", [128, NT, RES])
        st_max = sb("st_max", [128, NT, GH])
        st_den = sb("st_den", [128, NT, GH])
        st_num = sb("st_num", [128, NT, GF])
        s1, s2, s3, s4 = (sb(f"s{k}", [128, NT, GH]) for k in range(1, 5))
        acc = view(3, CAP * NT, [NT, RES])
        raw_i = sb("raw_i", [128, 2, GROUP], I32)
        over_i = sb("over_i", [1, 1], I32)
        flag_row = sb("flag_row", [1, 1])
        wts = sb("wts", [128, 3, NT, GH])
        gnum = sb("gnum", [128, NT, GF])
        gsq = sb("gsq", [128, NT, GF])
        own_row = sb("own_row", [128, 1])
        gate = sb("gate", [128, NT, EX])
        hid = tok_x[:, 0:EX, :]
        yexp = view(0, 0, [NT, EX, D])
        wide = view(3, 0, [CAP * NT])
        res = view(5, 0, [CAP, RES])

        tok_in = sem("tok_in")
        mix_in = sem("mix_in")
        edges_in = sem("edges_in")
        consts_in = sem("consts_in")
        tgt_in = sem("tgt_in")
        weights_in = sem("weights_in")
        zeros_set = sem("zeros_set")
        exchange_zeroed = sem("exchange_zeroed")
        state_zeroed = sem("state_zeroed")
        vec = sem("vec")
        act_own = sem("act_own")
        tok_sum = sem("tok_sum")
        tok_state = sem("tok_state")
        mix_done = sem("mix_done")
        h_ready = sem("h_ready")
        slots_ready = sem("slots_ready")
        scattered = sem("scattered")
        table_in = sem("table_in")
        hot_ready = sem("hot_ready")
        hist_done = sem("hist_done")
        hist_added = sem("hist_added")
        clamped_ready = sem("clamped_ready")
        histT_done = sem("histT_done")
        tgt_slots_ready = sem("tgt_slots_ready")
        tgt_listed = sem("tgt_listed")
        more_out = sem("more_out")
        more_in = sem("more_in")
        more_own = sem("more_own")
        more_ready = sem("more_ready")
        last_zeroed = sem("last_zeroed")
        last_scattered = sem("last_scattered")
        more_scattered = sem("more_scattered")
        last_written = sem("last_written")
        last_in = sem("last_in")
        last_ready = sem("last_ready")
        attr_in = sem("attr_in")
        bparts_ready = sem("bparts_ready")
        biasT_done = sem("biasT_done")
        biasT_ready = sem("biasT_ready")
        centred = sem("centred")
        squared = sem("squared")
        var_ready = sem("var_ready")
        std_ready = sem("std_ready")
        xn_ready = sem("xn_ready")
        xT_done = sem("xT_done")
        xT_ready = sem("xT_ready")
        misc_full = sem("misc_full")
        misc_free = sem("misc_free")
        xb_ready = sem("xb_ready")
        qk32_ready = sem("qk32_ready")
        parts_ready = sem("parts_ready")
        score_full = sem("score_full")
        scoreT_full = sem("scoreT_full")
        max_done = sem("max_done")
        exp_done = sem("exp_done")
        pv_done = sem("pv_done")
        oT_ready = sem("oT_ready")
        negmax_ready = sem("negmax_ready")
        attn_added = sem("attn_added")
        gat_done = sem("gat_done")
        tab_ready = sem("tab_ready")
        tab_out = sem("tab_out")
        lastrow_in = sem("lastrow_in")
        gathered = sem("gathered")
        lists_ready = sem("lists_ready")
        hid_full = sem("hid_full")
        hid_ready = sem("hid_ready")
        y_full = sem("y_full")
        y_copied = sem("y_copied")
        exp_in = sem("exp_in")
        exp_out = sem("exp_out")
        res_ready = sem("res_ready")
        res_out = sem("res_out")
        ends_in = sem("ends_in")
        out_ready = sem("out_ready")
        out_done = sem("out_done")
        flags_ready = sem("flags_ready")
        flags_done = sem("flags_done")
        over_own = sem("over_own")
        over_ready = sem("over_ready")
        g_next = sem("g_next")
        g_raw_in = sem("g_raw_in")
        g_lists = sem("g_lists")
        g_gathered = sem("g_gathered")
        g_rows_in = sem("g_rows_in")
        g_ends_gathered = sem("g_ends_gathered")
        g_exp_in = sem("g_exp_in")
        g_exp_out = sem("g_exp_out")
        g_res = sem("g_res")
        g_res_out = sem("g_res_out")
        g_ends_in = sem("g_ends_in")
        ones_set = sem("ones_set")
        cut = sem("cut")
        ncut = sem("ncut")
        rden_ready = sem("rden_ready")
        onT_one = sem("onT_one")

        block = ctx.enter_context(nc.Block())

        class Own:

            def __init__(self, eng, own):
                self.eng, self.own, self.n = eng, own, 0

            def did(self, ins):
                ins.then_inc(self.own, 1)
                self.n += 1

            def settle(self):
                self.eng.wait_ge(self.own, self.n)

        def take(eng, s, n):
            eng.wait_ge(s, n)
            eng.sem_clear(s)

        def if_lists_overflowed(eng, body):
            eng.wait_ge(over_ready, 1)
            over = eng.value_load(over_i[0:1, 0:1], min_val=0, max_val=1)
            with eng.If(over > 0):
                with eng.Fori(0, E_GAT // GROUP) as i:
                    body(i)

        N_CONSTS = 6
        N_WEIGHTS = 10
        HALF_U = ((0, 2), (64, 0))

        PRE = ["qk", "v01", "v2", "q0", "q1", "k0", "k1", "q2", "q3", "k2", "k3"]
        POST = ["norm0", "norm1", "onT", "out"]

        def order(prelims, extra):
            seq = [("score", k) for k in range(H)] + [("maxT", 0)]
            pre = list(PRE) if prelims else []
            for k in range(H):
                seq.append(("exp", k))
                if k:
                    seq.append(("pv", k - 1))
                for _ in range(2 if k >= H - 3 else 1):
                    if pre:
                        seq.append((pre.pop(0), 0))
                seq.append((extra, k))
            seq.append(("pv", H - 1))
            seq += [(s, 0) for s in pre] + [(s, 0) for s in POST]
            return seq

        MISC = 1 + len(PRE) + len(POST)

        def batches(eng, body):
            with eng.Fori(0, B - 2, 2) as b:
                body(b, 0, True, "hist")
                body(b + 1, 1, True, "hist")
            body(B - 2, 0, True, "owner6")
            body(B - 1, 1, False, "owner7")

        @block.sync
        def _(sp):
            sp.dma_start(tgt_i[:, :], att_tgt).then_inc(tgt_in, 16)
            sp.dma_start(iota[:, :], c_iota).then_inc(tgt_in, 16)
            sp.dma_start(part[:, :], c_part).then_inc(tgt_in, 16)
            sp.dma_start(dst_i, gat_dst).then_inc(edges_in, 16)
            sp.dma_start(src_i, gat_src).then_inc(edges_in, 16)
            sp.wait_ge(zeros_set, 2)
            sp.dma_start(last_edges.rearrange("(p l) a -> p (l a)", p=P), own_tab[0:P, 0:KT * 128]).then_inc(last_zeroed, 16)
            sp.dma_start(exchange.rearrange("(p s) a -> p (s a)", p=P), own_tab[0:P, :]).then_inc(exchange_zeroed, 16)
            for a, b_ in ((wmix[:, :], w_mix), (wc[:, :], w_c)):
                sp.dma_start(a, b_).then_inc(mix_in, 16)
            for a, b_ in ((sel[:, :, :, :, :], c_sel), (ext[:, :, :, :], c_ext), (row[:, :, :], c_row),
                          (eyeb[:, :], c_eyeb), (qk_scale[:, :], c_scale), (hot[:, :, :], c_hot)):
                sp.dma_start(a, b_).then_inc(consts_in, 16)
            for a, b_ in ((wqk[:, :], w_qk), (wv[:, :], w_v), (wo[:, :], w_o), (wgat[:, :], w_gat),
                          (w1s[:, :, :], w1), (w2s[:, :, :], w2), (b2s[:, :, :], b2),
                          (lower[:, :], c_lower),
                          (we[:, :, :], w_e.rearrange("(o k) h -> o k h", o=1).to_broadcast([128, 4, H])),
                          (vecs[:, :, :], att_vec.rearrange("(o k) h -> o k h", o=1).to_broadcast([128, 5, GF]))):
                sp.dma_start(a, b_).then_inc(weights_in, 16)
            sp.wait_ge(tgt_listed, 1)
            sp.dma_start(beyond_few, tgt_list[:, FEW:FEW + 1]).then_inc(more_out, 16)
            sp.wait_ge(more_out, 16)
            sp.dma_start(more_row[0:1, :], beyond_few.rearrange("l a -> a l")).then_inc(more_in, 16)
            sp.wait_ge(last_written, 1)
            sp.dma_start(last[0:P, :, :], last_edges.rearrange("(k p l) a -> p k (l a)", k=KT, p=P)).then_inc(last_in, 16)
            sp.wait_ge(scattered, 16 * CAP)
            sp.dma_start(own_tab[0:P, :], exchange.rearrange("(p s) a -> p (s a)", p=P)).then_inc(table_in, 16)
            sp.wait_ge(tab_ready, 1)
            sp.dma_start(node_rows.rearrange("(t p) f -> p t f", p=P), tab[0:P, :, :]).then_inc(tab_out, 16)
            sp.wait_ge(tab_out, 16)
            sp.dma_start(lastrow[:, :], node_rows[LAST:LAST + 1, :].to_broadcast([128, GF + GH])).then_inc(lastrow_in, 16)
            sp.wait_ge(res_ready, 1)
            sp.dma_start(edge_rows.rearrange("(p c) f -> p c f", p=P), res[0:P, :, :]).then_inc(res_out, 16)

            def group_in(i):
                take(sp, g_next, 1)
                for k, a in enumerate((gat_src, gat_dst)):
                    flat = a.rearrange("(o p) j -> o (p j)", o=1)
                    sp.dma_start(raw_i[:, k, :], flat[:, bass.ds(i * GROUP, GROUP)].to_broadcast([128, GROUP])).then_inc(g_raw_in, 16)
                take(sp, g_res, 1)
                sp.dma_start(edge_rows.rearrange("(p c) f -> p c f", p=P), res[0:P, :, :]).then_inc(g_res_out, 16)

            if_lists_overflowed(sp, group_in)
            sp.wait_ge(out_ready, 1)
            sp.dma_start(out.rearrange("b (k p) d -> p (b k) d", p=P), h[0:P, :, :]).then_inc(out_done, 16)
            sp.wait_ge(out_done, 16)

        @block.gpsimd
        def _(pool):
            pool.memset(xaug[:, :, :], 1.0).then_inc(zeros_set, 1)
            pool.wait_ge(zeros_set, 1)
            pool.memset(own_tab[:, :], 0.0).then_inc(zeros_set, 1)
            def write_last(first, end, done):
                for c in range(first, end):
                    pool.indirect_dma_start(
                        out=last_edges, out_offset=bass.IndirectOffsetOnAxis(ap=tgt_slot_i[:, c:c + 1], axis=0),
                        in_=tgt_val[:, c:c + 1], in_offset=None,
                        bounds_check=L * 128 - 1, oob_is_err=False).then_inc(done, 16)

            pool.wait_ge(tgt_slots_ready, 1)
            pool.wait_ge(last_zeroed, 16)
            write_last(0, FEW, last_scattered)
            pool.wait_ge(more_ready, 1)
            more = pool.value_load(more_i[0:1, 0:1], min_val=0, max_val=1)
            with pool.If(more > 0):
                write_last(FEW, JA, more_scattered)
                pool.wait_ge(more_scattered, 16 * (JA - FEW))
            pool.wait_ge(last_scattered, 16 * FEW)
            pool.sem_inc(last_written, 1)

            def gather_attributes():
                pool.wait_ge(last_ready, 1)
                for k in range(KT):
                    pool.indirect_dma_start(
                        out=attr[0:P, k, :], out_offset=None, in_=att_attr,
                        in_offset=bass.IndirectOffsetOnAxis(ap=last_i[0:P, k:k + 1], axis=0)).then_inc(attr_in, 16)

            pool.wait_ge(slots_ready, 1)
            pool.wait_ge(exchange_zeroed, 16)
            for c in range(CAP):
                if c == ATTR_AT:
                    gather_attributes()
                pool.indirect_dma_start(
                    out=exchange, out_offset=bass.IndirectOffsetOnAxis(ap=slot_i[:, c:c + 1], axis=0),
                    in_=lane_list[:, c:c + 1], in_offset=None,
                    bounds_check=P * SLOTS - 1, oob_is_err=False).then_inc(scattered, 16)
            def gather_rows(n, done):
                for c in range(n):
                    pool.indirect_dma_start(
                        out=got[0:P, c, :], out_offset=None, in_=node_rows,
                        in_offset=bass.IndirectOffsetOnAxis(ap=src_idx[0:P, c:c + 1], axis=0)).then_inc(done, 16)

            def gather_ends(done):
                for t in range(NT):
                    pool.indirect_dma_start(
                        out=ends[0:P, t, :], out_offset=None, in_=edge_rows,
                        in_offset=bass.IndirectOffsetOnAxis(ap=end_idx[0:P, t:t + 1], axis=0)).then_inc(done, 16)

            pool.wait_ge(lists_ready, 1)
            pool.wait_ge(tab_out, 16)
            gather_rows(CAP, gathered)
            pool.wait_ge(res_out, 16)
            gather_ends(ends_in)

            def landed(done, n, tell):
                pool.wait_ge(done, 16 * n)
                pool.dma_reset(range(done.num, done.num + 1))
                pool.sem_clear(done)
                pool.sem_inc(tell, 1)

            def group_rows(i):
                take(pool, g_lists, 1)
                gather_rows(GROUP, g_gathered)
                landed(g_gathered, GROUP, g_rows_in)
                take(pool, g_res_out, 16)
                gather_ends(g_ends_gathered)
                landed(g_ends_gathered, NT, g_ends_in)

            if_lists_overflowed(pool, group_rows)

        @block.tensor
        def _(pe):
            pe.wait_ge(tok_in, 64)
            for b in range(B):
                pe.matmul(ps[:, b, 0:L], win[0:6, :], xaug[0:6, b, :], start=True, stop=True).then_inc(tok_sum, 1)
            pe.wait_ge(state_zeroed, 1)
            with pe.Fori(1, STEPS) as r:
                for b in range(B):
                    pe.wait_ge(tok_state, (r - 1) * (2 * B) + 2 * (b + 1))
                    pe.matmul(ps[:, b, 0:L], eye[:, :], add_in[:, b, :], start=True, stop=False)
                    pe.matmul(ps[:, b, 0:L], wstep[:, :], state[:, b, 1:L + 1], start=False, stop=True).then_inc(tok_sum, 1)
            pe.wait_ge(mix_in, 32)
            pe.wait_ge(tok_state, STEPS * 2 * B)
            for t in range(NT):
                b, k = divmod(t, KT)
                bank, col = divmod(t, 8)
                o = ps[0:P, bank, col * D:(col + 1) * D]
                pe.matmul(o, state[:, b, 1 + k * P:1 + (k + 1) * P], wmix[:, :], start=True, stop=False)
                mm = pe.matmul(o, xaug[0:7, b, k * P:(k + 1) * P], wc[:, :], start=False, stop=True)
            mm.then_inc(mix_done, 1)

            pe.wait_ge(consts_in, 16 * N_CONSTS)
            pe.wait_ge(bparts_ready, 1)
            for k in range(KT):
                mm = pe.matmul(ps[0:3 * H, 7, k * P:(k + 1) * P], bparts[0:P, k, :, :].rearrange("p h c -> p (h c)"),
                               eyeb[0:P, 0:P], start=True, stop=True)
            mm.then_inc(biasT_done, 1)

            def turn_xn(n):
                pe.wait_ge(xn_ready, n)
                for b in range(B):
                    for k in range(KT):
                        mm = pe.matmul(ps[0:D, b, k * P:(k + 1) * P], xn[0:P, b * KT + k, :], eye[0:P, 0:P],
                                       start=True, stop=True)
                    mm.then_inc(xT_done, 1)

            pe.wait_ge(h_ready, 3)
            turn_xn(1)

            pe.wait_ge(biasT_ready, 1)
            pe.wait_ge(weights_in, 16 * N_WEIGHTS)
            misc = ps[:, 7, :]

            def pass_through(kind, par, n, b=None):
                pe.wait_ge(misc_free, n)
                if kind == "qk":
                    pe.wait_ge(xb_ready, b + 1)
                    mm = pe.matmul(misc[:, 0:L], wqk[:, :], xb[:, par, :], start=True, stop=True)
                elif kind in ("v01", "v2"):
                    for k in ((0, 1) if kind == "v01" else (2,)):
                        mm = pe.matmul(misc[0:P, 256 * (k % 2):256 * (k % 2) + 256],
                                       xb[:, par, k * P:(k + 1) * P], wv[:, :], start=True, stop=True)
                elif kind[0] in "qk" and len(kind) == 2:
                    side, pair = "qk".index(kind[0]), int(kind[1])
                    if kind == "q0":
                        pe.wait_ge(parts_ready, b + 1)
                    for part_ in range(3):
                        pe.matmul(misc[:, 0:L], sel[:, side, part_, pair, :], parts[:, part_, :],
                                  start=(part_ == 0), stop=False)
                    mm = pe.matmul(misc[:, 0:L], ext[:, side, pair, :], biasT[:, :], start=False, stop=True)
                elif kind == "maxT":
                    pe.wait_ge(negmax_ready, b + 1)
                    for k in range(KT):
                        mm = pe.matmul(misc[0:3 * H, k * P:(k + 1) * P], nparts[0:P, k, :, :].rearrange("p h c -> p (h c)"),
                                       eyeb[0:P, 0:P], start=True, stop=True)
                elif kind in ("norm0", "norm1"):
                    g = int(kind[4])
                    pe.wait_ge(oT_ready, 2 * b + g + 2)
                    for k in range(KT):
                        mm = pe.matmul(misc[0:P, k * 128:(k + 1) * 128], oT[:, g, k * P:(k + 1) * P], eye[:, :],
                                       start=True, stop=True)
                elif kind == "onT":
                    for k in range(KT):
                        mm = pe.matmul(misc[0:D, k * P:(k + 1) * P], on[0:P, k, :], eye[0:P, 0:P],
                                       start=True, stop=True)
                elif kind == "out":
                    for k in range(KT):
                        mm = pe.matmul(misc[0:P, k * D:(k + 1) * D], onT[:, k * P:(k + 1) * P], wo[:, :],
                                       start=True, stop=True)
                mm.then_inc(misc_full, 1)

            pe.wait_ge(xT_ready, 8)
            pe.wait_ge(onT_one, 1)
            for n, kind in enumerate(PRE):
                pass_through(kind, 0, n, 0)
            pe.wait_ge(misc_free, len(PRE))

            def batch(b, par, prelims, extra):
                n = b * MISC + len(PRE)
                pe.wait_ge(misc_free, n - len(POST))
                for kind, k in order(prelims, extra):
                    base, pair, q0 = 64 * (k % 2), k // 2, 32 * (k % 4)
                    bank = 3 * (k % 2)
                    if kind == "score":
                        if k < 2:
                            pe.wait_ge(exp_done, b * H + k + 1)
                        else:
                            pe.wait_ge(max_done, b * H + k - 1)
                        for t in range(KT):
                            mm = pe.matmul(ps[0:P, bank + t, 0:L], qst[base:base + 64, par, pair, t * P:(t + 1) * P],
                                           kst[base:base + 64, par, pair, :], start=True, stop=True)
                        mm.then_inc(score_full, 1)
                    elif kind == "exp":
                        if k < 2:
                            pe.wait_ge(max_done, b * H + H - 1 + k)
                        else:
                            pe.wait_ge(exp_done, b * H + k + 1)
                        for t in range(KT):
                            pe.matmul(ps[0:P, bank + t, 0:L], kst[base:base + 64, par, pair, t * P:(t + 1) * P],
                                      qst[base:base + 64, par, pair, :], start=True, stop=False)
                            mm = pe.matmul(ps[0:P, bank + t, 0:L], row[:, k, :], maxT[:, :], start=False, stop=True)
                        mm.then_inc(scoreT_full, 1)
                    elif kind == "hist":
                        pe.wait_ge(hot_ready, b * H + k + 1)
                        if k in (0, 4):
                            pe.wait_ge(oT_ready, 2 * b + k // 4 + 1)
                        for j in range(16):
                            mm = pe.matmul(ps[0:NT, 6, 384:384 + P], hot_tile[:, k % 2, :, j], hot_own[:, k % 2, 0:P, j],
                                           start=(j == 0), stop=(j == 15))
                        mm.then_inc(hist_done, 1)
                    elif kind == "owner6":
                        if k == 0:
                            pe.wait_ge(hist_added, HOTS + 1)
                            pe.wait_ge(oT_ready, 2 * b + 1)
                            pe.matmul(ps[0:P, 6, 384:384 + NT], clampT[:, 0:P], eye[0:NT, 0:NT],
                                      start=True, stop=True).then_inc(histT_done, 1)
                    elif kind == "owner7":
                        pass
                    elif kind == "pv":
                        pe.wait_ge(exp_done, b * H + k + 3)
                        if k % 4 == 0:
                            pe.wait_ge(oT_ready, 2 * b + k // 4 + 1)
                        if extra == "hist":
                            pe.wait_ge(hist_added, b * H + k + 2)
                        elif extra == "owner6":
                            pe.wait_ge(clamped_ready, 1)
                        for t in range(KT):
                            mm = pe.matmul(ps[q0:q0 + 32, 6, 0:L], vv[0:P, par, t, 32 * k:32 * k + 32],
                                           probs[0:P, k % 2, t, :], start=(t == 0), stop=(t == KT - 1))
                        mm.then_inc(pv_done, 1)
                    else:
                        nxt = kind in PRE
                        pass_through(kind, 1 - par if nxt else par, n, b + 1 if nxt else b)
                        n = n + 1
                    if kind == "maxT":
                        pe.wait_ge(misc_free, n)

            batches(pe, batch)

            pe.wait_ge(attn_added, B)
            turn_xn(2)
            pe.wait_ge(xT_ready, 16)
            for t in range(NT):
                mm = pe.matmul(ps[0:P, 7, t * GF:(t + 1) * GF], xT[0:D, t * P:(t + 1) * P], wgat[:, :],
                               start=True, stop=True)
            mm.then_inc(gat_done, 1)

            pe.sem_inc(y_full, EX)
            pe.wait_ge(tab_ready, 1)
            with pe.Fori(0, B) as b:
                for e in range(EX):
                    pe.wait_ge(hid_ready, b * EX + e + 1)
                    pe.matmul(ps[:, e, 0:L], w1s[:, e, :], xT[:, bass.ds(b * L, L)], start=True, stop=True).then_inc(hid_full, 1)
                for e in range(EX):
                    pe.wait_ge(hid_ready, b * EX + e + 5)
                    pe.wait_ge(y_copied, b * EX + e + 1)
                    for k in range(KT):
                        o = ps[0:P, 4 + e, k * D:(k + 1) * D]
                        pe.matmul(o, hid[:, e, k * P:(k + 1) * P], w2s[:, e, :], start=True, stop=False)
                        mm = pe.matmul(o, ones1[:, 0:P], b2s[:, e, :], start=False, stop=True)
                    mm.then_inc(y_full, 1)
            pe.wait_ge(flags_ready, 1)
            pe.wait_ge(hid_ready, B * EX + EX)
            pe.matmul(ps[0:1, 0, 0:128], flags[:, 3:4], eye[:, :], start=True, stop=True).then_inc(flags_done, 1)

        @block.scalar
        def _(act):
            own = Own(act, act_own)
            for a, b_ in ((wstep[:, :], w_step), (win[:, :], w_in), (eye[:, :], c_eye)):
                act.dma_start(a, b_).then_inc(tok_in, 16)
            act.wait_ge(zeros_set, 1)
            act.dma_start(xaug[0:DIN, :, :], x.rearrange("b c l -> c b l")).then_inc(tok_in, 16)
            act.wait_ge(state_zeroed, 1)
            for b in range(B):
                act.wait_ge(tok_sum, b + 1)
                own.did(act.activation(add_in[:, b, :], ps[:, b, 0:L], ACT.Copy))
                act.wait_ge(act_own, b + 1)
                for p0, at in HALF_U:
                    act.activation(state[p0:p0 + 64, b, at:at + L], ps[p0:p0 + 64, b, 0:L], ACT.Relu).then_inc(tok_state, 1)
            with act.Fori(1, STEPS) as r:
                for b in range(B):
                    act.wait_ge(tok_sum, r * B + b + 1)
                    for p0, at in HALF_U:
                        act.activation(state[p0:p0 + 64, b, at:at + L], ps[p0:p0 + 64, b, 0:L], ACT.Relu).then_inc(tok_state, 1)
            act.wait_ge(mix_done, 1)
            for k in range(3):
                act.activation(h[0:P, 8 * k:8 * k + 8, :].rearrange("p t d -> p (t d)"), ps[0:P, k, :], ACT.Relu).then_inc(h_ready, 1)

            def norm_part(n):
                act.wait_ge(centred, n)
                act.activation(sq[0:P, :, :], xn[0:P, :, :], ACT.Square).then_inc(squared, 1)
                act.wait_ge(var_ready, n)
                act.activation(stat[0:P, 3, :], stat[0:P, 2, :], ACT.Sqrt).then_inc(std_ready, 1)
                for b in range(B):
                    act.wait_ge(xT_done, (n - 1) * B + b + 1)
                    act.activation(xT[0:D, b * L:(b + 1) * L], ps[0:D, b, 0:L], ACT.Copy).then_inc(xT_ready, 1)

            norm_part(1)

            def batch_in(b, par):
                act.activation(xb[:, par, :], xT[:, bass.ds(b * L, L)], ACT.Copy).then_inc(xb_ready, 1)

            def passed(kind, par, n, b, first=False):
                if kind == "qk":
                    act.wait_ge(misc_full, n + 1)
                    if not first:
                        act.wait_ge(parts_ready, b)
                    act.activation(qk32[:, :], ps[:, 7, 0:L], ACT.Copy, scale=qk_scale[:, 0:1]).then_inc(misc_free, 1)
                elif kind == "v01":
                    act.wait_ge(misc_full, n + 1)
                    act.activation(vv[0:P, par, 0:2, :].rearrange("p k c -> p (k c)"), ps[0:P, 7, :], ACT.Copy).then_inc(misc_free, 1)
                elif kind == "v2":
                    act.wait_ge(misc_full, n + 1)
                    act.activation(vv[0:P, par, 2, :], ps[0:P, 7, 0:256], ACT.Copy).then_inc(misc_free, 1)
                elif kind in ("k0", "k1", "k2", "k3"):
                    act.wait_ge(misc_full, n + 1)
                    act.activation(kst[:, par, int(kind[1]), :], ps[:, 7, 0:L], ACT.Copy).then_inc(misc_free, 1)
                elif kind == "onT":
                    act.wait_ge(misc_full, n + 1)
                    act.activation(onT[0:D, :], ps[0:D, 7, 0:L], ACT.Copy).then_inc(misc_free, 1)

            act.wait_ge(xT_ready, B)
            act.wait_ge(ones_set, 1)
            batch_in(0, 0)
            for n, kind in enumerate(PRE):
                passed(kind, 0, n, 0, first=True)

            def batch(b, par, prelims, extra):
                n = b * MISC + len(PRE)
                for kind, k in order(prelims, extra):
                    if kind == "exp":
                        act.wait_ge(scoreT_full, b * H + k + 1)
                        act.wait_ge(pv_done, b * H + k + 1)
                        act.activation(probs[0:P, k % 2, :, :], ps[0:P, 3 * (k % 2):3 * (k % 2) + 3, 0:L],
                                       ACT.Exp).then_inc(exp_done, 1)
                        if k == 0 and prelims:
                            batch_in(b + 1, 1 - par)
                    elif kind == "pv":
                        if k % 4 == 3:
                            act.wait_ge(pv_done, b * H + k + 3)
                            act.activation(oT[:, k // 4, :], ps[:, 6, 0:L], ACT.Copy).then_inc(oT_ready, 1)
                    elif kind in PRE or kind in POST or kind == "maxT":
                        nxt = kind in PRE
                        passed(kind, 1 - par if nxt else par, n, b + 1 if nxt else b)
                        n = n + 1

            act.sem_inc(exp_done, 2)
            act.sem_inc(pv_done, 2)
            act.sem_inc(oT_ready, 1)
            batches(act, batch)
            norm_part(2)

            act.sem_inc(hid_ready, EX)
            with act.Fori(0, B) as b:
                for e in range(EX):
                    act.wait_ge(hid_full, b * EX + e + 1)
                    act.wait_ge(y_full, b * EX + e + 1)
                    act.activation(hid[:, e, :], ps[:, e, 0:L], ACT.Gelu).then_inc(hid_ready, 1)

            def exponentials(n, out_, in_):
                act.wait_ge(exp_in, n)
                act.activation(out_, in_, ACT.Exp).then_inc(exp_out, 1)

            exponentials(1, expo[0:P, :, :, :], expo[0:P, :, :, :])

            def group_exponentials(i):
                take(act, g_exp_in, 1)
                act.activation(expo[0:P, :, :, :], expo[0:P, :, :, :], ACT.Exp).then_inc(g_exp_out, 1)
                take(act, g_exp_in, 1)
                act.activation(wts[0:P, 0:2, :, :], wts[0:P, 0:2, :, :], ACT.Exp).then_inc(g_exp_out, 1)

            if_lists_overflowed(act, group_exponentials)
            exponentials(2, wts[0:P, :, :, :], wts[0:P, :, :, :])
            act.wait_ge(centred, 3)
            act.activation(gsq[0:P, :, :], gnum[0:P, :, :], ACT.Square).then_inc(squared, 1)
            act.wait_ge(var_ready, 3)
            act.activation(stat[0:P, 3, :], stat[0:P, 2, :], ACT.Sqrt).then_inc(std_ready, 1)
            exponentials(3, gate[0:P, :, :], gate[0:P, :, :])

        @block.vector
        def _(v):
            own = Own(v, vec)
            did, settle = own.did, own.settle

            def bc(ap, axis, shape):
                return ap.unsqueeze(axis).to_broadcast(shape)

            v.memset(state[:, :, :], 0.0).then_inc(state_zeroed, 1)
            did(v.memset(flags[:, :], 0.0))
            did(v.memset(biasT[:, :], 1.0))
            did(v.memset(ones1[:, :], 1.0))
            did(v.memset(clampT[:, :], 0.0))
            did(v.memset(own_h[:, KEPT:KEPT + 144], 0.0))
            did(v.memset(tile_h[:, KEPT:KEPT + 144], 0.0))

            v.wait_ge(tgt_in, 48)
            did(v.scalar_tensor_tensor(out=tgt_key, in0=tgt_i[:, :], scalar=float(JA), in1=iota[:, 1:JA + 1],
                                       op0=ALU.mult, op1=ALU.add))
            settle()
            did(v.scalar_tensor_tensor(out=tgt_key, in0=tgt_i[:, :], scalar=float(L), in1=tgt_key,
                                       op0=ALU.is_lt, op1=ALU.mult))
            settle()
            for c in range(0, JA, 8):
                did(v.max(tgt_list[:, c:c + 8], tgt_key))
                settle()
                did(v.match_replace(tgt_key, tgt_list[:, c:c + 8], tgt_key, -1.0))
                settle()
            v.sem_inc(tgt_listed, 1)
            did(v.tensor_scalar(tgt_no, tgt_list, -1.0, 0.0, ALU.add, ALU.max))
            did(v.tensor_scalar(tgt[:, :], part[:, :].to_broadcast([128, JA]), float(JA) / RANKS, 1.0, ALU.mult, ALU.add))
            settle()
            did(v.tensor_scalar(tgt_j, tgt_no, JA - 1, None, ALU.bitwise_and))
            settle()
            did(v.tensor_tensor(tgt_val, tgt[:, :], tgt_j, ALU.add))
            did(v.tensor_tensor(tgt_slot, tgt_no, tgt_j, ALU.subtract))
            settle()
            did(v.tensor_tensor(tgt_new[:, 1:JA], tgt_slot[:, 1:JA], tgt_slot[:, 0:JA - 1], ALU.not_equal))
            did(v.memset(tgt_new[:, 0:1], 1.0))
            settle()
            did(v.scalar_tensor_tensor(out=tgt_new, in0=tgt_list, scalar=0.0, in1=tgt_new, op0=ALU.is_gt, op1=ALU.mult))
            did(v.tensor_scalar(own_row[:, :], part[:, :], 1.0 / RANKS, -NO_SLOT, ALU.mult, ALU.add))
            settle()
            did(v.scalar_tensor_tensor(out=tgt_slot, in0=tgt_slot, scalar=own_row[:, 0:1], in1=tgt_new,
                                       op0=ALU.add, op1=ALU.mult))
            settle()
            v.tensor_scalar(tgt_slot_i, tgt_slot, NO_SLOT, None, ALU.add).then_inc(tgt_slots_ready, 1)
            v.wait_ge(edges_in, 32)

            def edge_keys(src, dst, key, own_tile, tile, source, tmp):
                did(v.tensor_scalar(tmp, dst, 1.0 / P, 0.504 - 1.0, ALU.mult, ALU.add))
                did(v.tensor_scalar(source, src, float(LAST), 1.0, ALU.min, ALU.add))
                settle()
                did(v.tensor_scalar(tile, tmp, MAGIC, -MAGIC, ALU.add, ALU.add))
                settle()
                did(v.tensor_scalar(tmp, tile, float(2 ** TILE_BITS * P - 1), None, ALU.mult))
                settle()
                did(v.scalar_tensor_tensor(out=own_tile, in0=dst, scalar=float(2 ** TILE_BITS), in1=tmp,
                                           op0=ALU.mult, op1=ALU.subtract))
                settle()
                did(v.scalar_tensor_tensor(out=key, in0=own_tile, scalar=float(2 ** SRC_BITS), in1=source,
                                           op0=ALU.mult, op1=ALU.add))
                settle()
                did(v.scalar_tensor_tensor(out=key, in0=dst, scalar=float(M), in1=key, op0=ALU.is_lt, op1=ALU.mult))

            edge_keys(src_i, dst_i, f_key, f_own, f_tile, f_real, f_tmp)
            v.wait_ge(more_in, 16)
            v.tensor_reduce(more_top[0:1, 0:1], more_row[0:1, :], AX, ALU.max).then_inc(more_own, 1)
            v.wait_ge(more_own, 1)
            v.tensor_scalar(more_i[:, :], more_top[:, :], 0.0, None, ALU.is_gt).then_inc(more_ready, 1)
            settle()

            for r in range(KEEP // 8):
                best = [kept[:, 8 * (NPART * r + g):8 * (NPART * r + g + 1)] for g in range(NPART)]
                groups = [f_key[:, g * PART:(g + 1) * PART] for g in range(NPART)]
                for g in range(NPART):
                    did(v.max(best[g], groups[g]))
                settle()
                for g in range(NPART):
                    did(v.match_replace(groups[g], best[g], groups[g], -1.0))
                settle()
            did(v.tensor_reduce(flags[:, 4:5], f_key, AX, ALU.max))
            did(v.tensor_scalar(kept_i, kept, 0.0, None, ALU.max))
            settle()
            did(v.tensor_scalar(low_i, kept_i, 2 ** SRC_BITS - 1, None, ALU.bitwise_and))
            settle()
            did(v.scalar_tensor_tensor(out=kept_real, in0=low_i, scalar=float(LAST + 1), in1=kept,
                                       op0=ALU.is_lt, op1=ALU.mult))
            did(v.tensor_scalar(no_count, low_i, float(LAST + 1), 200.0, ALU.is_lt, ALU.mult))
            settle()

            for c in range(0, CAP, 8):
                did(v.max(lane_list[:, c:c + 8], kept_real))
                settle()
                did(v.match_replace(kept_real, lane_list[:, c:c + 8], kept_real, -1.0))
                settle()
            did(v.tensor_reduce(flags[:, 0:1], kept_real, AX, ALU.max))
            did(v.tensor_scalar(lane_list[:, :], lane_list[:, :], 0.0, None, ALU.max))
            settle()
            did(v.tensor_copy(lane_int[:, :], lane_list[:, :]))
            settle()
            did(v.tensor_scalar(own_tmp_i[:, 0, :], lane_int[:, :], SRC_BITS + TILE_BITS, None, ALU.logical_shift_right))
            settle()
            lane_own, same, rank, slot = (lane_tmp[:, k, :] for k in range(4))
            did(v.tensor_copy(lane_own, own_tmp_i[:, 0, :]))
            did(v.memset(same[:, 0:1], 0.0))
            settle()
            did(v.tensor_tensor(same[:, 1:CAP], lane_own[:, 1:CAP], lane_own[:, 0:CAP - 1], ALU.is_equal))
            settle()
            did(v.tensor_tensor_scan(rank, same, same, 0.0, ALU.mult, ALU.add))
            settle()
            did(v.scalar_tensor_tensor(out=slot, in0=lane_own, scalar=float(SLOTS), in1=rank, op0=ALU.mult, op1=ALU.add))
            did(v.tensor_scalar(same, rank, float(RANKS), None, ALU.is_lt))
            settle()
            v.wait_ge(consts_in, 16 * N_CONSTS)
            did(v.tensor_scalar(slot, slot, part[:, 0:1], -SKIP, ALU.add, ALU.add))
            did(v.scalar_tensor_tensor(out=same, in0=lane_list[:, :], scalar=0.0, in1=same, op0=ALU.is_gt, op1=ALU.mult))
            did(v.tensor_scalar(lane_own, rank, float(RANKS), None, ALU.is_ge))
            settle()
            did(v.tensor_tensor(slot, slot, same, ALU.mult))
            did(v.scalar_tensor_tensor(out=lane_own, in0=lane_list[:, :], scalar=0.0, in1=lane_own, op0=ALU.is_gt, op1=ALU.mult))
            settle()
            did(v.tensor_reduce(flags[:, 1:2], lane_own, AX, ALU.max))
            v.tensor_scalar(slot_i[:, :], slot, SKIP, None, ALU.add).then_inc(slots_ready, 1)

            did(v.tensor_scalar(code_i, kept_i, SRC_BITS, 2 ** TILE_BITS - 1, ALU.logical_shift_right, ALU.bitwise_and))
            settle()
            did(v.tensor_tensor(tile_h[:, 0:KEPT], no_count, code_i, ALU.add))
            settle()
            did(v.tensor_scalar(code_i, kept_i, SRC_BITS + TILE_BITS, None, ALU.logical_shift_right))
            settle()
            did(v.tensor_copy(own_h[:, 0:KEPT], code_i))
            settle()

            def hot_block(i, par):
                v.tensor_tensor(hot_own[:, par, 0:P, :], bc(own_h[:, bass.ds(i * 16, 16)], 1, [128, P, 16]),
                                hot[:, 0:P, :], ALU.is_equal)
                v.tensor_tensor(hot_tile[:, par, :, :], bc(tile_h[:, bass.ds(i * 16, 16)], 1, [128, NT, 16]),
                                hot[:, 0:NT, :], ALU.is_equal).then_inc(hot_ready, 1)

            hot_block(0, 0)
            v.sem_inc(hist_added, 1)

            v.wait_ge(last_in, 16)
            did(v.tensor_reduce(lastf[0:P, 0, :], last[0:P, :, :], AX, ALU.max))
            settle()
            did(v.tensor_scalar(lastf[0:P, 1, :], lastf[0:P, 0, :], 0.0, None, ALU.is_gt))
            v.tensor_scalar(last_i[0:P, :], lastf[0:P, 0, :], -1.0, 0.0, ALU.add, ALU.max).then_inc(last_ready, 1)
            v.wait_ge(attr_in, 16 * KT)
            v.wait_ge(weights_in, 16 * N_WEIGHTS)
            for k in range(KT):
                for i in range(3):
                    did(v.scalar_tensor_tensor(out=bias[0:P, k, :], in0=we[0:P, i, :], scalar=attr[0:P, k, i:i + 1],
                                               in1=we[0:P, 3, :] if i == 0 else bias[0:P, k, :],
                                               op0=ALU.mult, op1=ALU.add))
                    settle()
                did(v.tensor_scalar(bias[0:P, k, :], bias[0:P, k, :], lastf[0:P, 1, k:k + 1], None, ALU.mult))
            settle()

            def three_parts(out_parts, value, left, last_sem):
                did(v.tensor_copy(out_parts(0), value))
                settle()
                did(v.tensor_tensor(left, value, out_parts(0), ALU.subtract))
                settle()
                did(v.tensor_copy(out_parts(1), left))
                settle()
                v.tensor_tensor(out_parts(2), left, out_parts(1), ALU.subtract).then_inc(last_sem, 1)

            three_parts(lambda c: bparts[0:P, :, :, c], bias[0:P, :, :], nrest[0:P, :, :], bparts_ready)
            v.wait_ge(biasT_done, 1)
            v.tensor_copy(biasT[0:3 * H, :], ps[0:3 * H, 7, 0:L]).then_inc(biasT_ready, 1)
            v.wait_ge(mix_done, 1)
            v.memset(xT[D:D + 1, :], 1.0).then_inc(ones_set, 1)

            def owner_round(c):
                did(v.max(own_list[0:P, c:c + 8], own_tab[0:P, :]))
                settle()
                did(v.match_replace(own_tab[0:P, :], own_list[0:P, c:c + 8], own_tab[0:P, :], -1.0))
                settle()

            def decode(ready):
                did(v.tensor_scalar(own_list[0:P, :], own_list[0:P, :], 0.0, None, ALU.max))
                settle()
                did(v.tensor_copy(own_int[0:P, :], own_list[0:P, :]))
                did(v.tensor_scalar(keep[0:P, :], own_list[0:P, :], 0.0, None, ALU.is_le))
                settle()
                did(v.tensor_scalar(own_tmp_i[0:P, 0, :], own_int[0:P, :], SRC_BITS, 2 ** TILE_BITS - 1,
                                    ALU.logical_shift_right, ALU.bitwise_and))
                did(v.tensor_scalar(own_tmp_i[0:P, 1, :], own_int[0:P, :], 2 ** SRC_BITS - 1, None, ALU.bitwise_and))
                settle()
                did(v.scalar_tensor_tensor(out=seg[0:P, :], in0=keep[0:P, :], scalar=-64.0, in1=own_tmp_i[0:P, 0, :],
                                           op0=ALU.mult, op1=ALU.add))
                did(v.tensor_scalar(src_idx[0:P, :], own_tmp_i[0:P, 1, :], -1.0, 0.0, ALU.add, ALU.max))
                settle()
                did(v.memset(keep[0:P, 0:1], 0.0))
                did(v.tensor_tensor(keep[0:P, 1:CAP], seg[0:P, 1:CAP], seg[0:P, 0:CAP - 1], ALU.is_equal))
                did(v.tensor_tensor(member[0:P, :, :], bc(seg[0:P, :], 2, [P, CAP, NT]),
                                    bc(iota[0:P, 0:NT], 1, [P, CAP, NT]), ALU.is_equal))
                did(v.tensor_tensor(at_least[0:P, :, :], bc(seg[0:P, :], 1, [P, NT, CAP]),
                                    bc(iota[0:P, 0:NT], 2, [P, NT, CAP]), ALU.is_ge))
                settle()
                did(v.tensor_scalar(keep[0:P, :], keep[0:P, :], -1.0, -NEG, ALU.add, ALU.mult))
                did(v.tensor_reduce(endf[0:P, 0, :], at_least[0:P, :, :], AX, ALU.add))
                did(v.tensor_scalar(own_row[0:P, :], part[0:P, :], float(CAP) / RANKS, None, ALU.mult))
                settle()
                did(v.tensor_tensor(has_real[0:P, 0:NT - 1], endf[0:P, 0, 0:NT - 1], endf[0:P, 0, 1:NT], ALU.is_gt))
                did(v.tensor_scalar(has_real[0:P, NT - 1:NT], endf[0:P, 0, NT - 1:NT], 0.0, None, ALU.is_gt))
                did(v.tensor_scalar(endf[0:P, 1, :], endf[0:P, 0, :], -1.0, 0.0, ALU.add, ALU.max))
                settle()
                v.tensor_scalar(end_idx[0:P, :], endf[0:P, 1, :], own_row[0:P, 0:1], None, ALU.add).then_inc(ready, 1)

            def owner_step(n):
                if n == 0:
                    v.wait_ge(table_in, 16)
                if n < CAP // 8:
                    owner_round(8 * n)
                elif n == CAP // 8:
                    did(v.tensor_reduce(flags[0:P, 2:3], own_tab[0:P, :], AX, ALU.max))
                    settle()
                    did(v.tensor_reduce(flags[:, 3:4], flags[:, 0:3], AX, ALU.max))
                    settle()
                    did(v.tensor_tensor(flags[:, 3:4], flags[:, 3:4], flags[:, 4:5], ALU.max))
                    settle()
                    v.sem_inc(flags_ready, 1)
                    decode(lists_ready)

            def normalise(n, x_, c_, width, mean_row):
                r3 = [P, NT, width]
                did(v.tensor_reduce(stat[0:P, 0, :], x_, AX, ALU.add))
                settle()
                did(v.tensor_scalar(stat[0:P, 1, :], stat[0:P, 0, :], 1.0 / width, None, ALU.mult))
                settle()
                v.tensor_tensor(c_, x_, bc(stat[0:P, 1, :], 2, r3), ALU.subtract).then_inc(centred, 1)
                v.wait_ge(squared, n)
                did(v.tensor_reduce(stat[0:P, 0, :], mean_row, AX, ALU.add))
                settle()
                v.tensor_scalar(stat[0:P, 2, :], stat[0:P, 0, :], 1.0 / width, EPS, ALU.mult, ALU.add).then_inc(var_ready, 1)
                v.wait_ge(std_ready, n)
                did(v.reciprocal(stat[0:P, 1, :], stat[0:P, 3, :]))
                settle()
                ins = v.tensor_tensor(c_, c_, bc(stat[0:P, 1, :], 2, r3), ALU.mult)
                return ins

            v.wait_ge(h_ready, 3)
            normalise(1, h[0:P, :, :], xn[0:P, :, :], D, sq[0:P, :, :]).then_inc(xn_ready, 1)

            v.memset(onT[D:D + 1, :], 1.0).then_inc(onT_one, 1)

            def make_parts(b, n):
                v.wait_ge(misc_free, n + 1)
                v.tensor_copy(parts[:, 0, :], qk32[:, :]).then_inc(cut, 1)
                v.wait_ge(cut, 3 * b + 1)
                v.tensor_tensor(rest[:, :], qk32[:, :], parts[:, 0, :], ALU.subtract).then_inc(cut, 1)
                v.wait_ge(cut, 3 * b + 2)
                v.tensor_copy(parts[:, 1, :], rest[:, :]).then_inc(cut, 1)
                v.wait_ge(cut, 3 * b + 3)
                v.tensor_tensor(parts[:, 2, :], rest[:, :], parts[:, 1, :], ALU.subtract).then_inc(parts_ready, 1)

            def passed(kind, par, n, b):
                if kind == "qk":
                    make_parts(b, n)
                elif kind in ("q0", "q1", "q2", "q3"):
                    v.wait_ge(misc_full, n + 1)
                    v.tensor_copy(qst[:, par, int(kind[1]), :], ps[:, 7, 0:L]).then_inc(misc_free, 1)
                elif kind == "maxT":
                    v.wait_ge(misc_full, n + 1)
                    v.tensor_copy(maxT[:, :], ps[0:3 * H, 7, 0:L]).then_inc(misc_free, 1)
                elif kind in ("norm0", "norm1"):
                    g = int(kind[4])
                    v.wait_ge(misc_full, n + 1)
                    turned = ps[0:P, 7, 0:KT * 128].rearrange("p (k q c) -> p k q c", k=KT, q=4)
                    v.reciprocal(rden[0:P, :, :], turned[:, :, :, HD]).then_inc(rden_ready, 1)
                    v.wait_ge(rden_ready, 2 * b + g + 1)
                    v.tensor_tensor(on[0:P, :, g * 32:(g + 1) * 32].rearrange("p k (q d) -> p k q d", q=4),
                                    turned[:, :, :, 0:HD], bc(rden[0:P, :, :], 3, [P, KT, 4, HD]),
                                    ALU.mult).then_inc(misc_free, 1)
                elif kind == "out":
                    v.wait_ge(misc_full, n + 1)
                    rows = h[0:P, bass.ds(b * KT, KT), :]
                    v.tensor_tensor(rows, ps[0:P, 7, 0:KT * D].rearrange("p (k d) -> p k d", k=KT), rows,
                                    ALU.add).then_inc(misc_free, 1)

            for n, kind in enumerate(PRE):
                passed(kind, 0, n, 0)

            def batch(b, par, prelims, extra):
                n = b * MISC + len(PRE)
                for kind, k in order(prelims, extra):
                    if kind == "score":
                        v.wait_ge(score_full, b * H + k + 1)
                        v.tensor_reduce(negmax[0:P, :, k], ps[0:P, 3 * (k % 2):3 * (k % 2) + 3, 0:L], AX, ALU.max,
                                        negate=True).then_inc(max_done, 1)
                    elif kind == "hist":
                        hot_block(b * H + k + 1, (k + 1) % 2)
                        v.wait_ge(hist_done, b * H + k + 1)
                        v.wait_ge(hist_added, b * H + k + 1)
                        v.tensor_tensor(clampT[:, 0:P], ps[0:NT, 6, 384:384 + P], clampT[:, 0:P], ALU.add).then_inc(hist_added, 1)
                    elif kind == "owner6":
                        if k == 0:
                            v.wait_ge(histT_done, 1)
                            v.tensor_copy(clamped[0:P, :], ps[0:P, 6, 384:384 + NT]).then_inc(clamped_ready, 1)
                        owner_step(k)
                    elif kind == "owner7":
                        owner_step(H + k)
                    elif kind not in ("exp", "pv"):
                        if kind == "maxT":
                            v.wait_ge(max_done, b * H + H)
                            part_ = [nparts[0:P, :, :, c] for c in range(3)]
                            v.tensor_copy(part_[0], negmax[0:P, :, :]).then_inc(ncut, 1)
                            v.wait_ge(ncut, 3 * b + 1)
                            v.tensor_tensor(nrest[0:P, :, :], negmax[0:P, :, :], part_[0], ALU.subtract).then_inc(ncut, 1)
                            v.wait_ge(ncut, 3 * b + 2)
                            v.tensor_copy(part_[1], nrest[0:P, :, :]).then_inc(ncut, 1)
                            v.wait_ge(ncut, 3 * b + 3)
                            v.tensor_tensor(part_[2], nrest[0:P, :, :], part_[1], ALU.subtract).then_inc(negmax_ready, 1)
                        nxt = kind in PRE
                        passed(kind, 1 - par if nxt else par, n, b + 1 if nxt else b)
                        n = n + 1

            batches(v, batch)
            v.wait_ge(misc_free, B * MISC)
            v.sem_inc(attn_added, B)
            normalise(2, h[0:P, :, :], xn[0:P, :, :], D, sq[0:P, :, :]).then_inc(xn_ready, 1)

            v.wait_ge(gat_done, 1)
            hg = ps[0:P, 7, 0:NT * GF].rearrange("p (t f) -> p t f", t=NT)
            r16 = [P, NT, GF]

            def by_head(ap):
                return ap.rearrange("p t (h e) -> p t h e", h=GH)

            did(v.tensor_copy(tab[0:P, :, 0:GF], hg))
            did(v.tensor_tensor(gprod[0:P, :, :], hg, bc(vecs[0:P, 0, :], 1, r16), ALU.mult))
            settle()
            did(v.tensor_reduce(tab[0:P, :, GF:GF + GH], by_head(gprod[0:P, :, :]), AX, ALU.add))
            settle()
            did(v.tensor_tensor(gprod[0:P, :, :], hg, bc(vecs[0:P, 1, :], 1, r16), ALU.mult))
            v.sem_inc(tab_ready, 1)
            settle()
            did(v.tensor_reduce(adst[0:P, :, :], by_head(gprod[0:P, :, :]), AX, ALU.add))
            settle()
            wide3 = wide[0:P, :].rearrange("p (c t) -> p c t", t=NT)

            def target_scores():
                for g in range(GH):
                    did(v.tensor_tensor(wide3, member[0:P, :, :], bc(adst[0:P, :, g], 1, [P, CAP, NT]), ALU.mult))
                    settle()
                    did(v.tensor_reduce(adst_e[0:P, :, g], wide3, AX, ALU.add))
                    settle()

            target_scores()

            v.sem_inc(y_copied, EX)
            with v.Fori(0, B) as b:
                for e in range(EX):
                    v.wait_ge(y_full, b * EX + e + EX + 1)
                    v.tensor_copy(yexp[0:P, bass.ds(b * KT, KT), e, :],
                                  ps[0:P, 4 + e, 0:KT * D].rearrange("p (k d) -> p k d", k=KT)).then_inc(y_copied, 1)

            def edge_sums(ask_exp):
                did(v.tensor_tensor(score[0:P, :, :], got[0:P, :, GF:GF + GH], adst_e[0:P, :, :], ALU.add))
                did(v.memset(expo[0:P, 0, 0:1, :], NEG))
                settle()
                did(v.scalar_tensor_tensor(out=score[0:P, :, :], in0=score[0:P, :, :], scalar=0.2, in1=score[0:P, :, :],
                                           op0=ALU.mult, op1=ALU.max))
                settle()
                for g in range(GH):
                    did(v.tensor_tensor_scan(run_max[0:P, :, g], keep[0:P, :], score[0:P, :, g], NEG, ALU.add, ALU.max))
                settle()
                did(v.tensor_tensor(expo[0:P, 0, 1:CAP, :], run_max[0:P, 0:CAP - 1, :], run_max[0:P, 1:CAP, :], ALU.subtract))
                did(v.tensor_tensor(expo[0:P, 1, :, :], score[0:P, :, :], run_max[0:P, :, :], ALU.subtract))
                did(v.tensor_copy(res[0:P, :, 0:GH], run_max[0:P, :, :]))
                settle()
                did(v.tensor_tensor(expo[0:P, 0, 1:CAP, :], expo[0:P, 0, 1:CAP, :], bc(keep[0:P, 1:CAP], 2, [P, CAP - 1, GH]),
                                    ALU.add))
                settle()
                ask_exp()
                decay, weight = expo[0:P, 0, :, :], expo[0:P, 1, :, :]
                did(v.tensor_tensor(by_head(msg[0:P, :, :]), by_head(got[0:P, :, 0:GF]), bc(weight, 3, [P, CAP, GH, EX]), ALU.mult))
                for g in range(GH):
                    did(v.tensor_tensor_scan(res[0:P, :, GH + g], decay[:, :, g], weight[:, :, g], 0.0, ALU.mult, ALU.add))
                settle()
                for f in range(GF):
                    did(v.tensor_tensor_scan(res[0:P, :, 2 * GH + f], decay[:, :, f // EX], msg[0:P, :, f], 0.0, ALU.mult, ALU.add))
                settle()

            def ask_exp():
                v.sem_inc(exp_in, 1)
                v.wait_ge(exp_out, 1)

            v.wait_ge(gathered, 16 * CAP)
            edge_sums(ask_exp)
            v.sem_inc(res_ready, 1)

            v.wait_ge(lastrow_in, 16)
            r4 = [P, NT, GH]
            e_self, e_clamp, e_real, mask = (s[0:P, :, :] for s in (s1, s2, s3, s4))
            did(v.tensor_tensor(e_self, tab[0:P, :, GF:GF + GH], adst[0:P, :, :], ALU.add))
            settle()
            did(v.scalar_tensor_tensor(out=e_self, in0=e_self, scalar=0.2, in1=e_self, op0=ALU.mult, op1=ALU.max))

            def clamped_scores():
                did(v.tensor_tensor(e_clamp, adst[0:P, :, :], bc(lastrow[0:P, GF:GF + GH], 1, r4), ALU.add))
                did(v.tensor_scalar(endf[0:P, 0, :], clamped[0:P, :], 0.0, None, ALU.is_gt))
                settle()
                did(v.scalar_tensor_tensor(out=e_clamp, in0=e_clamp, scalar=0.2, in1=e_clamp, op0=ALU.mult, op1=ALU.max))
                did(v.tensor_scalar(endf[0:P, 0, :], endf[0:P, 0, :], -1.0, -NEG, ALU.add, ALU.mult))
                settle()
                did(v.tensor_tensor(e_clamp, e_clamp, bc(endf[0:P, 0, :], 2, r4), ALU.add))
                settle()
                did(v.tensor_tensor(mask, e_self, e_clamp, ALU.max))

            clamped_scores()
            v.wait_ge(flags_done, 1)
            v.tensor_reduce(flag_row[0:1, 0:1], ps[0:1, 0, 0:128], AX, ALU.max).then_inc(over_own, 1)
            v.wait_ge(over_own, 1)
            v.tensor_scalar(over_i[:, :], flag_row[0:1, 0:1], 0.0, None, ALU.is_gt).then_inc(over_ready, 1)
            v.wait_ge(ends_in, 16 * NT)
            settle()

            def ask_group_exp():
                settle()
                v.sem_inc(g_exp_in, 1)
                take(v, g_exp_out, 1)

            r4 = [P, NT, GH]

            def group_sums(i):
                v.sem_clear(vec)
                own.n = 0
                v.sem_inc(g_next, 1)
                take(v, g_raw_in, 32)
                raw = [lane_tmp[0:P, k, 0:GROUP] for k in range(4)]
                key, tmp = own_tab[0:P, 0:GROUP], own_tab[0:P, GROUP:2 * GROUP]
                edge_keys(raw_i[0:P, 0, :], raw_i[0:P, 1, :], key, raw[0], raw[1], raw[2], tmp)
                settle()
                did(v.scalar_tensor_tensor(out=tmp, in0=raw_i[0:P, 0, :], scalar=float(LAST), in1=key,
                                           op0=ALU.is_ge, op1=ALU.mult))
                settle()
                did(v.tensor_tensor(key, key, tmp, ALU.subtract))
                did(v.scalar_tensor_tensor(out=raw[0], in0=raw[1], scalar=-float(P), in1=raw_i[0:P, 1, :],
                                           op0=ALU.mult, op1=ALU.add))
                did(v.tensor_scalar(own_row[0:P, :], part[0:P, :], 1.0 / RANKS, None, ALU.mult))
                settle()
                did(v.scalar_tensor_tensor(out=key, in0=raw[0], scalar=own_row[0:P, 0:1], in1=key,
                                           op0=ALU.is_equal, op1=ALU.mult))
                did(v.scalar_tensor_tensor(out=tmp, in0=raw[0], scalar=own_row[0:P, 0:1], in1=tmp,
                                           op0=ALU.is_equal, op1=ALU.mult))
                did(v.memset(own_list[0:P, :], 0.0))
                settle()
                did(v.tensor_scalar(tmp, tmp, 0.0, None, ALU.is_gt))
                did(v.tensor_scalar(raw[1], raw[1], 1.0, None, ALU.add))
                settle()
                did(v.tensor_tensor(tmp, tmp, raw[1], ALU.mult))
                settle()
                hits = wide[0:P, 0:NT * GROUP].rearrange("p (t c) -> p t c", t=NT)
                did(v.tensor_tensor(hits, bc(tmp, 1, [P, NT, GROUP]), bc(iota[0:P, 1:NT + 1], 2, [P, NT, GROUP]), ALU.is_equal))
                settle()
                did(v.tensor_reduce(stat[0:P, 0, :], hits, AX, ALU.add))
                settle()
                did(v.tensor_tensor(clamped[0:P, :], clamped[0:P, :], stat[0:P, 0, :], ALU.add))
                settle()
                for c in range(0, GROUP, 8):
                    did(v.max(own_list[0:P, c:c + 8], key))
                    settle()
                    did(v.match_replace(key, own_list[0:P, c:c + 8], key, -1.0))
                    settle()
                decode(vec)
                own.n += 1
                settle()
                v.sem_inc(g_lists, 1)
                target_scores()
                take(v, g_rows_in, 1)
                edge_sums(ask_group_exp)
                v.sem_inc(g_res, 1)
                take(v, g_ends_in, 1)
                g_real, g_max = gsq[0:P, :, 0:GH], gsq[0:P, :, GH:2 * GH]
                did(v.tensor_scalar(endf[0:P, 1, :], has_real[0:P, :], -1.0, -NEG, ALU.add, ALU.mult))
                settle()
                did(v.tensor_tensor(g_real, ends[0:P, :, 0:GH], bc(endf[0:P, 1, :], 2, r4), ALU.add))
                settle()
                did(v.tensor_tensor(g_max, g_real, acc[0:P, :, 0:GH], ALU.max))
                settle()
                did(v.tensor_tensor(wts[0:P, 0, :, :], acc[0:P, :, 0:GH], g_max, ALU.subtract))
                did(v.tensor_tensor(wts[0:P, 1, :, :], g_real, g_max, ALU.subtract))
                settle()
                did(v.tensor_copy(acc[0:P, :, 0:GH], g_max))
                ask_group_exp()
                did(v.tensor_tensor(wts[0:P, 1, :, :], wts[0:P, 1, :, :], bc(has_real[0:P, :], 2, r4), ALU.mult))
                settle()
                for part_, k in ((acc, 0), (ends, 1)):
                    did(v.tensor_tensor(part_[0:P, :, GH:2 * GH], part_[0:P, :, GH:2 * GH], wts[0:P, k, :, :], ALU.mult))
                    did(v.tensor_tensor(by_head(part_[0:P, :, 2 * GH:RES]), by_head(part_[0:P, :, 2 * GH:RES]),
                                        bc(wts[0:P, k, :, :], 3, [P, NT, GH, EX]), ALU.mult))
                settle()
                did(v.tensor_tensor(acc[0:P, :, GH:RES], acc[0:P, :, GH:RES], ends[0:P, :, GH:RES], ALU.add))
                settle()

            counted = own.n
            v.wait_ge(over_ready, 1)
            over = v.value_load(over_i[0:1, 0:1], min_val=0, max_val=1)
            with v.If(over > 0):
                did(v.memset(acc[0:P, :, :], 0.0))
                did(v.memset(clamped[0:P, :], 0.0))
                settle()
                did(v.memset(acc[0:P, :, 0:GH], NEG))
                settle()
                with v.Fori(0, E_GAT // GROUP) as i:
                    group_sums(i)
                v.sem_clear(vec)
                own.n = 0
                did(v.tensor_copy(ends[0:P, :, :], acc[0:P, :, :]))
                did(v.memset(has_real[0:P, :], 1.0))
                settle()
                clamped_scores()
                settle()
                v.sem_inc(vec, counted - own.n)
            own.n = counted
            did(v.tensor_scalar(endf[0:P, 1, :], has_real[0:P, :], -1.0, -NEG, ALU.add, ALU.mult))
            settle()
            did(v.tensor_tensor(e_real, ends[0:P, :, 0:GH], bc(endf[0:P, 1, :], 2, r4), ALU.add))
            settle()
            did(v.tensor_tensor(mask, mask, e_real, ALU.max))
            settle()
            for k, e_ in enumerate((e_real, e_self, e_clamp)):
                did(v.tensor_tensor(wts[0:P, k, :, :], e_, mask, ALU.subtract))
            settle()
            v.sem_inc(exp_in, 1)
            v.wait_ge(exp_out, 2)
            did(v.tensor_tensor(wts[0:P, 2, :, :], wts[0:P, 2, :, :], bc(clamped[0:P, :], 2, r4), ALU.mult))
            did(v.tensor_tensor(e_real, ends[0:P, :, GH:2 * GH], wts[0:P, 0, :, :], ALU.mult))
            r44 = [P, NT, GH, EX]
            did(v.tensor_tensor(by_head(gnum[0:P, :, :]), by_head(ends[0:P, :, 2 * GH:RES]), bc(wts[0:P, 0, :, :], 3, r44), ALU.mult))
            did(v.tensor_tensor(by_head(gprod[0:P, :, :]), by_head(tab[0:P, :, 0:GF]), bc(wts[0:P, 1, :, :], 3, r44), ALU.mult))
            settle()
            did(v.tensor_tensor(e_real, e_real, wts[0:P, 1, :, :], ALU.add))
            did(v.tensor_tensor(gnum[0:P, :, :], gnum[0:P, :, :], gprod[0:P, :, :], ALU.add))
            settle()
            did(v.tensor_tensor(e_real, e_real, wts[0:P, 2, :, :], ALU.add))
            did(v.tensor_tensor(by_head(gprod[0:P, :, :]), by_head(bc(lastrow[0:P, 0:GF], 1, r16)),
                                bc(wts[0:P, 2, :, :], 3, r44), ALU.mult))
            settle()
            did(v.tensor_tensor(gnum[0:P, :, :], gnum[0:P, :, :], gprod[0:P, :, :], ALU.add))
            did(v.tensor_scalar(e_real, e_real, 1e-16, None, ALU.add))
            settle()
            did(v.reciprocal(e_real, e_real))
            settle()
            did(v.tensor_tensor(by_head(gnum[0:P, :, :]), by_head(gnum[0:P, :, :]), bc(e_real, 3, r44), ALU.mult))
            settle()
            did(v.tensor_tensor(gnum[0:P, :, :], gnum[0:P, :, :], bc(vecs[0:P, 2, :], 1, r16), ALU.add))
            settle()
            did(normalise(3, gnum[0:P, :, :], gnum[0:P, :, :], GF, gsq[0:P, :, :]))
            settle()
            did(v.tensor_tensor(gnum[0:P, :, :], gnum[0:P, :, :], bc(vecs[0:P, 3, :], 1, r16), ALU.mult))
            settle()
            did(v.tensor_tensor(gnum[0:P, :, :], gnum[0:P, :, :], bc(vecs[0:P, 4, :], 1, r16), ALU.add))
            settle()

            did(v.tensor_reduce(s1[0:P, :, :], gnum[0:P, :, :].rearrange("p t (h e) -> p t e h", h=GH), AX, ALU.add))
            settle()
            sc = s2[0:P, :, :]
            did(v.tensor_scalar(sc, s1[0:P, :, :], 1.0 / GH, None, ALU.mult))
            settle()
            ree = [P, NT, EX, EX]
            other, mine = bc(sc, 2, ree), bc(sc, 3, ree)
            first = lower[0:P, :].rearrange("p (e j) -> p e j", e=EX).unsqueeze(1).to_broadcast(ree)
            beats = gprod[0:P, :, :].rearrange("p t (e j) -> p t e j", e=EX)
            ties = gnum[0:P, :, :].rearrange("p t (e j) -> p t e j", e=EX)
            did(v.tensor_tensor(beats, other, mine, ALU.is_gt))
            did(v.tensor_tensor(ties, other, mine, ALU.is_equal))
            did(v.tensor_reduce(stat[0:P, 0, :], sc, AX, ALU.max))
            settle()
            did(v.tensor_tensor(ties, ties, first, ALU.mult))
            v.tensor_tensor(gate[0:P, :, :], sc, bc(stat[0:P, 0, :], 2, [P, NT, EX]), ALU.subtract).then_inc(exp_in, 1)
            settle()
            did(v.tensor_tensor(beats, beats, ties, ALU.add))
            settle()
            did(v.tensor_reduce(s3[0:P, :, :], beats, AX, ALU.add))
            settle()
            did(v.tensor_scalar(s3[0:P, :, :], s3[0:P, :, :], 2.0, None, ALU.is_lt))
            settle()
            v.wait_ge(exp_out, 3)
            did(v.tensor_tensor(gate[0:P, :, :], gate[0:P, :, :], s3[0:P, :, :], ALU.mult))
            settle()
            did(v.tensor_reduce(stat[0:P, 0, :], gate[0:P, :, :], AX, ALU.add))
            settle()
            did(v.reciprocal(stat[0:P, 1, :], stat[0:P, 0, :]))
            settle()
            did(v.tensor_tensor(gate[0:P, :, :], gate[0:P, :, :], bc(stat[0:P, 1, :], 2, [P, NT, EX]), ALU.mult))
            settle()
            v.wait_ge(y_copied, B * EX + EX)
            for e in range(EX):
                did(v.tensor_tensor(yexp[0:P, :, e, :], yexp[0:P, :, e, :], bc(gate[0:P, :, e], 2, [P, NT, D]), ALU.mult))
            settle()
            for e in range(EX):
                ins = v.tensor_tensor(h[0:P, :, :], h[0:P, :, :], yexp[0:P, :, e, :], ALU.add)
                if e < EX - 1:
                    did(ins)
                    settle()
                else:
                    ins.then_inc(out_ready, 1)


_ARGS = ("x", "w_step", "w_in", "w_mix", "w_c", "att_tgt", "att_attr", "w_qk", "w_v", "w_o", "w_e",
         "w_gat", "att_vec", "w1", "b2", "w2", "gat_src", "gat_dst")


def layouts(x, L0_tok_W1, L0_tok_b1, L0_tok_W2, L0_tok_b2, L0_tok_W3, L0_tok_b3, L0_tok_W4, L0_tok_b4,
            L0_attn_edge_index, L0_attn_edge_attr, L0_attn_Wq, L0_attn_bq, L0_attn_Wk, L0_attn_bk, L0_attn_Wv,
            L0_attn_bv, L0_attn_Wo, L0_attn_bo, L0_attn_We, L0_attn_be, L0_ffn_W_gat, L0_ffn_att_src,
            L0_ffn_att_dst, L0_ffn_b_gat, L0_ffn_ln_gamma, L0_ffn_ln_beta, L0_ffn_W1, L0_ffn_b1, L0_ffn_W2,
            L0_ffn_b2, L0_ffn_edge_index):
    cat = np.concatenate
    z = np.zeros((D, D), np.float32)
    step = cat([cat([L0_tok_W2.T, z], 1), cat([z, L0_tok_W2.T], 1)], 0)
    one_half = cat([L0_tok_W1.T, L0_tok_b1[None], L0_tok_b2[None]], 0)
    wv = np.zeros((D + 1, H, 32), np.float32)
    wv[:D, :, :HD] = L0_attn_Wv.reshape(D, H, HD)
    wv[D, :, :HD] = L0_attn_bv.reshape(H, HD)
    wv[D, :, HD] = 1
    w1 = cat([L0_ffn_W1, L0_ffn_b1[:, None, :]], 1)
    return {
        "x": x,
        "w_step": step,
        "w_in": cat([one_half, one_half], 1),
        "w_mix": cat([L0_tok_W4.T, L0_tok_W4.T], 0),
        "w_c": cat([L0_tok_W3.T, L0_tok_b3[None], L0_tok_b4[None], L0_tok_b4[None]], 0),
        "att_tgt": L0_attn_edge_index[1].reshape(128, JA),
        "att_attr": L0_attn_edge_attr,
        "w_qk": cat([cat([L0_attn_Wq, L0_attn_bq[None]], 0), cat([L0_attn_Wk, L0_attn_bk[None]], 0)], 1),
        "w_v": wv.reshape(D + 1, 32 * H),
        "w_o": cat([L0_attn_Wo, L0_attn_bo[None]], 0),
        "w_e": cat([L0_attn_We, L0_attn_be[None]], 0),
        "w_gat": L0_ffn_W_gat,
        "att_vec": np.stack([L0_ffn_att_src.reshape(-1), L0_ffn_att_dst.reshape(-1), L0_ffn_b_gat,
                             L0_ffn_ln_gamma, L0_ffn_ln_beta]),
        "w1": np.transpose(w1, (1, 0, 2)),
        "b2": L0_ffn_b2[None],
        "w2": np.transpose(L0_ffn_W2, (1, 0, 2)),
        "gat_src": L0_ffn_edge_index[0].reshape(128, JG),
        "gat_dst": L0_ffn_edge_index[1].reshape(128, JG),
    }


def kernel(**inputs):
    import concourse.bacc as bacc
    from concourse.bass_utils import run_bass_kernel_spmd

    laid = layouts(**{k: np.asarray(a) for k, a in inputs.items()})
    laid.update(constants())
    nc = bacc.Bacc("TRN2", target_bir_lowering=False, num_devices=1)
    arrays, args = {}, {}
    for name, a in laid.items():
        a = np.ascontiguousarray(a)
        arrays[f"in_{name}"] = a
        args[name] = nc.dram_tensor(f"in_{name}", a.shape, mybir.dt.from_np(a.dtype), kind="ExternalInput").ap()
    out = nc.dram_tensor("out_dram", (B, L, D), F32, kind="ExternalOutput").ap()
    graph_transformer_block(nc, out=out, **args)
    r = run_bass_kernel_spmd(nc, [arrays], core_ids=[0])
    return r.results[0]["out_dram"]
```

```python
from contextlib import ExitStack

import numpy as np

import concourse.bass as bass
from concourse import mybir

F32 = mybir.dt.float32
F16 = mybir.dt.float16
BF16 = mybir.dt.bfloat16
I32 = mybir.dt.int32
ALU = mybir.AluOpType
ACT = mybir.ActivationFunctionType
AX = mybir.AxisListType.X
MAX_ALL = bass.bass_isa.ReduceOp.max

B, DIN, L, D = 8, 4, 375, 64
STEPS = 8
H, HD = 8, 8
M = B * L
P = 125
KT = L // P
NT = M // P
GH, EX = 4, 4
GF = GH * EX
HID = 2 * D
E_ATT = 16384
JA = E_ATT // 128
E_GAT = 262144
JG = E_GAT // 128
LAST = M - 1
EPS = 1e-5
NEG = -1e30
MAGIC = 12582912.0

CAP = 104
OWN_PARTS, OWN_KEEP = 4, 40
RANKS = 8
SLOTS = 128 * RANKS
SRC_BITS, TILE_BITS = 12, 5
SKIP = float(P * SLOTS + 72000)
SPLIT, LONG = 72, 96
UPPER = 12
GROUP = 64
PART, KEEP = 128, 48
NPART = JG // PART
KEPT = NPART * KEEP
HOTS = KEPT // 16
CONST_AT = 8
FEW = 72
NO_SLOT = float(L * 128)
RES = 2 * GH + GF

Q_PART = (0, 0, 1, 0, 2, 1)
K_PART = (0, 1, 0, 2, 0, 1)
BIAS_ROW = 8 * len(Q_PART)
MAX_ROW = BIAS_ROW + 3
MAX_PARTS = 2
ONES_ROW = 3 * H


def constants():
    bf = mybir.dt.np(BF16)
    sel = np.zeros((128, 2, 3, 4, 128), np.float32)
    ext = np.zeros((3 * H + 1, 4, 128), np.float32)
    q_ones = np.zeros((128, 1), np.float32)
    for h in range(H):
        pair, base = h // 2, 64 * (h % 2)
        for c, (qp, kp) in enumerate(zip(Q_PART, K_PART)):
            for d in range(HD):
                sel[h * HD + d, 0, qp, pair, base + c * HD + d] = 1
                sel[64 + h * HD + d, 1, kp, pair, base + c * HD + d] = 1
        for part in range(3):
            q_ones[base + BIAS_ROW + part] = 1
            ext[h * 3 + part, pair, base + BIAS_ROW + part] = 1
            if part < MAX_PARTS:
                ext[ONES_ROW, pair, base + MAX_ROW + part] = 1
    eye = np.eye(128, dtype=np.float32)
    lane = np.broadcast_to(np.arange(128, dtype=np.float32), (128, 128))
    iota = np.broadcast_to(np.arange(512, dtype=np.float32), (128, 512))
    fold = np.ascontiguousarray(np.tile(np.eye(32, dtype=np.float32), (4, 1))[:, :NT])
    scale = np.ones((128, 1), np.float32)
    scale[:64] = HD ** -0.5
    hot = np.broadcast_to(np.arange(128, dtype=np.float32)[None, :, None], (128, 128, 16))
    hot = np.ascontiguousarray(hot).astype(bf)
    lower = np.tril(np.ones((EX, EX), np.float32), -1)
    return {
        "c_sel": sel.astype(bf), "c_ext": ext.astype(bf), "c_q_ones": q_ones, "c_fold": fold,
        "c_eye": eye, "c_eyeb": eye.astype(bf), "c_iota": np.ascontiguousarray(iota),
        "c_scale": scale, "c_hot": hot,
        "c_part": RANKS * np.arange(128, dtype=np.float32)[:, None],
        "c_lower": np.ascontiguousarray(np.broadcast_to(lower.reshape(1, -1), (128, EX * EX))),
    }


def graph_transformer_block(nc, x, w_step, w_in, w_mix, w_c,
                            att_tgt, att_attr, w_qk, w_v, w_o, w_e,
                            w_gat, att_vec, w1, b2, w2, gat_src, gat_dst,
                            c_sel, c_ext, c_q_ones, c_fold, c_eye, c_eyeb, c_iota, c_scale, c_hot, c_part, c_lower,
                            out):
    ctx = ExitStack()
    with ctx:
        def sb(name, shape, dt=F32):
            return ctx.enter_context(nc.sbuf_tensor(name, shape, dt))

        def sem(name):
            return ctx.enter_context(nc.semaphore(name))

        exchange = nc.dram_tensor("exchange", (P * SLOTS, 1), F32, kind="Internal").ap()
        node_rows = nc.dram_tensor("node_rows", (M, GF + GH), F32, kind="Internal").ap()
        beyond_few = nc.dram_tensor("beyond_few", (128, 1), F32, kind="Internal").ap()
        upper_rows = nc.dram_tensor("upper_rows", (P * SPLIT, RES), F32, kind="Internal").ap()
        last_edges = nc.dram_tensor("last_edges", (L * 128, 1), F32, kind="Internal").ap()
        edge_rows = nc.dram_tensor("edge_rows", (P * CAP, RES), F32, kind="Internal").ap()

        ps = ctx.enter_context(nc.psum_tensor("ps", [128, 8, 512], F32))

        wstep = sb("wstep", [128, 128])
        win = sb("win", [6, 128])
        wmix = sb("wmix", [128, D])
        wc = sb("wc", [7, D])
        wqk = sb("wqk", [D + 1, 128])
        wv = sb("wv", [D + 1, (HD + 1) * H])
        wo = sb("wo", [D + 1, D])
        wgat = sb("wgat", [128, 2 * GF])
        we = sb("we", [128, 4, H])
        vecs = sb("vecs", [128, 5, GF])
        w1s = sb("w1s", [D + 1, EX, HID])
        w2s = sb("w2s", [HID, EX, D])
        b2s = sb("b2s", [128, EX, D])
        sel = sb("sel", [128, 2, 3, 4, 128], BF16)
        ext = sb("ext", [ONES_ROW + 1, 4, 128], BF16)
        q_ones = sb("q_ones", [128, 1])
        fold = sb("fold", [128, NT])
        kbias = sb("kbias", [128, 4, L], BF16)
        eye = sb("eye", [128, 128])
        eyeb = sb("eyeb", [128, 128], BF16)
        iota = sb("iota", [128, 512])
        qk_scale = sb("qk_scale", [128, 1])
        hot = sb("hot", [128, 128, 16], BF16)
        part = sb("part", [128, 1])
        lower = sb("lower", [128, EX * EX])
        tok_x = sb("tok_x", [128, B, L])
        xaug = tok_x[0:7, :, :]
        state = sb("state", [128, B, L + 2])
        add_in = sb("add_in", [128, B, L])
        big = sb("big", [128, 8, JG])

        def view(first, at, shape, dt=F32):
            n = int(np.prod(shape))
            flat = big[:, first:8, :].rearrange("p a b -> p (a b)")
            flat = flat[:, at:at + n] if dt is F32 else flat[:, at:at + n // 2].bitcast(dt)
            names = "abcd"[:len(shape)]
            if len(shape) == 1:
                return flat
            return flat.rearrange(f"p ({' '.join(names)}) -> p {' '.join(names)}", **dict(zip(names[1:], shape[1:])))

        h = sb("h", [128, NT, D])
        xn = sb("xn", [128, NT, D])
        sq = sb("sq", [128, NT, D])
        stat = sb("stat", [128, 4, NT])
        xT = add_in[0:D + 1, :, :].rearrange("p b l -> p (b l)")
        probs = view(0, 0, [2, KT, L])
        vv = view(2, 0, [2, KT, 32 * H])
        qst = view(3, 0, [2, 4, L], BF16)
        kst = view(3, L * 4, [2, 4, L], BF16)
        qk32 = view(5, 0, [L])
        rest = view(5, L, [L])
        parts = view(5, 2 * L, [3, L + 1], BF16)[:, :, 0:L]
        oT = view(5, 4 * L, [2, L])
        xb = view(5, 6 * L, [2, L])[0:D + 1]
        onT = view(5, 8 * L, [L])[0:D + 1]
        on = view(5, 9 * L, [KT, D])
        negmax = sb("negmax", [128, KT, H])
        nrest = sb("nrest", [128, KT, H])
        nparts = sb("nparts", [128, 2, KT, 2, 2, MAX_PARTS], BF16)
        maxT = sb("maxT", [MAX_PARTS * H // 2, 2, L], BF16)
        rden = sb("rden", [128, KT, 4])
        tgt = sb("tgt", [128, JA])
        tgt_i = sb("tgt_i", [128, JA], I32)
        more_i = sb("more_i", [1, 1], I32)
        more_row = sb("more_row", [1, 128])
        more_top = sb("more_top", [1, 1])
        last = sb("last", [128, KT, 128])
        lastf = sb("lastf", [128, 2, KT])
        last_i = sb("last_i", [128, KT], I32)
        attr = sb("attr", [128, KT, 3])
        bias = sb("bias", [128, KT, H])
        bparts = sb("bparts", [128, KT, H, 3], BF16)
        biasT = sb("biasT", [ONES_ROW + 1, L], BF16)
        src_i = big[:, 0, :].bitcast(I32)
        dst_i = big[:, 1, :].bitcast(I32)
        f_tile, f_own, f_key, f_real, f_tmp = (big[:, k, :] for k in range(2, 7))
        kept = big[:, 7, 0:KEPT]
        kept_i, low_i, code_i = (big[:, k, 0:KEPT].bitcast(I32) for k in (0, 1, 2))
        no_count, kept_real = big[:, 3, 0:KEPT], big[:, 5, 0:KEPT]
        own_h = sb("own_h", [128, KEPT + 32], BF16)
        tile_h = sb("tile_h", [128, KEPT + 32], BF16)
        hot_own = sb("hot_own", [128, 2, 128, 16], BF16)
        hot_tile = sb("hot_tile", [128, 2, 32, 16], BF16)
        lane_list = sb("lane_list", [128, CAP])
        lane_int = sb("lane_int", [128, CAP], I32)
        lane_tmp = sb("lane_tmp", [128, 4, CAP])
        slot_i = sb("slot_i", [128, CAP], I32)
        own_tab = sb("own_tab", [128, SLOTS])
        own_list = sb("own_list", [128, CAP])
        own_int = sb("own_int", [128, CAP], I32)
        own_tmp_i = sb("own_tmp_i", [128, 2, CAP], I32)
        src_idx = sb("src_idx", [128, CAP], I32)
        seg = sb("seg", [128, CAP])
        keep = sb("keep", [128, CAP])
        member = sb("member", [128, CAP, NT])
        at_least = tok_x[:, :, :].rearrange("p a b -> p (a b)")[:, 0:NT * CAP].rearrange("p (t c) -> p t c", t=NT)
        spare = member[:, :, :].rearrange("p a b -> p (a b)")
        tgt_key, tgt_list, tgt_val, tgt_slot, tgt_new = (spare[:, k * JA:(k + 1) * JA] for k in range(5))
        tgt_no, tgt_j, tgt_slot_i = (spare[:, k * JA:(k + 1) * JA].bitcast(I32) for k in range(5, 8))
        endf = sb("endf", [128, 2, NT])
        upper_idx = sb("upper_idx", [128, NT], I32)
        end_idx = sb("end_idx", [128, NT], I32)
        has_real = sb("has_real", [128, NT])
        flags = sb("flags", [128, 5])
        clamped = sb("clamped", [128, NT])
        clampT = sb("clampT", [128, 128])
        got = state[:, :, :].rearrange("p a b -> p (a b)")[:, 0:CAP * (GF + GH)].rearrange(
            "p (c f) -> p c f", f=GF + GH)
        msg = view(7, 0, [CAP, GF])
        adst_e = sb("adst_e", [128, CAP, GH])
        score = sb("score", [128, CAP, GH])
        run_max = sb("run_max", [128, CAP, GH])
        expo = sb("expo", [128, 2, CAP, GH])
        tab = sb("tab", [128, NT, GF + GH])
        adst = sb("adst", [128, NT, GH])
        gprod = sb("gprod", [128, NT, GF])
        sums = sb("sums", [128, NT])
        lastrow = sb("lastrow", [128, GF + GH])
        ends = sb("ends", [128, NT, RES])
        st_max = sb("st_max", [128, NT, GH])
        st_den = sb("st_den", [128, NT, GH])
        st_num = sb("st_num", [128, NT, GF])
        s1, s2, s3, s4 = (sb(f"s{k}", [128, NT, GH]) for k in range(1, 5))
        acc = view(3, CAP * NT, [NT, RES])
        raw_i = sb("raw_i", [128, 2, GROUP], I32)
        over_i = sb("over_i", [1, 2], I32)
        flag_row = sb("flag_row", [1, 2])
        wts = sb("wts", [128, 3, NT, GH])
        gnum = sb("gnum", [128, NT, GF])
        gsq = sb("gsq", [128, NT, GF])
        own_row = sb("own_row", [128, 1])
        gate = sb("gate", [128, NT, EX])
        hid = tok_x[:, 0:EX, :]
        pairs = view(0, 0, [B // 2, L])
        yexp = view(0, 0, [NT, EX, D])
        wide = view(3, 0, [CAP * NT])
        res = view(5, 0, [CAP, RES])

        tok_in = sem("tok_in")
        mix_in = sem("mix_in")
        edges_in = sem("edges_in")
        consts_in = sem("consts_in")
        tgt_in = sem("tgt_in")
        weights_in = sem("weights_in")
        zeros_set = sem("zeros_set")
        exchange_zeroed = sem("exchange_zeroed")
        state_zeroed = sem("state_zeroed")
        vec = sem("vec")
        act_own = sem("act_own")
        tok_sum = sem("tok_sum")
        tok_state = sem("tok_state")
        mix_done = sem("mix_done")
        h_ready = sem("h_ready")
        slots_ready = sem("slots_ready")
        scattered = sem("scattered")
        table_in = sem("table_in")
        hot_ready = sem("hot_ready")
        hist_added = sem("hist_added")
        tgt_slots_ready = sem("tgt_slots_ready")
        tgt_listed = sem("tgt_listed")
        more_out = sem("more_out")
        more_in = sem("more_in")
        more_own = sem("more_own")
        more_ready = sem("more_ready")
        last_zeroed = sem("last_zeroed")
        last_scattered = sem("last_scattered")
        more_scattered = sem("more_scattered")
        last_written = sem("last_written")
        last_in = sem("last_in")
        last_ready = sem("last_ready")
        attr_in = sem("attr_in")
        bparts_ready = sem("bparts_ready")
        biasT_done = sem("biasT_done")
        biasT_ready = sem("biasT_ready")
        centred = sem("centred")
        squared = sem("squared")
        var_ready = sem("var_ready")
        std_ready = sem("std_ready")
        stats_ready = sem("stats_ready")
        rows_added = sem("rows_added")
        xn_ready = sem("xn_ready")
        xT_done = sem("xT_done")
        xT_ready = sem("xT_ready")
        pairs_ready = sem("pairs_ready")
        misc_full = sem("misc_full")
        misc_free = sem("misc_free")
        first_free = sem("first_free")
        xb_ready = sem("xb_ready")
        qk32_ready = sem("qk32_ready")
        parts_ready = sem("parts_ready")
        score_full = sem("score_full")
        scoreT_full = sem("scoreT_full")
        max_done = sem("max_done")
        exp_done = sem("exp_done")
        pv_done = sem("pv_done")
        oT_ready = sem("oT_ready")
        negmax_ready = sem("negmax_ready")
        maxT_ready = sem("maxT_ready")
        max0_in = sem("max0_in")
        max1_in = sem("max1_in")
        kbias_done = sem("kbias_done")
        kbias_ready = sem("kbias_ready")
        gat_done = sem("gat_done")
        gat_read = sem("gat_read")
        tab_ready = sem("tab_ready")
        tab_out = sem("tab_out")
        lastrow_in = sem("lastrow_in")
        gathered = sem("gathered")
        gathered_late = sem("gathered_late")
        long_in = sem("long_in")
        long_gathered = sem("long_gathered")
        lists_ready = sem("lists_ready")
        hid_full = sem("hid_full")
        hid_ready = sem("hid_ready")
        y_full = sem("y_full")
        y_copied = sem("y_copied")
        exp_in = sem("exp_in")
        exp_out = sem("exp_out")
        res_ready = sem("res_ready")
        res_out = sem("res_out")
        res_late_out = sem("res_late_out")
        ends_in = sem("ends_in")
        out_ready = sem("out_ready")
        out_done = sem("out_done")
        flags_ready = sem("flags_ready")
        flags_done = sem("flags_done")
        over_own = sem("over_own")
        over_ready = sem("over_ready")
        g_next = sem("g_next")
        g_raw_in = sem("g_raw_in")
        g_lists = sem("g_lists")
        g_gathered = sem("g_gathered")
        g_rows_in = sem("g_rows_in")
        g_ends_gathered = sem("g_ends_gathered")
        g_exp_in = sem("g_exp_in")
        g_exp_out = sem("g_exp_out")
        g_res = sem("g_res")
        g_res_out = sem("g_res_out")
        g_ends_in = sem("g_ends_in")
        ones_set = sem("ones_set")
        xT_ones_set = sem("xT_ones_set")
        gates_ready = sem("gates_ready")
        act_weighed = sem("act_weighed")
        pool_weighed = sem("pool_weighed")
        cut = sem("cut")
        ncut = sem("ncut")
        rden_ready = sem("rden_ready")

        block = ctx.enter_context(nc.Block())

        class Own:

            def __init__(self, eng, own):
                self.eng, self.own, self.n = eng, own, 0

            def did(self, ins):
                ins.then_inc(self.own, 1)
                self.n += 1

            def settle(self):
                self.eng.wait_ge(self.own, self.n)

        def take(eng, s, n):
            eng.wait_ge(s, n)
            eng.sem_clear(s)

        def if_lists_overflowed(eng, body):
            eng.wait_ge(over_ready, 1)
            over = eng.value_load(over_i[0:1, 0:1], min_val=0, max_val=1)
            with eng.If(over > 0):
                with eng.Fori(0, E_GAT // GROUP) as i:
                    body(i)

        SOON = B - 2
        EARLY = 7
        N_CONSTS = 7
        N_WEIGHTS = 10
        HALF_U = ((0, 2), (64, 0))

        FIRST = [("qk", 0, 0), ("q0", 0, 0), ("k0", 0, 0), ("q1", 0, 0), ("k1", 0, 0), ("score", 0, 0), ("q2", 0, 0),
                 ("score", 1, 0), ("k2", 0, 0), ("score", 2, 0), ("q3", 0, 0), ("score", 3, 0), ("k3", 0, 0),
                 ("score", 4, 0), ("qk", 0, 1), ("score", 5, 0), ("v", 0, 0), ("score", 6, 0),
                 ("score", 7, 0), ("q0", 0, 1), ("k0", 0, 1), ("max0", 0, 0), ("q1", 0, 1), ("k1", 0, 1),
                 ("q2", 0, 1), ("k2", 0, 1), ("q3", 0, 1), ("k3", 0, 1)]
        ASIDE = [[("max1", 0), ("qk", 2)], [("norm1", -1), ("q0", 2)], [("k0", 2), ("onT", -1)], [("q1", 2), ("v", 1)],
                 [("k1", 2), ("out", -1)], [("q2", 2), ("norm0", 0)], [("k2", 2), ("max0", 1)], [("q3", 2), ("k3", 2)]]
        NOT_SHARED = ("score", "exp", "pv", "hist", "owner6", "owner7")

        def order(ahead, extra, behind=1):
            seq = []
            for k in range(H):
                (one, one_off), (two, two_off) = ASIDE[k]
                one, two, other = (one, 0, one_off), (two, 0, two_off), (extra, k, 0)
                if k == 0:
                    seq += [("score", 0, 1), ("exp", 0, 0), one, two, other]
                elif k in (1, 5):
                    seq += [("exp", k, 0), ("score", k, 1), one, other, ("pv", k - 1, 0), ("score", k + 1, 1), two]
                elif k == 2:
                    seq += [("exp", k, 0), one, ("pv", k - 1, 0), two, other]
                elif k == H - 2:
                    seq += [("exp", k, 0), one, ("pv", k - 1, 0), two, other, ("score", k + 1, 1)]
                elif k == H - 1:
                    seq += [("exp", k, 0), one, ("pv", k - 1, 0), two, other]
                else:
                    seq += [("exp", k, 0), one, ("score", k, 1), ("pv", k - 1, 0), two, other]
            seq.append(("pv", H - 1, 0))
            if not ahead:
                seq += [("norm1", 0, 0), ("onT", 0, 0), ("out", 0, 0)]
            return [step for step in seq if -behind <= step[2] <= ahead]

        def shared(seq):
            return sum(kind not in NOT_SHARED for kind, _, _ in seq)

        N_FIRST, N_ZERO, N_TURN = shared(FIRST), shared(order(2, "hist", 0)), shared(order(2, "hist"))
        N_SIX = N_FIRST + N_ZERO + (B - 3) * N_TURN
        N_SEVEN = N_SIX + shared(order(1, "owner6"))
        N_SHARED = N_SEVEN + shared(order(0, "owner7"))

        def first_free_of(n):
            return (misc_free if n % 2 else first_free), n // 2 + 1

        def bc(ap, axis, shape):
            return ap.unsqueeze(axis).to_broadcast(shape)

        def turns(eng, body):
            body(0, 0, N_FIRST, 2, "hist", 0)
            with eng.Fori(0, B // 2 - 2) as i:
                for par in (1, 0):
                    b = 2 * i + (2 - par)
                    body(b, par, (b - 1) * N_TURN + (N_FIRST + N_ZERO), 2, "hist")
            body(B - 3, 1, N_SIX - N_TURN, 2, "hist")
            body(B - 2, 0, N_SIX, 1, "owner6")
            body(B - 1, 1, N_SEVEN, 0, "owner7")

        @block.sync
        def _(sp):
            sp.dma_start(tgt_i[:, :], att_tgt).then_inc(tgt_in, 16)
            sp.dma_start(iota[:, :], c_iota).then_inc(tgt_in, 16)
            sp.dma_start(part[:, :], c_part).then_inc(tgt_in, 16)
            sp.dma_start(dst_i, gat_dst).then_inc(edges_in, 16)
            sp.dma_start(src_i, gat_src).then_inc(edges_in, 16)
            sp.wait_ge(zeros_set, 2)
            sp.dma_start(last_edges.rearrange("(p l) a -> p (l a)", p=P), own_tab[0:P, 0:KT * 128]).then_inc(last_zeroed, 16)
            sp.dma_start(exchange.rearrange("(p s) a -> p (s a)", p=P), own_tab[0:P, :]).then_inc(exchange_zeroed, 16)
            for a, b_ in ((wmix[:, :], w_mix), (wc[:, :], w_c)):
                sp.dma_start(a, b_).then_inc(mix_in, 16)
            for a, b_ in ((sel[:, :, :, :, :], c_sel), (ext[:, :, :], c_ext), (q_ones[:, :], c_q_ones), (fold[:, :], c_fold),
                          (eyeb[:, :], c_eyeb), (qk_scale[:, :], c_scale), (hot[:, :, :], c_hot)):
                sp.dma_start(a, b_).then_inc(consts_in, 16)
            for a, b_ in ((wqk[:, :], w_qk), (wv[:, :], w_v), (wo[:, :], w_o), (wgat[:, :], w_gat),
                          (w1s[:, :, :], w1), (w2s[:, :, :], w2), (b2s[:, :, :], b2.to_broadcast([128, EX, D])),
                          (lower[:, :], c_lower),
                          (we[:, :, :], w_e.rearrange("(o k) h -> o k h", o=1).to_broadcast([128, 4, H])),
                          (vecs[:, :, :], att_vec.rearrange("(o k) h -> o k h", o=1).to_broadcast([128, 5, GF]))):
                sp.dma_start(a, b_).then_inc(weights_in, 16)
            sp.wait_ge(tgt_listed, 1)
            sp.dma_start(beyond_few, tgt_list[:, FEW:FEW + 1]).then_inc(more_out, 16)
            sp.wait_ge(more_out, 16)
            sp.dma_start(more_row[0:1, :], beyond_few.rearrange("l a -> a l")).then_inc(more_in, 16)
            sp.wait_ge(last_written, 1)
            sp.dma_start(last[0:P, :, :], last_edges.rearrange("(k p l) a -> p k (l a)", k=KT, p=P)).then_inc(last_in, 16)
            with sp.Fori(0, B // 2) as i:
                for par in range(2):
                    for g, done in enumerate((max0_in, max1_in)):
                        sp.wait_ge(maxT_ready, 4 * i + 2 * par + g + 1)
                        for r in range(2):
                            for w in range(2):
                                to, at = 64 * w + MAX_ROW, (2 * w + r) * MAX_PARTS
                                sp.dma_start(qst[to:to + MAX_PARTS, par, 2 * g + r, :], maxT[at:at + MAX_PARTS, g, :]).then_inc(done, 16)
            sp.wait_ge(tab_ready, 1)
            sp.dma_start(node_rows.rearrange("(t p) f -> p t f", p=P), tab[0:P, :, :]).then_inc(tab_out, 16)
            sp.wait_ge(tab_out, 16)
            sp.dma_start(lastrow[:, :], node_rows[LAST:LAST + 1, :].to_broadcast([128, GF + GH])).then_inc(lastrow_in, 16)
            by_owner = edge_rows.rearrange("(p c) f -> p c f", p=P)
            sp.wait_ge(res_ready, 1)
            sp.dma_start(upper_rows.rearrange("(p c) f -> p c f", p=P), res[0:P, 0:SPLIT, :]).then_inc(res_out, 16)
            sp.dma_start(by_owner[:, 0:SPLIT, :], res[0:P, 0:SPLIT, :]).then_inc(res_late_out, 16)
            sp.wait_ge(res_ready, 2)
            sp.dma_start(by_owner[:, SPLIT:CAP, :], res[0:P, SPLIT:CAP, :]).then_inc(res_late_out, 16)

            def group_in(i):
                take(sp, g_next, 1)
                for k, a in enumerate((gat_src, gat_dst)):
                    flat = a.rearrange("(o p) j -> o (p j)", o=1)
                    sp.dma_start(raw_i[:, k, :], flat[:, bass.ds(i * GROUP, GROUP)].to_broadcast([128, GROUP])).then_inc(g_raw_in, 16)
                take(sp, g_res, 1)
                sp.dma_start(edge_rows.rearrange("(p c) f -> p c f", p=P), res[0:P, :, :]).then_inc(g_res_out, 16)

            if_lists_overflowed(sp, group_in)
            for half in range(2):
                t = slice(half * NT // 2, (half + 1) * NT // 2)
                sp.wait_ge(out_ready, half + 1)
                sp.dma_start(out.rearrange("b (k p) d -> p (b k) d", p=P)[:, t, :], h[0:P, t, :]).then_inc(out_done, 16)
            sp.wait_ge(out_done, 32)

        @block.gpsimd
        def _(pool):
            pool.memset(xaug[:, :, :], 1.0).then_inc(zeros_set, 1)
            pool.wait_ge(zeros_set, 1)
            pool.memset(own_tab[:, :], 0.0).then_inc(zeros_set, 1)
            def write_last(first, end, done):
                for c in range(first, end):
                    pool.indirect_dma_start(
                        out=last_edges, out_offset=bass.IndirectOffsetOnAxis(ap=tgt_slot_i[:, c:c + 1], axis=0),
                        in_=tgt_val[:, c:c + 1], in_offset=None,
                        bounds_check=L * 128 - 1, oob_is_err=False).then_inc(done, 16)

            pool.wait_ge(tgt_slots_ready, 1)
            pool.wait_ge(last_zeroed, 16)
            write_last(0, FEW, last_scattered)
            pool.wait_ge(more_ready, 1)
            more = pool.value_load(more_i[0:1, 0:1], min_val=0, max_val=1)
            with pool.If(more > 0):
                write_last(FEW, JA, more_scattered)
                pool.wait_ge(more_scattered, 16 * (JA - FEW))
            pool.wait_ge(last_scattered, 16 * FEW)
            pool.sem_inc(last_written, 1)

            def gather_attributes():
                pool.wait_ge(last_ready, 1)
                for k in range(KT):
                    pool.indirect_dma_start(
                        out=attr[0:P, k, :], out_offset=None, in_=att_attr,
                        in_offset=bass.IndirectOffsetOnAxis(ap=last_i[0:P, k:k + 1], axis=0)).then_inc(attr_in, 16)

            def constant_rows():
                pool.memset(xb[D:D + 1, :, :], 1.0).then_inc(ones_set, 1)
                pool.wait_ge(ones_set, 1)
                pool.memset(onT[D:D + 1, :], 1.0).then_inc(ones_set, 1)
                pool.wait_ge(ones_set, 2)
                pool.memset(vv[:, :, :, :], 0.0).then_inc(ones_set, 1)

            gather_attributes()
            pool.wait_ge(slots_ready, 1)
            pool.wait_ge(exchange_zeroed, 16)
            for c in range(CAP):
                if c == CONST_AT:
                    pool.wait_ge(bparts_ready, 1)
                    constant_rows()
                pool.indirect_dma_start(
                    out=exchange, out_offset=bass.IndirectOffsetOnAxis(ap=slot_i[:, c:c + 1], axis=0),
                    in_=lane_list[:, c:c + 1], in_offset=None,
                    bounds_check=P * SLOTS - 1, oob_is_err=False).then_inc(scattered, 16)
            pool.wait_ge(scattered, 16 * CAP)
            pool.dma_start(own_tab[0:P, :], exchange.rearrange("(p s) a -> p (s a)", p=P)).then_inc(table_in, 16)

            def gather_rows(first, end, done):
                for c in range(first, end):
                    pool.indirect_dma_start(
                        out=got[0:P, c, :], out_offset=None, in_=node_rows,
                        in_offset=bass.IndirectOffsetOnAxis(ap=src_idx[0:P, c:c + 1], axis=0)).then_inc(done, 16)

            def gather_ends(first, end, done, table=edge_rows, idx=end_idx):
                for t in range(first, end):
                    pool.indirect_dma_start(
                        out=ends[0:P, t, :], out_offset=None, in_=table,
                        in_offset=bass.IndirectOffsetOnAxis(ap=idx[0:P, t:t + 1], axis=0)).then_inc(done, 16)

            pool.wait_ge(ones_set, 3)
            pool.wait_ge(mix_done, 1)
            pool.memset(xT[D:D + 1, :], 1.0).then_inc(xT_ones_set, 1)
            pool.wait_ge(lists_ready, 1)
            pool.wait_ge(tab_out, 16)
            gather_rows(0, SPLIT, gathered)
            gather_rows(SPLIT, LONG, gathered_late)
            pool.wait_ge(over_ready, 1)
            long_ = pool.value_load(over_i[0:1, 1:2], min_val=0, max_val=1)
            with pool.If(long_ > 0):
                gather_rows(LONG, CAP, long_in)
                pool.wait_ge(long_in, 16 * (CAP - LONG))
            pool.sem_inc(long_gathered, 1)
            pool.wait_ge(res_out, 16)
            gather_ends(UPPER, NT, ends_in, upper_rows, upper_idx)
            pool.wait_ge(res_late_out, 32)
            gather_ends(0, UPPER, ends_in)

            def landed(done, n, tell):
                pool.wait_ge(done, 16 * n)
                pool.dma_reset(range(done.num, done.num + 1))
                pool.sem_clear(done)
                pool.sem_inc(tell, 1)

            def group_rows(i):
                take(pool, g_lists, 1)
                gather_rows(0, GROUP, g_gathered)
                landed(g_gathered, GROUP, g_rows_in)
                take(pool, g_res_out, 16)
                gather_ends(0, NT, g_ends_gathered)
                landed(g_ends_gathered, NT, g_ends_in)

            if_lists_overflowed(pool, group_rows)
            pool.wait_ge(gates_ready, 1)
            for half, e in ((0, 3), (1, 3), (1, 1)):
                t = slice(half * NT // 2, (half + 1) * NT // 2)
                pool.tensor_tensor(yexp[0:P, t, e, :], yexp[0:P, t, e, :], bc(gate[0:P, t, e], 2, [P, NT // 2, D]),
                                   ALU.mult).then_inc(pool_weighed, 1)

        @block.tensor
        def _(pe):
            pe.wait_ge(tok_in, 64)
            for b in range(B):
                pe.matmul(ps[:, b, 0:L], win[0:6, :], xaug[0:6, b, :], start=True, stop=True).then_inc(tok_sum, 1)
            pe.wait_ge(state_zeroed, 1)
            with pe.Fori(1, STEPS) as r:
                for b in range(B):
                    pe.wait_ge(tok_state, (r - 1) * (2 * B) + 2 * (b + 1))
                    pe.matmul(ps[:, b, 0:L], eye[:, :], add_in[:, b, :], start=True, stop=False)
                    pe.matmul(ps[:, b, 0:L], wstep[:, :], state[:, b, 1:L + 1], start=False, stop=True).then_inc(tok_sum, 1)
            pe.wait_ge(mix_in, 32)
            pe.wait_ge(tok_state, STEPS * 2 * B)
            for t in range(NT):
                b, k = divmod(t, KT)
                bank, col = divmod(t, 8)
                o = ps[0:P, bank, col * D:(col + 1) * D]
                pe.matmul(o, state[:, b, 1 + k * P:1 + (k + 1) * P], wmix[:, :], start=True, stop=False)
                mm = pe.matmul(o, xaug[0:7, b, k * P:(k + 1) * P], wc[:, :], start=False, stop=True)
            mm.then_inc(mix_done, 1)

            pe.wait_ge(consts_in, 16 * N_CONSTS)
            def turn_xn(q):
                for j in range(KT):
                    t = q * 2 * KT + 2 * j
                    mm = pe.matmul(ps[:, q, j * P:(j + 1) * P], xn[0:P, t:t + 2, :].rearrange("p a d -> p (a d)"),
                                   eye[0:P, 0:P], start=True, stop=True)
                mm.then_inc(xT_done, 1)

            pe.wait_ge(bparts_ready, 1)
            for k in range(KT):
                mm = pe.matmul(ps[0:3 * H, 3, k * P:(k + 1) * P], bparts[0:P, k, :, :].rearrange("p h c -> p (h c)"),
                               eyeb[0:P, 0:P], start=True, stop=True)
            mm.then_inc(biasT_done, 1)

            pe.wait_ge(h_ready, 3)
            pe.wait_ge(biasT_ready, 1)
            for r in range(4):
                mm = pe.matmul(ps[:, 2 + r, 0:L], ext[:, r, :], biasT[:, :], start=True, stop=True)
            mm.then_inc(kbias_done, 1)
            pe.wait_ge(xn_ready, 1)
            turn_xn(0)
            turn_xn(1)
            pe.wait_ge(weights_in, 16 * N_WEIGHTS)
            pe.wait_ge(ones_set, 3)

            def pass_through(kind, par, n, b=None, bank=7):
                misc = ps[:, bank, :]
                if isinstance(n, int) and n < N_FIRST:
                    if n > 1:
                        pe.wait_ge(*first_free_of(n - 2))
                else:
                    pe.wait_ge(misc_free, n)
                if kind == "qk":
                    pe.wait_ge(xb_ready, b + 1)
                    mm = pe.matmul(misc[:, 0:L], wqk[:, :], xb[:, par, :], start=True, stop=True)
                elif kind == "v":
                    for k in range(KT):
                        mm = pe.matmul(misc[0:P, (HD + 1) * H * k:(HD + 1) * H * (k + 1)],
                                       xb[:, par, k * P:(k + 1) * P], wv[:, :], start=True, stop=True)
                elif kind[0] in "qk" and len(kind) == 2:
                    side, pair = "qk".index(kind[0]), int(kind[1])
                    if kind == "q0":
                        pe.wait_ge(parts_ready, b + 1)
                    for part_ in range(3):
                        mm = pe.matmul(misc[:, 0:L], sel[:, side, part_, pair, :], parts[:, part_, :],
                                       start=(part_ == 0), stop=(part_ == 2))
                elif kind in ("max0", "max1"):
                    g = int(kind[3])
                    pe.wait_ge(negmax_ready, 2 * b + g + 1)
                    for k in range(KT):
                        mm = pe.matmul(misc[0:MAX_PARTS * H // 2, k * P:(k + 1) * P],
                                       nparts[0:P, g, k, :, :, :].rearrange("p w r c -> p (w r c)"),
                                       eyeb[0:P, 0:P], start=True, stop=True)
                elif kind in ("norm0", "norm1"):
                    g = int(kind[4])
                    pe.wait_ge(oT_ready, 2 * b + g + 2)
                    for k in range(KT):
                        mm = pe.matmul(misc[0:P, k * 128:(k + 1) * 128], oT[:, g, k * P:(k + 1) * P], eye[:, :],
                                       start=True, stop=True)
                elif kind == "onT":
                    for k in range(KT):
                        mm = pe.matmul(misc[0:D, k * P:(k + 1) * P], on[0:P, k, :], eye[0:P, 0:P],
                                       start=True, stop=True)
                elif kind == "out":
                    for k in range(KT):
                        mm = pe.matmul(misc[0:P, k * D:(k + 1) * D], onT[:, k * P:(k + 1) * P], wo[:, :],
                                       start=True, stop=True)
                mm.then_inc(misc_full, 1)

            pass_through("qk", 0, 0, 0, 6)
            pe.wait_ge(kbias_ready, 1)
            for q in range(2, B // 2):
                turn_xn(q)
            pe.wait_ge(xT_ready, B)


            def scores(c, par, k):
                base, pair = 64 * (k % 2), k // 2
                for t in range(KT):
                    mm = pe.matmul(ps[0:P, t, 0:L], qst[base:base + 64, par, pair, t * P:(t + 1) * P],
                                   kst[base:base + 64, par, pair, :], start=True, stop=True)
                mm.then_inc(score_full, 1)

            n = 1
            for kind, k, off in FIRST[1:]:
                if kind == "score":
                    for m in (n - 2, n - 1):
                        pe.wait_ge(*first_free_of(m))
                    if k:
                        pe.wait_ge(max_done, k)
                    scores(0, 0, k)
                else:
                    pass_through(kind, off, n, off, 6 + n % 2)
                    n += 1
            for m in (N_FIRST - 2, N_FIRST - 1):
                pe.wait_ge(*first_free_of(m))
            pe.sem_inc(misc_free, (N_FIRST + 1) // 2)

            def turn(b, par, n, ahead, extra, behind=1):
                for kind, k, off in order(ahead, extra, behind):
                    base, pair, q0 = 64 * (k % 2), k // 2, 32 * (k % 4)
                    if kind == "score":
                        pe.wait_ge(max_done, (b + 1) * H + k)
                        if extra == "hist":
                            pe.wait_ge(hot_ready, b * H + k + 1)
                            for j in range(16):
                                q = 32 * (j % 4)
                                pe.matmul(ps[q:q + 32, 2, 384:384 + P], hot_tile[:, k % 2, :, j], hot_own[:, k % 2, 0:P, j],
                                          start=(j < 4), stop=(j >= 12))
                        elif extra == "owner6" and k == 0:
                            pe.matmul(ps[0:P, 2, 384:384 + NT], clampT[:, 0:P], fold[:, :], start=True, stop=True)
                        scores(b + 1, 1 - par, k)
                    elif kind == "exp":
                        pe.wait_ge(exp_done, b * H + k + 2)
                        if k in (0, H // 2):
                            pe.wait_ge(max1_in if k else max0_in, (b + 1) * (8 * H))
                        for t in range(KT):
                            mm = pe.matmul(ps[0:P, 3 + t, 0:L], kst[base:base + 64, par, pair, t * P:(t + 1) * P],
                                           qst[base:base + 64, par, pair, :], start=True, stop=True)
                        mm.then_inc(scoreT_full, 1)
                    elif kind in ("hist", "owner6", "owner7"):
                        pass
                    elif kind == "pv":
                        pe.wait_ge(exp_done, b * H + k + 3)
                        if k % 4 == 0:
                            pe.wait_ge(oT_ready, 2 * b + k // 4 + 1)
                        for t in range(KT):
                            mm = pe.matmul(ps[q0:q0 + 32, 6, 0:L], vv[0:P, par, t, 32 * k:32 * k + 32],
                                           probs[0:P, k % 2, t, :], start=(t == 0), stop=(t == KT - 1))
                        mm.then_inc(pv_done, 1)
                    else:
                        pass_through(kind, (par + off) % 2, n, b + off)
                        n = n + 1

            turns(pe, turn)

            def gat(q):
                pe.wait_ge(pairs_ready, q + 1)
                for j in range(KT):
                    i = q * KT + j
                    mm = pe.matmul(ps[0:P, 7, i * 2 * GF:(i + 1) * 2 * GF], pairs[:, q, j * P:(j + 1) * P], wgat[:, :],
                                   start=True, stop=True)
                mm.then_inc(gat_done, 1)

            pe.wait_ge(exp_done, B * H + 2)
            pe.wait_ge(misc_free, N_SHARED)
            for q in range(B // 2):
                pe.wait_ge(xn_ready, 2 * q + 3)
                turn_xn(q)
                if q:
                    gat(q - 1)
            gat(B // 2 - 1)
            pe.wait_ge(flags_ready, 1)
            pe.matmul(ps[0:1, 6, 0:128], flags[:, 3:4], eye[:, :], start=True, stop=True)
            pe.matmul(ps[0:1, 6, 128:256], own_list[0:P, LONG:LONG + 1], eye[0:P, :], start=True,
                      stop=True).then_inc(flags_done, 1)

            pe.sem_inc(y_full, EX)
            def hidden(b, e):
                pe.matmul(ps[:, e, 0:L], w1s[:, e, :], xT[:, bass.ds(b * L, L)], start=True, stop=True).then_inc(hid_full, 1)

            def outputs(b, e):
                pe.wait_ge(y_copied, b * EX + e + 1)
                for k in range(KT):
                    mm = pe.matmul(ps[0:P, 4 + e, k * D:(k + 1) * D], hid[:, e, k * P:(k + 1) * P], w2s[:, e, :],
                                   start=True, stop=True)
                mm.then_inc(y_full, 1)

            pe.wait_ge(xT_ready, 2 * B)
            pe.wait_ge(xT_ones_set, 1)
            for e in range(EX):
                hidden(0, e)
            pe.wait_ge(gat_read, 1)
            pe.wait_ge(over_ready, 1)
            with pe.Fori(0, B - 1) as b:
                for e in range(EX):
                    pe.wait_ge(hid_ready, b * EX + e + 1)
                    hidden(b + 1, e)
                    outputs(b, e)
            for e in range(EX):
                pe.wait_ge(hid_ready, (B - 1) * EX + e + 1)
                outputs(B - 1, e)
        @block.scalar
        def _(act):
            own = Own(act, act_own)
            for a, b_ in ((wstep[:, :], w_step), (win[:, :], w_in), (eye[:, :], c_eye)):
                act.dma_start(a, b_).then_inc(tok_in, 16)
            act.wait_ge(zeros_set, 1)
            act.dma_start(xaug[0:DIN, :, :], x.rearrange("b c l -> c b l")).then_inc(tok_in, 16)
            act.wait_ge(state_zeroed, 1)
            for b in range(B):
                act.wait_ge(tok_sum, b + 1)
                own.did(act.activation(add_in[:, b, :], ps[:, b, 0:L], ACT.Copy))
                act.wait_ge(act_own, b + 1)
                for p0, at in HALF_U:
                    act.activation(state[p0:p0 + 64, b, at:at + L], ps[p0:p0 + 64, b, 0:L], ACT.Relu).then_inc(tok_state, 1)
            with act.Fori(1, STEPS) as r:
                for b in range(B):
                    act.wait_ge(tok_sum, r * B + b + 1)
                    for p0, at in HALF_U:
                        act.activation(state[p0:p0 + 64, b, at:at + L], ps[p0:p0 + 64, b, 0:L], ACT.Relu).then_inc(tok_state, 1)
            act.wait_ge(mix_done, 1)
            for k in range(3):
                act.activation(h[0:P, 8 * k:8 * k + 8, :].rearrange("p t d -> p (t d)"), ps[0:P, k, :], ACT.Relu).then_inc(h_ready, 1)

            def deviations(n, first=0, end=NT):
                act.wait_ge(var_ready, n)
                act.activation(stat[0:P, 3, first:end], stat[0:P, 2, first:end], ACT.Sqrt).then_inc(std_ready, 1)

            def columns_in(n, q):
                act.wait_ge(xT_done, (n - 1) * (B // 2) + q + 1)
                if n == 2:
                    act.activation(pairs[:, q, :], ps[:, q, 0:L], ACT.Copy).then_inc(pairs_ready, 1)
                cols = xT[0:D, q * 2 * L:(q + 1) * 2 * L].rearrange("d (j w p) -> d j w p", j=KT, w=2)
                for w in range(2):
                    act.activation(cols[:, :, w, :], ps[64 * w:64 * w + 64, q, 0:L].rearrange("d (j p) -> d j p", j=KT),
                                   ACT.Copy).then_inc(xT_ready, 1)

            act.wait_ge(centred, 1)
            act.activation(sq[0:P, :, :], xn[0:P, :, :], ACT.Square).then_inc(squared, 1)
            deviations(1)
            columns_in(1, 0)

            def batch_in(b, par):
                act.activation(xb[0:D, par, :], xT[0:D, bass.ds(b * L, L)], ACT.Copy).then_inc(xb_ready, 1)

            def passed(kind, par, n, b, first=False, bank=7, free=misc_free):
                if kind == "qk":
                    act.wait_ge(misc_full, n + 1)
                    if not first:
                        act.wait_ge(parts_ready, b)
                    act.activation(qk32[:, :], ps[:, bank, 0:L], ACT.Copy, scale=qk_scale[:, 0:1])
                    act.activation(parts[:, 0, :], ps[:, bank, 0:L], ACT.Copy, scale=qk_scale[:, 0:1]).then_inc(free, 1)
                elif kind == "v":
                    act.wait_ge(misc_full, n + 1)
                    act.activation(vv[0:P, par, :, :].rearrange("p k (h c) -> p k h c", h=H)[:, :, :, 0:HD + 1],
                                   ps[0:P, bank, 0:KT * (HD + 1) * H].rearrange("p (k h c) -> p k h c", k=KT, h=H),
                                   ACT.Copy).then_inc(free, 1)
                elif kind in ("q0", "q1", "q2", "q3"):
                    act.wait_ge(misc_full, n + 1)
                    act.activation(qst[:, par, int(kind[1]), :], ps[:, bank, 0:L], ACT.Identity,
                                   bias=q_ones[:, 0:1]).then_inc(free, 1)
                elif kind == "onT":
                    act.wait_ge(misc_full, n + 1)
                    act.activation(onT[0:D, :], ps[0:D, bank, 0:L], ACT.Copy).then_inc(free, 1)

            act.wait_ge(xT_ready, 2)
            act.wait_ge(ones_set, 3)
            batch_in(0, 0)
            columns_in(1, 1)
            passed("qk", 0, 0, 0, first=True, bank=6, free=first_free_of(0)[0])
            for q in range(2, B // 2):
                columns_in(1, q)
            act.wait_ge(xT_ready, B)
            n = 1
            for kind, k, off in FIRST[1:]:
                if kind == "qk":
                    batch_in(off, off)
                if kind not in NOT_SHARED:
                    passed(kind, off, n, off, first=(off == 0), bank=6 + n % 2, free=first_free_of(n)[0])
                    n += 1

            def row_stats(b, piece):
                for k in range(KT):
                    t = bass.ds(b * KT + k, 1)
                    row, scrap = h[0:P, t, :], sq[0:P, k, :]
                    row = row.rearrange("p a d -> p (a d)")
                    if piece == 0:
                        act.activation(scrap, row, ACT.Copy, scale=-1.0 / D, accum_out=stat[0:P, 0, t]).then_inc(stats_ready, 1)
                    else:
                        act.activation(scrap, row, ACT.Square, bias=stat[0:P, 0, t], accum_out=sums[0:P, t]).then_inc(stats_ready, 1)

            def turn(b, par, n, ahead, extra, behind=1):
                for kind, k, off in order(ahead, extra, behind):
                    if behind and kind == "pv" and k in (5, 6):
                        if k == 5:
                            act.wait_ge(rows_added, b)
                        else:
                            act.wait_ge(stats_ready, (b - 1) * (2 * KT) + KT)
                        row_stats(b - 1, k - 5)
                    if kind == "exp":
                        if k == 0 and ahead == 2:
                            batch_in(b + 2, par)
                        act.wait_ge(scoreT_full, b * H + k + 1)
                        act.wait_ge(pv_done, b * H + k + 1)
                        act.activation(probs[0:P, k % 2, :, :], ps[0:P, 3:6, 0:L], ACT.Exp).then_inc(exp_done, 1)
                    elif kind == "pv":
                        if k % 4 == 3:
                            act.wait_ge(pv_done, b * H + k + 3)
                            act.activation(oT[:, k // 4, :], ps[:, 6, 0:L], ACT.Copy).then_inc(oT_ready, 1)
                        if not ahead and k == H - 1:
                            deviations(2, 0, SOON * KT)
                    elif kind not in NOT_SHARED:
                        passed(kind, (par + off) % 2, n, b + off)
                        n = n + 1

            act.sem_inc(exp_done, 2)
            act.sem_inc(pv_done, 2)
            act.sem_inc(oT_ready, 1)
            turns(act, turn)
            act.wait_ge(rows_added, B)
            row_stats(B - 1, 0)
            act.wait_ge(stats_ready, (B - 1) * (2 * KT) + KT)
            row_stats(B - 1, 1)
            columns_in(2, 0)
            deviations(3, SOON * KT, NT)
            for q in range(1, B // 2):
                columns_in(2, q)

            def hidden(b):
                for e in range(EX):
                    act.wait_ge(hid_full, b * EX + e + 1)
                    act.wait_ge(y_full, b * EX + e + 1)
                    act.activation(hid[:, e, :], ps[:, e, 0:L], ACT.Gelu).then_inc(hid_ready, 1)

            with act.Fori(0, EARLY) as b:
                hidden(b)

            def exponentials(n, out_, in_):
                act.wait_ge(exp_in, n)
                act.activation(out_, in_, ACT.Exp).then_inc(exp_out, 1)

            exponentials(1, expo[0:P, :, 0:SPLIT, :], expo[0:P, :, 0:SPLIT, :])
            exponentials(2, expo[0:P, :, SPLIT:CAP, :], expo[0:P, :, SPLIT:CAP, :])
            with act.Fori(EARLY, B) as b:
                hidden(b)

            def group_exponentials(i):
                take(act, g_exp_in, 1)
                act.activation(expo[0:P, :, :, :], expo[0:P, :, :, :], ACT.Exp).then_inc(g_exp_out, 1)
                take(act, g_exp_in, 1)
                act.activation(wts[0:P, 0:2, :, :], wts[0:P, 0:2, :, :], ACT.Exp).then_inc(g_exp_out, 1)

            if_lists_overflowed(act, group_exponentials)
            exponentials(3, wts[0:P, :, :, :], wts[0:P, :, :, :])
            deviations(4)
            exponentials(4, gate[0:P, :, :], gate[0:P, :, :])
            act.wait_ge(gates_ready, 1)
            for t in range(NT):
                act.activation(yexp[0:P, t, 2, :], yexp[0:P, t, 2, :], ACT.Copy, scale=gate[0:P, t, 2:3]).then_inc(act_weighed, 1)

        @block.vector
        def _(v):
            own = Own(v, vec)
            did, settle = own.did, own.settle

            v.memset(state[:, :, :], 0.0).then_inc(state_zeroed, 1)
            did(v.memset(flags[:, :], 0.0))
            did(v.memset(biasT[:, :], 1.0))
            did(v.memset(clampT[:, :], 0.0))
            did(v.memset(own_h[:, KEPT:KEPT + 32], 0.0))
            did(v.memset(tile_h[:, KEPT:KEPT + 32], 0.0))

            v.wait_ge(tgt_in, 48)
            did(v.scalar_tensor_tensor(out=tgt_key, in0=tgt_i[:, :], scalar=float(JA), in1=iota[:, 1:JA + 1],
                                       op0=ALU.mult, op1=ALU.add))
            settle()
            did(v.scalar_tensor_tensor(out=tgt_key, in0=tgt_i[:, :], scalar=float(L), in1=tgt_key,
                                       op0=ALU.is_lt, op1=ALU.mult))
            settle()
            for c in range(0, JA, 8):
                did(v.max(tgt_list[:, c:c + 8], tgt_key))
                settle()
                did(v.match_replace(tgt_key, tgt_list[:, c:c + 8], tgt_key, -1.0))
                settle()
            v.sem_inc(tgt_listed, 1)
            did(v.tensor_scalar(tgt_no, tgt_list, -1.0, 0.0, ALU.add, ALU.max))
            did(v.tensor_scalar(tgt[:, :], part[:, :].to_broadcast([128, JA]), float(JA) / RANKS, 1.0, ALU.mult, ALU.add))
            settle()
            did(v.tensor_scalar(tgt_j, tgt_no, JA - 1, None, ALU.bitwise_and))
            settle()
            did(v.tensor_tensor(tgt_val, tgt[:, :], tgt_j, ALU.add))
            did(v.tensor_tensor(tgt_slot, tgt_no, tgt_j, ALU.subtract))
            settle()
            did(v.tensor_tensor(tgt_new[:, 1:JA], tgt_slot[:, 1:JA], tgt_slot[:, 0:JA - 1], ALU.not_equal))
            did(v.memset(tgt_new[:, 0:1], 1.0))
            settle()
            did(v.scalar_tensor_tensor(out=tgt_new, in0=tgt_list, scalar=0.0, in1=tgt_new, op0=ALU.is_gt, op1=ALU.mult))
            did(v.tensor_scalar(own_row[:, :], part[:, :], 1.0 / RANKS, -NO_SLOT, ALU.mult, ALU.add))
            settle()
            did(v.scalar_tensor_tensor(out=tgt_slot, in0=tgt_slot, scalar=own_row[:, 0:1], in1=tgt_new,
                                       op0=ALU.add, op1=ALU.mult))
            settle()
            v.tensor_scalar(tgt_slot_i, tgt_slot, NO_SLOT, None, ALU.add).then_inc(tgt_slots_ready, 1)
            v.wait_ge(edges_in, 32)

            def edge_keys(src, dst, key, own_tile, tile, source, tmp):
                did(v.tensor_scalar(tmp, dst, 1.0 / P, 0.504 - 1.0, ALU.mult, ALU.add))
                did(v.tensor_scalar(source, src, float(LAST), 1.0, ALU.min, ALU.add))
                settle()
                did(v.tensor_scalar(tile, tmp, MAGIC, -MAGIC, ALU.add, ALU.add))
                settle()
                did(v.tensor_scalar(tmp, tile, float(2 ** TILE_BITS * P - 1), None, ALU.mult))
                settle()
                did(v.scalar_tensor_tensor(out=own_tile, in0=dst, scalar=float(2 ** TILE_BITS), in1=tmp,
                                           op0=ALU.mult, op1=ALU.subtract))
                settle()
                did(v.scalar_tensor_tensor(out=key, in0=own_tile, scalar=float(2 ** SRC_BITS), in1=source,
                                           op0=ALU.mult, op1=ALU.add))
                settle()
                did(v.scalar_tensor_tensor(out=key, in0=dst, scalar=float(M), in1=key, op0=ALU.is_lt, op1=ALU.mult))

            edge_keys(src_i, dst_i, f_key, f_own, f_tile, f_real, f_tmp)
            v.wait_ge(more_in, 16)
            v.tensor_reduce(more_top[0:1, 0:1], more_row[0:1, :], AX, ALU.max).then_inc(more_own, 1)
            v.wait_ge(more_own, 1)
            v.tensor_scalar(more_i[:, :], more_top[:, :], 0.0, None, ALU.is_gt).then_inc(more_ready, 1)
            settle()

            for r in range(KEEP // 8):
                best = [kept[:, 8 * (NPART * r + g):8 * (NPART * r + g + 1)] for g in range(NPART)]
                groups = [f_key[:, g * PART:(g + 1) * PART] for g in range(NPART)]
                for g in range(NPART):
                    did(v.max(best[g], groups[g]))
                settle()
                for g in range(NPART):
                    did(v.match_replace(groups[g], best[g], groups[g], -1.0))
                settle()
            did(v.tensor_reduce(flags[:, 4:5], f_key, AX, ALU.max))
            did(v.tensor_scalar(kept_i, kept, 0.0, None, ALU.max))
            settle()
            did(v.tensor_scalar(low_i, kept_i, 2 ** SRC_BITS - 1, None, ALU.bitwise_and))
            settle()
            did(v.scalar_tensor_tensor(out=kept_real, in0=low_i, scalar=float(LAST + 1), in1=kept,
                                       op0=ALU.is_lt, op1=ALU.mult))
            did(v.tensor_scalar(no_count, low_i, float(LAST + 1), 200.0, ALU.is_lt, ALU.mult))
            settle()

            for c in range(0, CAP, 8):
                did(v.max(lane_list[:, c:c + 8], kept_real))
                settle()
                did(v.match_replace(kept_real, lane_list[:, c:c + 8], kept_real, -1.0))
                settle()
            v.wait_ge(last_in, 16)
            did(v.tensor_reduce(lastf[0:P, 0, :], last[0:P, :, :], AX, ALU.max))
            settle()
            did(v.tensor_scalar(lastf[0:P, 1, :], lastf[0:P, 0, :], 0.0, None, ALU.is_gt))
            v.tensor_scalar(last_i[0:P, :], lastf[0:P, 0, :], -1.0, 0.0, ALU.add, ALU.max).then_inc(last_ready, 1)
            did(v.tensor_reduce(flags[:, 0:1], kept_real, AX, ALU.max))
            did(v.tensor_scalar(lane_list[:, :], lane_list[:, :], 0.0, None, ALU.max))
            settle()
            did(v.tensor_copy(lane_int[:, :], lane_list[:, :]))
            settle()
            did(v.tensor_scalar(own_tmp_i[:, 0, :], lane_int[:, :], SRC_BITS + TILE_BITS, None, ALU.logical_shift_right))
            settle()
            lane_own, same, rank, slot = (lane_tmp[:, k, :] for k in range(4))
            did(v.tensor_copy(lane_own, own_tmp_i[:, 0, :]))
            did(v.memset(same[:, 0:1], 0.0))
            settle()
            did(v.tensor_tensor(same[:, 1:CAP], lane_own[:, 1:CAP], lane_own[:, 0:CAP - 1], ALU.is_equal))
            settle()
            did(v.tensor_tensor_scan(rank, same, same, 0.0, ALU.mult, ALU.add))
            settle()
            did(v.scalar_tensor_tensor(out=slot, in0=lane_own, scalar=float(SLOTS), in1=rank, op0=ALU.mult, op1=ALU.add))
            did(v.tensor_scalar(same, rank, float(RANKS), None, ALU.is_lt))
            settle()
            v.wait_ge(consts_in, 16 * N_CONSTS)
            did(v.tensor_scalar(slot, slot, part[:, 0:1], -SKIP, ALU.add, ALU.add))
            did(v.scalar_tensor_tensor(out=same, in0=lane_list[:, :], scalar=0.0, in1=same, op0=ALU.is_gt, op1=ALU.mult))
            did(v.tensor_scalar(lane_own, rank, float(RANKS), None, ALU.is_ge))
            settle()
            did(v.tensor_tensor(slot, slot, same, ALU.mult))
            did(v.scalar_tensor_tensor(out=lane_own, in0=lane_list[:, :], scalar=0.0, in1=lane_own, op0=ALU.is_gt, op1=ALU.mult))
            settle()
            did(v.tensor_reduce(flags[:, 1:2], lane_own, AX, ALU.max))
            settle()
            did(v.tensor_tensor(flags[:, 4:5], flags[:, 4:5], flags[:, 1:2], ALU.max))
            v.tensor_scalar(slot_i[:, :], slot, SKIP, None, ALU.add).then_inc(slots_ready, 1)

            did(v.tensor_scalar(code_i, kept_i, SRC_BITS, 2 ** TILE_BITS - 1, ALU.logical_shift_right, ALU.bitwise_and))
            settle()
            did(v.tensor_tensor(tile_h[:, 0:KEPT], no_count, code_i, ALU.add))
            settle()
            did(v.tensor_scalar(code_i, kept_i, SRC_BITS + TILE_BITS, None, ALU.logical_shift_right))
            settle()
            did(v.tensor_copy(own_h[:, 0:KEPT], code_i))
            settle()

            def hot_block(i, par):
                v.tensor_tensor(hot_own[:, par, 0:P, :], bc(own_h[:, bass.ds(i * 16, 16)], 1, [128, P, 16]),
                                hot[:, 0:P, :], ALU.is_equal)
                v.tensor_tensor(hot_tile[:, par, :, :], bc(tile_h[:, bass.ds(i * 16, 16)], 1, [128, 32, 16]),
                                hot[:, 0:32, :], ALU.is_equal).then_inc(hot_ready, 1)


            v.wait_ge(attr_in, 16 * KT)
            v.wait_ge(weights_in, 16 * N_WEIGHTS)
            for k in range(KT):
                for i in range(3):
                    did(v.scalar_tensor_tensor(out=bias[0:P, k, :], in0=we[0:P, i, :], scalar=attr[0:P, k, i:i + 1],
                                               in1=we[0:P, 3, :] if i == 0 else bias[0:P, k, :],
                                               op0=ALU.mult, op1=ALU.add))
                    settle()
                did(v.tensor_scalar(bias[0:P, k, :], bias[0:P, k, :], lastf[0:P, 1, k:k + 1], None, ALU.mult))
            settle()

            def three_parts(out_parts, value, left, last_sem):
                did(v.tensor_copy(out_parts(0), value))
                settle()
                did(v.tensor_tensor(left, value, out_parts(0), ALU.subtract))
                settle()
                did(v.tensor_copy(out_parts(1), left))
                settle()
                v.tensor_tensor(out_parts(2), left, out_parts(1), ALU.subtract).then_inc(last_sem, 1)

            three_parts(lambda c: bparts[0:P, :, :, c], bias[0:P, :, :], nrest[0:P, :, :], bparts_ready)

            def normalise(n, x_, c_, width, mean_row, roots):
                r3 = [P, NT, width]
                did(v.tensor_reduce(stat[0:P, 0, :], x_, AX, ALU.add))
                settle()
                did(v.tensor_scalar(stat[0:P, 1, :], stat[0:P, 0, :], 1.0 / width, None, ALU.mult))
                settle()
                v.tensor_tensor(c_, x_, bc(stat[0:P, 1, :], 2, r3), ALU.subtract).then_inc(centred, 1)
                if n == 1:
                    v.wait_ge(biasT_done, 1)
                    v.tensor_copy(biasT[0:3 * H, :], ps[0:3 * H, 3, 0:L]).then_inc(biasT_ready, 1)
                    v.wait_ge(squared, 1)
                else:
                    v.wait_ge(centred, 2)
                    did(v.tensor_tensor(mean_row, c_, c_, ALU.mult))
                    settle()
                did(v.tensor_reduce(stat[0:P, 0, :], mean_row, AX, ALU.add))
                settle()
                v.tensor_scalar(stat[0:P, 2, :], stat[0:P, 0, :], 1.0 / width, EPS, ALU.mult, ALU.add).then_inc(var_ready, 1)
                v.wait_ge(std_ready, roots)
                did(v.reciprocal(stat[0:P, 1, :], stat[0:P, 3, :]))
                settle()
                ins = v.tensor_tensor(c_, c_, bc(stat[0:P, 1, :], 2, r3), ALU.mult)
                return ins

            v.wait_ge(h_ready, 3)
            normalise(1, h[0:P, :, :], xn[0:P, :, :], D, sq[0:P, :, :], 1).then_inc(xn_ready, 1)
            v.wait_ge(kbias_done, 1)
            v.tensor_copy(kbias[:, :, :], ps[:, 2:6, 0:L]).then_inc(kbias_ready, 1)


            quarter = SLOTS // OWN_PARTS
            quarters = [own_tab[0:P, q * quarter:(q + 1) * quarter] for q in range(OWN_PARTS)]
            own_some = lane_tmp[:, :, :].rearrange("p a b -> p (a b)")[0:P, 0:OWN_PARTS * OWN_KEEP]

            def quarter_round(r):
                best = [own_some[:, q * OWN_KEEP + 8 * r:q * OWN_KEEP + 8 * r + 8] for q in range(OWN_PARTS)]
                for q in range(OWN_PARTS):
                    did(v.max(best[q], quarters[q]))
                settle()
                for q in range(OWN_PARTS):
                    did(v.match_replace(quarters[q], best[q], quarters[q], -1.0))
                settle()

            def owner_round(c):
                did(v.max(own_list[0:P, c:c + 8], own_some))
                settle()
                did(v.match_replace(own_some, own_list[0:P, c:c + 8], own_some, -1.0))
                settle()

            def decode(ready):
                did(v.tensor_scalar(own_list[0:P, :], own_list[0:P, :], 0.0, None, ALU.max))
                settle()
                did(v.tensor_copy(own_int[0:P, :], own_list[0:P, :]))
                did(v.tensor_scalar(keep[0:P, :], own_list[0:P, :], 0.0, None, ALU.is_le))
                settle()
                did(v.tensor_scalar(own_tmp_i[0:P, 0, :], own_int[0:P, :], SRC_BITS, 2 ** TILE_BITS - 1,
                                    ALU.logical_shift_right, ALU.bitwise_and))
                did(v.tensor_scalar(own_tmp_i[0:P, 1, :], own_int[0:P, :], 2 ** SRC_BITS - 1, None, ALU.bitwise_and))
                settle()
                did(v.scalar_tensor_tensor(out=seg[0:P, :], in0=keep[0:P, :], scalar=-64.0, in1=own_tmp_i[0:P, 0, :],
                                           op0=ALU.mult, op1=ALU.add))
                did(v.tensor_scalar(src_idx[0:P, :], own_tmp_i[0:P, 1, :], -1.0, 0.0, ALU.add, ALU.max))
                settle()
                yield
                did(v.memset(keep[0:P, 0:1], 0.0))
                did(v.tensor_tensor(keep[0:P, 1:CAP], seg[0:P, 1:CAP], seg[0:P, 0:CAP - 1], ALU.is_equal))
                did(v.tensor_tensor(member[0:P, :, :], bc(seg[0:P, :], 2, [P, CAP, NT]),
                                    bc(iota[0:P, 0:NT], 1, [P, CAP, NT]), ALU.is_equal))
                yield
                did(v.tensor_tensor(at_least[0:P, :, :], bc(seg[0:P, :], 1, [P, NT, CAP]),
                                    bc(iota[0:P, 0:NT], 2, [P, NT, CAP]), ALU.is_ge))
                settle()
                yield
                did(v.tensor_scalar(keep[0:P, :], keep[0:P, :], -1.0, -NEG, ALU.add, ALU.mult))
                did(v.tensor_reduce(endf[0:P, 0, :], at_least[0:P, :, :], AX, ALU.add))
                did(v.tensor_scalar(own_row[0:P, :], part[0:P, :], float(CAP) / RANKS, None, ALU.mult))
                settle()
                did(v.tensor_tensor(has_real[0:P, 0:NT - 1], endf[0:P, 0, 0:NT - 1], endf[0:P, 0, 1:NT], ALU.is_gt))
                did(v.tensor_scalar(has_real[0:P, NT - 1:NT], endf[0:P, 0, NT - 1:NT], 0.0, None, ALU.is_gt))
                did(v.tensor_scalar(endf[0:P, 1, :], endf[0:P, 0, :], -1.0, 0.0, ALU.add, ALU.max))
                settle()
                yield
                v.tensor_scalar(end_idx[0:P, :], endf[0:P, 1, :], own_row[0:P, 0:1], None, ALU.add).then_inc(ready, 1)

            def owner_steps():
                v.wait_ge(table_in, 16)
                for r in range(OWN_KEEP // 8):
                    quarter_round(r)
                    yield
                did(v.tensor_reduce(flags[0:P, 1:2], own_tab[0:P, :], AX, ALU.max))
                for c in range(0, CAP, 8):
                    owner_round(c)
                    if c % 40 == 32:
                        yield
                did(v.tensor_reduce(flags[0:P, 2:3], own_some, AX, ALU.max))
                settle()
                did(v.tensor_reduce(flags[:, 3:4], flags[:, 0:3], AX, ALU.max))
                settle()
                did(v.tensor_tensor(flags[:, 3:4], flags[:, 3:4], flags[:, 4:5], ALU.max))
                settle()
                yield
                yield from decode(lists_ready)
                v.wait_ge(lists_ready, 1)
                did(v.tensor_scalar(flags[0:P, 1:2], endf[0:P, 0, UPPER:UPPER + 1], float(SPLIT), None, ALU.is_gt))
                did(v.tensor_scalar(own_row[0:P, :], part[0:P, :], float(SPLIT) / RANKS, None, ALU.mult))
                settle()
                did(v.tensor_tensor(flags[0:P, 3:4], flags[0:P, 3:4], flags[0:P, 1:2], ALU.max))
                did(v.tensor_scalar(upper_idx[0:P, :], endf[0:P, 1, :], float(SPLIT - 1), own_row[0:P, 0:1], ALU.min, ALU.add))
                settle()
                v.sem_inc(flags_ready, 1)

            owner_work = owner_steps()

            def make_parts(b, written):
                v.wait_ge(*written)
                v.tensor_tensor(rest[:, :], qk32[:, :], parts[:, 0, :], ALU.subtract).then_inc(cut, 1)
                v.wait_ge(cut, 2 * b + 1)
                v.tensor_copy(parts[:, 1, :], rest[:, :]).then_inc(cut, 1)
                v.wait_ge(cut, 2 * b + 2)
                v.tensor_tensor(parts[:, 2, :], rest[:, :], parts[:, 1, :], ALU.subtract).then_inc(parts_ready, 1)

            def passed(kind, par, n, b, bank=7, free=misc_free):
                if kind == "qk":
                    make_parts(b, first_free_of(n) if isinstance(n, int) and n < N_FIRST else (misc_free, n + 1))
                elif kind in ("k0", "k1", "k2", "k3"):
                    v.wait_ge(misc_full, n + 1)
                    v.tensor_tensor(kst[:, par, int(kind[1]), :], ps[:, bank, 0:L], kbias[:, int(kind[1]), :],
                                    ALU.add).then_inc(free, 1)
                elif kind in ("max0", "max1"):
                    g = int(kind[3])
                    v.wait_ge(max_done, b * H + 4 * g + 4)
                    high, low = (nparts[0:P, g, :, :, :, c] for c in range(MAX_PARTS))
                    top = negmax[0:P, :, 4 * g:4 * g + 4].rearrange("p k (r w) -> p k w r", w=2)
                    v.tensor_copy(high, top).then_inc(ncut, 1)
                    v.wait_ge(ncut, 2 * b + g + 1)
                    v.tensor_tensor(low, top, high, ALU.subtract).then_inc(negmax_ready, 1)
                    v.wait_ge(misc_full, n + 1)
                    v.tensor_copy(maxT[:, g, :], ps[0:MAX_PARTS * H // 2, bank, 0:L]).then_inc(maxT_ready, 1)
                    v.wait_ge(maxT_ready, 2 * b + g + 1)
                    v.sem_inc(free, 1)
                elif kind in ("norm0", "norm1"):
                    g = int(kind[4])
                    v.wait_ge(misc_full, n + 1)
                    turned = ps[0:P, bank, 0:KT * 128].rearrange("p (k q c) -> p k q c", k=KT, q=4)
                    v.reciprocal(rden[0:P, :, :], turned[:, :, :, HD]).then_inc(rden_ready, 1)
                    v.wait_ge(rden_ready, 2 * b + g + 1)
                    v.tensor_tensor(on[0:P, :, g * 32:(g + 1) * 32].rearrange("p k (q d) -> p k q d", q=4),
                                    turned[:, :, :, 0:HD], bc(rden[0:P, :, :], 3, [P, KT, 4, HD]),
                                    ALU.mult).then_inc(free, 1)
                elif kind == "out":
                    v.wait_ge(misc_full, n + 1)
                    rows = h[0:P, bass.ds(b * KT, KT), :]
                    v.tensor_tensor(rows, ps[0:P, bank, 0:KT * D].rearrange("p (k d) -> p k d", k=KT), rows,
                                    ALU.add).then_inc(rows_added, 1)
                    v.wait_ge(rows_added, b + 1)
                    v.sem_inc(free, 1)

            def maxima(c, k):
                v.wait_ge(score_full, c * H + k + 1)
                v.tensor_reduce(negmax[0:P, :, k], ps[0:P, 0:3, 0:L], AX, ALU.max, negate=True).then_inc(max_done, 1)

            n = 0
            for kind, k, off in FIRST:
                if kind == "score":
                    maxima(0, k)
                else:
                    passed(kind, off, n, off, 6 + n % 2, first_free_of(n)[0])
                    n += 1
                if (kind, off) == ("qk", 0):
                    hot_block(0, 0)
                    hot_block(1, 1)

            def variances(first, end):
                t = slice(first * KT, end * KT)
                v.wait_ge(stats_ready, 2 * KT * end)
                v.tensor_scalar(stat[0:P, 2, t], sums[0:P, t], 1.0 / D, EPS, ALU.mult, ALU.add).then_inc(var_ready, 1)

            def normalise_again(first, end, n):
                v.wait_ge(std_ready, n)
                did(v.reciprocal(stat[0:P, 1, first * KT:end * KT], stat[0:P, 3, first * KT:end * KT]))
                settle()
                for t in range(first * KT, end * KT):
                    ins = v.tensor_scalar(xn[0:P, t, :], h[0:P, t, :], stat[0:P, 0, t:t + 1], stat[0:P, 1, t:t + 1],
                                          ALU.add, ALU.mult)
                    if t % KT == KT - 1:
                        ins.then_inc(xn_ready, 1)

            def turn(b, par, n, ahead, extra, behind=1):
                for kind, k, off in order(ahead, extra, behind):
                    if kind == "score":
                        v.wait_ge(score_full, (b + 1) * H + k + 1)
                        if extra == "hist":
                            v.tensor_tensor(clampT[:, 0:P], ps[:, 2, 384:384 + P], clampT[:, 0:P], ALU.add).then_inc(hist_added, 1)
                        elif extra == "owner6" and k == 0:
                            did(v.tensor_copy(clamped[0:P, :], ps[0:P, 2, 384:384 + NT]))
                        maxima(b + 1, k)
                        if extra == "hist":
                            v.wait_ge(hist_added, b * H + k + 1)
                    elif kind == "hist":
                        hot_block(b * H + k + 2, k % 2)
                    elif kind == "owner6":
                        next(owner_work, None)
                    elif kind == "owner7":
                        next(owner_work, None)
                    elif kind == "pv":
                        if not ahead and k == H - 1:
                            variances(0, SOON)
                    elif kind not in NOT_SHARED:
                        passed(kind, (par + off) % 2, n, b + off)
                        n = n + 1
                        if not ahead and (kind, off) == ("norm1", 0):
                            normalise_again(0, SOON, 2)

            turns(v, turn)
            v.wait_ge(misc_free, N_SHARED)
            variances(SOON, B)
            normalise_again(SOON, B, 3)

            v.wait_ge(gat_done, B // 2)
            hg = ps[0:P, 7, 0:NT * GF].rearrange("p (t f) -> p t f", t=NT)
            r16 = [P, NT, GF]

            def by_head(ap):
                return ap.rearrange("p t (h e) -> p t h e", h=GH)

            did(v.tensor_tensor(gprod[0:P, :, :], hg, bc(vecs[0:P, 0, :], 1, r16), ALU.mult))
            did(v.tensor_copy(tab[0:P, :, 0:GF], hg))
            settle()
            did(v.tensor_reduce(tab[0:P, :, GF:GF + GH], by_head(gprod[0:P, :, :]), AX, ALU.add))
            settle()
            v.sem_inc(tab_ready, 1)
            v.tensor_tensor(gprod[0:P, :, :], hg, bc(vecs[0:P, 1, :], 1, r16), ALU.mult).then_inc(gat_read, 1)
            v.wait_ge(flags_done, 1)
            v.tensor_reduce(flag_row[0:1, :], ps[0:1, 6, 0:256].rearrange("p (a l) -> p a l", a=2), AX, ALU.max).then_inc(over_own, 1)
            v.wait_ge(over_own, 1)
            v.tensor_scalar(over_i[:, :], flag_row[0:1, :], 0.0, None, ALU.is_gt).then_inc(over_ready, 1)
            v.wait_ge(gat_read, 1)
            did(v.tensor_reduce(adst[0:P, :, :], by_head(gprod[0:P, :, :]), AX, ALU.add))
            settle()
            wide3 = wide[0:P, :].rearrange("p (c t) -> p c t", t=NT)

            def target_score(g):
                did(v.tensor_tensor(wide3, member[0:P, :, :], bc(adst[0:P, :, g], 1, [P, CAP, NT]), ALU.mult))
                settle()
                did(v.tensor_reduce(adst_e[0:P, :, g], wide3, AX, ALU.add))
                settle()

            def expert_outputs(b):
                for e in range(EX):
                    v.wait_ge(y_full, b * EX + e + EX + 1)
                    v.tensor_tensor(yexp[0:P, bass.ds(b * KT, KT), e, :],
                                    ps[0:P, 4 + e, 0:KT * D].rearrange("p (k d) -> p k d", k=KT),
                                    bc(b2s[0:P, e, :], 1, [P, KT, D]), ALU.add).then_inc(y_copied, 1)

            v.sem_inc(y_copied, EX)
            for g in range(GH):
                expert_outputs(g)
                target_score(g)
            with v.Fori(GH, EARLY) as b:
                expert_outputs(b)

            def differences(first, end):
                v.wait_ge(y_copied, end * EX + EX)
                t = slice(first * KT, end * KT)
                for e in range(1, EX):
                    did(v.tensor_tensor(yexp[0:P, t, e, :], yexp[0:P, t, e, :], yexp[0:P, t, 0, :], ALU.subtract))
                did(v.tensor_tensor(h[0:P, t, :], h[0:P, t, :], yexp[0:P, t, 0, :], ALU.add))

            differences(0, EARLY)

            v.wait_ge(lastrow_in, 16)
            r4 = [P, NT, GH]
            e_self, e_clamp, e_real, mask = (s[0:P, :, :] for s in (s1, s2, s3, s4))
            did(v.tensor_tensor(e_self, tab[0:P, :, GF:GF + GH], adst[0:P, :, :], ALU.add))
            settle()
            did(v.scalar_tensor_tensor(out=e_self, in0=e_self, scalar=0.2, in1=e_self, op0=ALU.mult, op1=ALU.max))

            def clamped_scores():
                did(v.tensor_tensor(e_clamp, adst[0:P, :, :], bc(lastrow[0:P, GF:GF + GH], 1, r4), ALU.add))
                did(v.tensor_scalar(endf[0:P, 0, :], clamped[0:P, :], 0.0, None, ALU.is_gt))
                settle()
                did(v.scalar_tensor_tensor(out=e_clamp, in0=e_clamp, scalar=0.2, in1=e_clamp, op0=ALU.mult, op1=ALU.max))
                did(v.tensor_scalar(endf[0:P, 0, :], endf[0:P, 0, :], -1.0, -NEG, ALU.add, ALU.mult))
                settle()
                did(v.tensor_tensor(e_clamp, e_clamp, bc(endf[0:P, 0, :], 2, r4), ALU.add))
                settle()
                did(v.tensor_tensor(mask, e_self, e_clamp, ALU.max))

            clamped_scores()

            def edge_sums(c0, c1, ask_exp):
                n, c = c1 - c0, slice(c0, c1)
                d0 = max(c0, 1)
                d, before = slice(d0, c1), slice(d0 - 1, c1 - 1)

                def so_far(ap, start):
                    return ap[:, c0 - 1:c0] if c0 else start

                did(v.tensor_tensor(score[0:P, c, :], got[0:P, c, GF:GF + GH], adst_e[0:P, c, :], ALU.add))
                if c0 == 0:
                    did(v.memset(expo[0:P, 0, 0:1, :], NEG))
                settle()
                did(v.scalar_tensor_tensor(out=score[0:P, c, :], in0=score[0:P, c, :], scalar=0.2, in1=score[0:P, c, :],
                                           op0=ALU.mult, op1=ALU.max))
                settle()
                for g in range(GH):
                    did(v.tensor_tensor_scan(run_max[0:P, c, g], keep[0:P, c], score[0:P, c, g],
                                             so_far(run_max[0:P, :, g], NEG), ALU.add, ALU.max))
                settle()
                did(v.tensor_tensor(expo[0:P, 0, d, :], run_max[0:P, before, :], run_max[0:P, d, :], ALU.subtract))
                did(v.tensor_tensor(expo[0:P, 1, c, :], score[0:P, c, :], run_max[0:P, c, :], ALU.subtract))
                did(v.tensor_copy(res[0:P, c, 0:GH], run_max[0:P, c, :]))
                settle()
                did(v.tensor_tensor(expo[0:P, 0, d, :], expo[0:P, 0, d, :], bc(keep[0:P, d], 2, [P, c1 - d0, GH]),
                                    ALU.add))
                settle()
                ask_exp()
                decay, weight = expo[0:P, 0, c, :], expo[0:P, 1, c, :]
                did(v.tensor_tensor(by_head(msg[0:P, c, :]), by_head(got[0:P, c, 0:GF]), bc(weight, 3, [P, n, GH, EX]), ALU.mult))
                for g in range(GH):
                    did(v.tensor_tensor_scan(res[0:P, c, GH + g], decay[:, :, g], weight[:, :, g],
                                             so_far(res[0:P, :, GH + g], 0.0), ALU.mult, ALU.add))
                settle()
                for f in range(GF):
                    did(v.tensor_tensor_scan(res[0:P, c, 2 * GH + f], decay[:, :, f // EX], msg[0:P, c, f],
                                             so_far(res[0:P, :, 2 * GH + f], 0.0), ALU.mult, ALU.add))
                settle()

            def ask_exp(n):
                v.sem_inc(exp_in, 1)
                v.wait_ge(exp_out, n)

            v.wait_ge(gathered, 16 * SPLIT)
            edge_sums(0, SPLIT, lambda: ask_exp(1))
            v.sem_inc(res_ready, 1)
            v.wait_ge(gathered_late, 16 * (LONG - SPLIT))
            v.wait_ge(long_gathered, 1)
            edge_sums(SPLIT, CAP, lambda: ask_exp(2))
            v.sem_inc(res_ready, 1)
            with v.Fori(EARLY, B) as b:
                expert_outputs(b)
            differences(EARLY, B)
            v.wait_ge(ends_in, 16 * NT)
            settle()

            def ask_group_exp():
                settle()
                v.sem_inc(g_exp_in, 1)
                take(v, g_exp_out, 1)

            r4 = [P, NT, GH]

            def group_sums(i):
                v.sem_clear(vec)
                own.n = 0
                v.sem_inc(g_next, 1)
                take(v, g_raw_in, 32)
                raw = [lane_tmp[0:P, k, 0:GROUP] for k in range(4)]
                key, tmp = own_tab[0:P, 0:GROUP], own_tab[0:P, GROUP:2 * GROUP]
                edge_keys(raw_i[0:P, 0, :], raw_i[0:P, 1, :], key, raw[0], raw[1], raw[2], tmp)
                settle()
                did(v.scalar_tensor_tensor(out=tmp, in0=raw_i[0:P, 0, :], scalar=float(LAST), in1=key,
                                           op0=ALU.is_ge, op1=ALU.mult))
                settle()
                did(v.tensor_tensor(key, key, tmp, ALU.subtract))
                did(v.scalar_tensor_tensor(out=raw[0], in0=raw[1], scalar=-float(P), in1=raw_i[0:P, 1, :],
                                           op0=ALU.mult, op1=ALU.add))
                did(v.tensor_scalar(own_row[0:P, :], part[0:P, :], 1.0 / RANKS, None, ALU.mult))
                settle()
                did(v.scalar_tensor_tensor(out=key, in0=raw[0], scalar=own_row[0:P, 0:1], in1=key,
                                           op0=ALU.is_equal, op1=ALU.mult))
                did(v.scalar_tensor_tensor(out=tmp, in0=raw[0], scalar=own_row[0:P, 0:1], in1=tmp,
                                           op0=ALU.is_equal, op1=ALU.mult))
                did(v.memset(own_list[0:P, :], 0.0))
                settle()
                did(v.tensor_scalar(tmp, tmp, 0.0, None, ALU.is_gt))
                did(v.tensor_scalar(raw[1], raw[1], 1.0, None, ALU.add))
                settle()
                did(v.tensor_tensor(tmp, tmp, raw[1], ALU.mult))
                settle()
                hits = wide[0:P, 0:NT * GROUP].rearrange("p (t c) -> p t c", t=NT)
                did(v.tensor_tensor(hits, bc(tmp, 1, [P, NT, GROUP]), bc(iota[0:P, 1:NT + 1], 2, [P, NT, GROUP]), ALU.is_equal))
                settle()
                did(v.tensor_reduce(stat[0:P, 0, :], hits, AX, ALU.add))
                settle()
                did(v.tensor_tensor(clamped[0:P, :], clamped[0:P, :], stat[0:P, 0, :], ALU.add))
                settle()
                for c in range(0, GROUP, 8):
                    did(v.max(own_list[0:P, c:c + 8], key))
                    settle()
                    did(v.match_replace(key, own_list[0:P, c:c + 8], key, -1.0))
                    settle()
                for _ in decode(vec):
                    pass
                own.n += 1
                settle()
                v.sem_inc(g_lists, 1)
                for g in range(GH):
                    target_score(g)
                take(v, g_rows_in, 1)
                edge_sums(0, CAP, ask_group_exp)
                v.sem_inc(g_res, 1)
                take(v, g_ends_in, 1)
                g_real, g_max = gsq[0:P, :, 0:GH], gsq[0:P, :, GH:2 * GH]
                did(v.tensor_scalar(endf[0:P, 1, :], has_real[0:P, :], -1.0, -NEG, ALU.add, ALU.mult))
                settle()
                did(v.tensor_tensor(g_real, ends[0:P, :, 0:GH], bc(endf[0:P, 1, :], 2, r4), ALU.add))
                settle()
                did(v.tensor_tensor(g_max, g_real, acc[0:P, :, 0:GH], ALU.max))
                settle()
                did(v.tensor_tensor(wts[0:P, 0, :, :], acc[0:P, :, 0:GH], g_max, ALU.subtract))
                did(v.tensor_tensor(wts[0:P, 1, :, :], g_real, g_max, ALU.subtract))
                settle()
                did(v.tensor_copy(acc[0:P, :, 0:GH], g_max))
                ask_group_exp()
                did(v.tensor_tensor(wts[0:P, 1, :, :], wts[0:P, 1, :, :], bc(has_real[0:P, :], 2, r4), ALU.mult))
                settle()
                for part_, k in ((acc, 0), (ends, 1)):
                    did(v.tensor_tensor(part_[0:P, :, GH:2 * GH], part_[0:P, :, GH:2 * GH], wts[0:P, k, :, :], ALU.mult))
                    did(v.tensor_tensor(by_head(part_[0:P, :, 2 * GH:RES]), by_head(part_[0:P, :, 2 * GH:RES]),
                                        bc(wts[0:P, k, :, :], 3, [P, NT, GH, EX]), ALU.mult))
                settle()
                did(v.tensor_tensor(acc[0:P, :, GH:RES], acc[0:P, :, GH:RES], ends[0:P, :, GH:RES], ALU.add))
                settle()

            counted = own.n
            v.wait_ge(over_ready, 1)
            over = v.value_load(over_i[0:1, 0:1], min_val=0, max_val=1)
            with v.If(over > 0):
                did(v.memset(acc[0:P, :, :], 0.0))
                did(v.memset(clamped[0:P, :], 0.0))
                settle()
                did(v.memset(acc[0:P, :, 0:GH], NEG))
                settle()
                with v.Fori(0, E_GAT // GROUP) as i:
                    group_sums(i)
                v.sem_clear(vec)
                own.n = 0
                did(v.tensor_copy(ends[0:P, :, :], acc[0:P, :, :]))
                did(v.memset(has_real[0:P, :], 1.0))
                settle()
                clamped_scores()
                settle()
                v.sem_inc(vec, counted - own.n)
            own.n = counted
            did(v.tensor_scalar(endf[0:P, 1, :], has_real[0:P, :], -1.0, -NEG, ALU.add, ALU.mult))
            settle()
            did(v.tensor_tensor(e_real, ends[0:P, :, 0:GH], bc(endf[0:P, 1, :], 2, r4), ALU.add))
            settle()
            did(v.tensor_tensor(mask, mask, e_real, ALU.max))
            settle()
            for k, e_ in enumerate((e_real, e_self, e_clamp)):
                did(v.tensor_tensor(wts[0:P, k, :, :], e_, mask, ALU.subtract))
            settle()
            v.sem_inc(exp_in, 1)
            v.wait_ge(exp_out, 3)
            did(v.tensor_tensor(wts[0:P, 2, :, :], wts[0:P, 2, :, :], bc(clamped[0:P, :], 2, r4), ALU.mult))
            did(v.tensor_tensor(e_real, ends[0:P, :, GH:2 * GH], wts[0:P, 0, :, :], ALU.mult))
            r44 = [P, NT, GH, EX]
            did(v.tensor_tensor(by_head(gnum[0:P, :, :]), by_head(ends[0:P, :, 2 * GH:RES]), bc(wts[0:P, 0, :, :], 3, r44), ALU.mult))
            did(v.tensor_tensor(by_head(gprod[0:P, :, :]), by_head(tab[0:P, :, 0:GF]), bc(wts[0:P, 1, :, :], 3, r44), ALU.mult))
            settle()
            did(v.tensor_tensor(e_real, e_real, wts[0:P, 1, :, :], ALU.add))
            did(v.tensor_tensor(gnum[0:P, :, :], gnum[0:P, :, :], gprod[0:P, :, :], ALU.add))
            settle()
            did(v.tensor_tensor(e_real, e_real, wts[0:P, 2, :, :], ALU.add))
            did(v.tensor_tensor(by_head(gprod[0:P, :, :]), by_head(bc(lastrow[0:P, 0:GF], 1, r16)),
                                bc(wts[0:P, 2, :, :], 3, r44), ALU.mult))
            settle()
            did(v.tensor_tensor(gnum[0:P, :, :], gnum[0:P, :, :], gprod[0:P, :, :], ALU.add))
            did(v.tensor_scalar(e_real, e_real, 1e-16, None, ALU.add))
            settle()
            did(v.reciprocal(e_real, e_real))
            settle()
            did(v.tensor_tensor(by_head(gnum[0:P, :, :]), by_head(gnum[0:P, :, :]), bc(e_real, 3, r44), ALU.mult))
            settle()
            did(v.tensor_tensor(gnum[0:P, :, :], gnum[0:P, :, :], bc(vecs[0:P, 2, :], 1, r16), ALU.add))
            settle()
            did(normalise(3, gnum[0:P, :, :], gnum[0:P, :, :], GF, gsq[0:P, :, :], 4))
            settle()
            did(v.tensor_tensor(gnum[0:P, :, :], gnum[0:P, :, :], bc(vecs[0:P, 3, :], 1, r16), ALU.mult))
            settle()
            did(v.tensor_tensor(gnum[0:P, :, :], gnum[0:P, :, :], bc(vecs[0:P, 4, :], 1, r16), ALU.add))
            settle()

            did(v.tensor_reduce(s1[0:P, :, :], gnum[0:P, :, :].rearrange("p t (h e) -> p t e h", h=GH), AX, ALU.add))
            settle()
            sc = s2[0:P, :, :]
            did(v.tensor_scalar(sc, s1[0:P, :, :], 1.0 / GH, None, ALU.mult))
            settle()
            ree = [P, NT, EX, EX]
            other, mine = bc(sc, 2, ree), bc(sc, 3, ree)
            first = lower[0:P, :].rearrange("p (e j) -> p e j", e=EX).unsqueeze(1).to_broadcast(ree)
            beats = gprod[0:P, :, :].rearrange("p t (e j) -> p t e j", e=EX)
            ties = gnum[0:P, :, :].rearrange("p t (e j) -> p t e j", e=EX)
            did(v.tensor_tensor(beats, other, mine, ALU.is_gt))
            did(v.tensor_tensor(ties, other, mine, ALU.is_equal))
            did(v.tensor_reduce(stat[0:P, 0, :], sc, AX, ALU.max))
            settle()
            did(v.tensor_tensor(ties, ties, first, ALU.mult))
            v.tensor_tensor(gate[0:P, :, :], sc, bc(stat[0:P, 0, :], 2, [P, NT, EX]), ALU.subtract).then_inc(exp_in, 1)
            settle()
            did(v.tensor_tensor(beats, beats, ties, ALU.add))
            settle()
            did(v.tensor_reduce(s3[0:P, :, :], beats, AX, ALU.add))
            settle()
            did(v.tensor_scalar(s3[0:P, :, :], s3[0:P, :, :], 2.0, None, ALU.is_lt))
            settle()
            v.wait_ge(exp_out, 4)
            did(v.tensor_tensor(gate[0:P, :, :], gate[0:P, :, :], s3[0:P, :, :], ALU.mult))
            settle()
            did(v.tensor_reduce(stat[0:P, 0, :], gate[0:P, :, :], AX, ALU.add))
            settle()
            did(v.reciprocal(stat[0:P, 1, :], stat[0:P, 0, :]))
            settle()
            v.tensor_tensor(gate[0:P, :, :], gate[0:P, :, :], bc(stat[0:P, 1, :], 2, [P, NT, EX]), ALU.mult).then_inc(gates_ready, 1)
            v.wait_ge(gates_ready, 1)
            for half in range(2):
                t = slice(half * NT // 2, (half + 1) * NT // 2)
                if half == 0:
                    did(v.tensor_tensor(yexp[0:P, t, 1, :], yexp[0:P, t, 1, :], bc(gate[0:P, t, 1], 2, [P, NT // 2, D]), ALU.mult))
                for e in ((1, 3, 2), (3, 1, 2))[half]:
                    settle()
                    if e == 2:
                        v.wait_ge(act_weighed, (half + 1) * (NT // 2))
                    elif e == 3:
                        v.wait_ge(pool_weighed, half + 1)
                    elif half == 1:
                        v.wait_ge(pool_weighed, 3)
                    ins = v.tensor_tensor(h[0:P, t, :], h[0:P, t, :], yexp[0:P, t, e, :], ALU.add)
                    if e != 2:
                        did(ins)
                    else:
                        ins.then_inc(out_ready, 1)


_ARGS = ("x", "w_step", "w_in", "w_mix", "w_c", "att_tgt", "att_attr", "w_qk", "w_v", "w_o", "w_e",
         "w_gat", "att_vec", "w1", "b2", "w2", "gat_src", "gat_dst")


def layouts(x, L0_tok_W1, L0_tok_b1, L0_tok_W2, L0_tok_b2, L0_tok_W3, L0_tok_b3, L0_tok_W4, L0_tok_b4,
            L0_attn_edge_index, L0_attn_edge_attr, L0_attn_Wq, L0_attn_bq, L0_attn_Wk, L0_attn_bk, L0_attn_Wv,
            L0_attn_bv, L0_attn_Wo, L0_attn_bo, L0_attn_We, L0_attn_be, L0_ffn_W_gat, L0_ffn_att_src,
            L0_ffn_att_dst, L0_ffn_b_gat, L0_ffn_ln_gamma, L0_ffn_ln_beta, L0_ffn_W1, L0_ffn_b1, L0_ffn_W2,
            L0_ffn_b2, L0_ffn_edge_index):
    cat = np.concatenate
    z = np.zeros((D, D), np.float32)
    step = cat([cat([L0_tok_W2.T, z], 1), cat([z, L0_tok_W2.T], 1)], 0)
    one_half = cat([L0_tok_W1.T, L0_tok_b1[None], L0_tok_b2[None]], 0)
    wv = np.zeros((D + 1, H, HD + 1), np.float32)
    wv[:D, :, :HD] = L0_attn_Wv.reshape(D, H, HD)
    wv[D, :, :HD] = L0_attn_bv.reshape(H, HD)
    wv[D, :, HD] = 1
    w1 = cat([L0_ffn_W1, L0_ffn_b1[:, None, :]], 1)
    return {
        "x": x,
        "w_step": step,
        "w_in": cat([one_half, one_half], 1),
        "w_mix": cat([L0_tok_W4.T, L0_tok_W4.T], 0),
        "w_c": cat([L0_tok_W3.T, L0_tok_b3[None], L0_tok_b4[None], L0_tok_b4[None]], 0),
        "att_tgt": L0_attn_edge_index[1].reshape(128, JA),
        "att_attr": L0_attn_edge_attr,
        "w_qk": cat([cat([L0_attn_Wq, L0_attn_bq[None]], 0), cat([L0_attn_Wk, L0_attn_bk[None]], 0)], 1),
        "w_v": wv.reshape(D + 1, (HD + 1) * H),
        "w_o": cat([L0_attn_Wo, L0_attn_bo[None]], 0),
        "w_e": cat([L0_attn_We, L0_attn_be[None]], 0),
        "w_gat": cat([cat([L0_ffn_W_gat, z[:, :GF]], 1), cat([z[:, :GF], L0_ffn_W_gat], 1)], 0),
        "att_vec": np.stack([L0_ffn_att_src.reshape(-1), L0_ffn_att_dst.reshape(-1), L0_ffn_b_gat,
                             L0_ffn_ln_gamma, L0_ffn_ln_beta]),
        "w1": np.transpose(w1, (1, 0, 2)),
        "b2": L0_ffn_b2[None],
        "w2": np.transpose(L0_ffn_W2, (1, 0, 2)),
        "gat_src": L0_ffn_edge_index[0].reshape(128, JG),
        "gat_dst": L0_ffn_edge_index[1].reshape(128, JG),
    }


def kernel(**inputs):
    import concourse.bacc as bacc
    from concourse.bass_utils import run_bass_kernel_spmd

    laid = layouts(**{k: np.asarray(a) for k, a in inputs.items()})
    laid.update(constants())
    nc = bacc.Bacc("TRN2", target_bir_lowering=False, num_devices=1)
    arrays, args = {}, {}
    for name, a in laid.items():
        a = np.ascontiguousarray(a)
        arrays[f"in_{name}"] = a
        args[name] = nc.dram_tensor(f"in_{name}", a.shape, mybir.dt.from_np(a.dtype), kind="ExternalInput").ap()
    out = nc.dram_tensor("out_dram", (B, L, D), F32, kind="ExternalOutput").ap()
    graph_transformer_block(nc, out=out, **args)
    r = run_bass_kernel_spmd(nc, [arrays], core_ids=[0])
    return r.results[0]["out_dram"]
```
